# Optimizing a Trainium2 kernel written in Bass

```python
import numpy as np
import jax
import jax.numpy as jnp

def _softmax(x, axis=-1):
    return jax.nn.softmax(x, axis=axis)

def _gelu(x):
    return jax.nn.gelu(x, approximate=True)

def _silu(x):
    return jax.nn.silu(x)

def _sigmoid(x):
    return jax.nn.sigmoid(x)

def _layernorm(x, axis=-1, eps=1e-05):
    m = jnp.mean(x, axis=axis, keepdims=True)
    v = jnp.var(x, axis=axis, keepdims=True)
    return (x - m) / jnp.sqrt(v + eps)

def _scatter_add(tgt, idx, src, axis=0):
    return tgt.at[idx].add(src)

def _segment_sum(src, seg, n):
    return jax.ops.segment_sum(src, seg, n)
kernel_name = 'mk_recurrent_d2_jaxref_r4_7bc2fc'

def setup_inputs(seed: int=0):
    np.random.seed(seed)
    _w = jnp.asarray

    def _L0_attn_setup():
        import jax, jax.numpy as jnp
        import numpy as np
        H = 16
        DK = 128
        DV = 128
        HID = 512
        KS = 4

        def _causal_dwconv(x, w, b):
            xc = jnp.transpose(x, (0, 2, 1))
            out = jax.lax.conv_general_dilated(xc, w[:, None, :], window_strides=(1,), padding=[(KS - 1, 0)], feature_group_count=xc.shape[1], dimension_numbers=('NCH', 'OIH', 'NCH'))
            out = out + b[None, :, None]
            return jnp.transpose(out, (0, 2, 1))

        def _forward(x, Wq, Wk, Wv, Wa, ba, Wb, bb, Wg, Wo, qcw, qcb, kcw, kcb, vcw, vcb, ln_w, ln_b):
            B, T, _ = x.shape
            q = jax.nn.silu(_causal_dwconv(x @ Wq, qcw, qcb))
            k = jax.nn.silu(_causal_dwconv(x @ Wk, kcw, kcb))
            v = jax.nn.silu(_causal_dwconv(x @ Wv, vcw, vcb))
            q = q.reshape(B, T, H, DK)
            k = k.reshape(B, T, H, DK) * DK ** (-0.5)
            v = v.reshape(B, T, H, DV)
            alpha = jax.nn.sigmoid(x @ Wa + ba)
            beta = jax.nn.sigmoid(x @ Wb + bb)
            qT = jnp.transpose(q, (1, 0, 2, 3))
            kT = jnp.transpose(k, (1, 0, 2, 3))
            vT = jnp.transpose(v, (1, 0, 2, 3))
            aT = jnp.transpose(alpha, (1, 0, 2))
            bT = jnp.transpose(beta, (1, 0, 2))

            def step(S, inps):
                qt, kt, vt, at, bt = inps
                Sk = jnp.einsum('bhvk,bhk->bhv', S, kt)
                err = Sk - vt
                S = at[..., None, None] * S - bt[..., None, None] * (err[..., None] * kt[:, :, None, :])
                ot = jnp.einsum('bhvk,bhk->bhv', S, qt)
                return (S, ot)
            S0 = jnp.zeros((B, H, DV, DK), x.dtype)
            _, oT = jax.lax.scan(step, S0, (qT, kT, vT, aT, bT))
            o = jnp.transpose(oT, (1, 0, 2, 3))
            mu = jnp.mean(o, axis=-1, keepdims=True)
            var = jnp.mean(jnp.square(o - mu), axis=-1, keepdims=True)
            o = (o - mu) * jax.lax.rsqrt(var + 1e-05) * ln_w + ln_b
            g = jax.nn.sigmoid(x @ Wg).reshape(B, T, H, DV)
            o = (o * g).reshape(B, T, H * DV)
            return o @ Wo
        key = jax.random.key(seed)
        ks = jax.random.split(key, 16)
        s = 0.02
        inp = {'x': jax.random.normal(ks[0], (4, 512, HID), jnp.float32), 'Wq': jax.random.normal(ks[1], (HID, H * DK), jnp.float32) * s, 'Wk': jax.random.normal(ks[2], (HID, H * DK), jnp.float32) * s, 'Wv': jax.random.normal(ks[3], (HID, H * DV), jnp.float32) * s, 'Wa': jax.random.normal(ks[4], (HID, H), jnp.float32) * s, 'ba': jnp.zeros((H,), jnp.float32), 'Wb': jax.random.normal(ks[5], (HID, H), jnp.float32) * s, 'bb': jnp.zeros((H,), jnp.float32), 'Wg': jax.random.normal(ks[6], (HID, H * DV), jnp.float32) * s, 'Wo': jax.random.normal(ks[7], (H * DV, HID), jnp.float32) * s, 'qcw': jax.random.normal(ks[8], (H * DK, KS), jnp.float32) * 0.3, 'qcb': jnp.zeros((H * DK,), jnp.float32), 'kcw': jax.random.normal(ks[9], (H * DK, KS), jnp.float32) * 0.3, 'kcb': jnp.zeros((H * DK,), jnp.float32), 'vcw': jax.random.normal(ks[10], (H * DV, KS), jnp.float32) * 0.3, 'vcb': jnp.zeros((H * DV,), jnp.float32), 'ln_w': jnp.ones((DV,), jnp.float32), 'ln_b': jnp.zeros((DV,), jnp.float32)}
        return inp
    _L0_attn_in = _L0_attn_setup()

    def _L0_ffn_setup():
        import jax, jax.numpy as jnp
        import numpy as np
        HIDDEN = 512
        INTER = 1408
        B, S = (2, 512)

        def _ternary(key, shape):
            return jax.random.randint(key, shape, -1, 2).astype(jnp.float32)
        key = jax.random.key(seed)
        ks = jax.random.split(key, 7)
        x = jax.random.normal(ks[0], (B, S, HIDDEN), dtype=jnp.float32)
        gate_w = _ternary(ks[1], (INTER, HIDDEN))
        up_w = _ternary(ks[2], (INTER, HIDDEN))
        down_w = _ternary(ks[3], (HIDDEN, INTER))
        gate_s = jax.random.uniform(ks[4], (INTER,), minval=0.01, maxval=0.1, dtype=jnp.float32)
        up_s = jax.random.uniform(ks[5], (INTER,), minval=0.01, maxval=0.1, dtype=jnp.float32)
        down_s = jax.random.uniform(ks[6], (HIDDEN,), minval=0.01, maxval=0.1, dtype=jnp.float32)
        return {'x': x, 'gate_w': gate_w, 'up_w': up_w, 'down_w': down_w, 'gate_s': gate_s, 'up_s': up_s, 'down_s': down_s}
    _L0_ffn_in = _L0_ffn_setup()

    def _L1_attn_setup():
        import jax, jax.numpy as jnp
        import numpy as np
        _MAX_SQRT_GRADIENT = 1000.0

        @jax.custom_vjp
        def sqrt_bound_derivative(x):
            return jnp.sqrt(x)

        def _sqrt_fwd(x):
            return (jnp.sqrt(x), x)

        def _sqrt_bwd(x, g):
            clipped_x_times_4 = jnp.clip(4.0 * x, 1.0 / _MAX_SQRT_GRADIENT ** 2)
            return (g / jnp.sqrt(clipped_x_times_4),)
        sqrt_bound_derivative.defvjp(_sqrt_fwd, _sqrt_bwd)

        def block_diagonal_linear(x, w, b):
            B, L, W = x.shape
            H = w.shape[0]
            xh = x.reshape(B, L, H, W // H)
            y = jnp.einsum('blhi,hij->blhj', xh, w) + b
            return y.reshape(B, L, W)

        def _reference_tuple_inner(x, a_param, ig_w, ig_b, ag_w, ag_b):
            B, L, W = x.shape
            gate_x = jax.nn.sigmoid(block_diagonal_linear(x, ig_w, ig_b))
            gate_a = jax.nn.sigmoid(block_diagonal_linear(x, ag_w, ag_b))
            log_a = -8.0 * gate_a * jax.nn.softplus(a_param)
            a = jnp.exp(log_a)
            a_square = jnp.exp(2.0 * log_a)
            gated_x = x * gate_x
            multiplier = sqrt_bound_derivative(1.0 - a_square)
            reset = (jnp.arange(L) == 0)[None, :, None]
            multiplier = jnp.where(reset, jnp.float32(1.0), multiplier)
            normalized_x = gated_x * multiplier.astype(x.dtype)
            h0 = jnp.zeros((B, W), dtype=jnp.float32)

            def step(h, inp):
                a_t, x_t = inp
                h = a_t.astype(jnp.float32) * h + x_t.astype(jnp.float32)
                return (h, h.astype(x.dtype))
            a_tl = jnp.swapaxes(a, 0, 1)
            x_tl = jnp.swapaxes(normalized_x, 0, 1)
            last_h, ys = jax.lax.scan(step, h0, (a_tl, x_tl))
            y = jnp.swapaxes(ys, 0, 1)
            return (y, last_h)
        key = jax.random.key(seed)
        ks = jax.random.split(key, 6)
        B, L, W, H = (8, 1024, 512, 16)
        bw = W // H
        x = jax.random.normal(ks[0], (B, L, W), dtype=jnp.float32)
        a_param = jax.random.uniform(ks[1], (W,), dtype=jnp.float32)
        ig_w = jax.random.normal(ks[2], (H, bw, bw), dtype=jnp.float32) / np.sqrt(bw)
        ig_b = jnp.zeros((H, bw), dtype=jnp.float32)
        ag_w = jax.random.normal(ks[3], (H, bw, bw), dtype=jnp.float32) / np.sqrt(bw)
        ag_b = jnp.zeros((H, bw), dtype=jnp.float32)
        return {'x': x, 'a_param': a_param, 'ig_w': ig_w, 'ig_b': ig_b, 'ag_w': ag_w, 'ag_b': ag_b}
    _L1_attn_in = _L1_attn_setup()

    def _L1_ffn_setup():
        import jax, jax.numpy as jnp
        import numpy as np
        BLOCK_SIZE = 32
        HIDDEN_SIZE = 512
        MLP_DIM = 4096
        NVFP4_LUT = jnp.array([0.0, 0.5, 1.0, 1.5, 2.0, 3.0, 4.0, 6.0, 0.0, -0.5, -1.0, -1.5, -2.0, -3.0, -4.0, -6.0], dtype=jnp.float32)

        def dequant_nvfp4(W_packed, scales, block=BLOCK_SIZE):
            N = W_packed.shape[0]
            low = W_packed & 15
            high = W_packed >> 4 & 15
            idx = jnp.stack([low, high], axis=-1).reshape(N, -1)
            vals = NVFP4_LUT[idx]
            K = vals.shape[1]
            vals = vals.reshape(N, K // block, block) * scales[:, :, None]
            return vals.reshape(N, K)
        key = jax.random.key(seed)
        ks = jax.random.split(key, 7)
        x = jax.random.normal(ks[0], (4, 32, HIDDEN_SIZE), dtype=jnp.float32)
        gate_W_packed = jax.random.randint(ks[1], (MLP_DIM, HIDDEN_SIZE // 2), 0, 64, dtype=jnp.int32)
        gate_scales = jax.random.uniform(ks[2], (MLP_DIM, HIDDEN_SIZE // BLOCK_SIZE), dtype=jnp.float32) * 0.1 + 0.001
        up_W_packed = jax.random.randint(ks[3], (MLP_DIM, HIDDEN_SIZE // 2), 0, 64, dtype=jnp.int32)
        up_scales = jax.random.uniform(ks[4], (MLP_DIM, HIDDEN_SIZE // BLOCK_SIZE), dtype=jnp.float32) * 0.1 + 0.001
        down_W_packed = jax.random.randint(ks[5], (HIDDEN_SIZE, MLP_DIM // 2), 0, 64, dtype=jnp.int32)
        down_scales = jax.random.uniform(ks[6], (HIDDEN_SIZE, MLP_DIM // BLOCK_SIZE), dtype=jnp.float32) * 0.1 + 0.001
        return {'x': x, 'gate_W_packed': gate_W_packed, 'gate_scales': gate_scales, 'up_W_packed': up_W_packed, 'up_scales': up_scales, 'down_W_packed': down_W_packed, 'down_scales': down_scales}
    _L1_ffn_in = _L1_ffn_setup()
    _d = {'L0_attn_x': _L0_attn_in['x'], 'L0_attn_Wq': _L0_attn_in['Wq'], 'L0_attn_Wk': _L0_attn_in['Wk'], 'L0_attn_Wv': _L0_attn_in['Wv'], 'L0_attn_Wa': _L0_attn_in['Wa'], 'L0_attn_ba': _L0_attn_in['ba'], 'L0_attn_Wb': _L0_attn_in['Wb'], 'L0_attn_bb': _L0_attn_in['bb'], 'L0_attn_Wg': _L0_attn_in['Wg'], 'L0_attn_Wo': _L0_attn_in['Wo'], 'L0_attn_qcw': _L0_attn_in['qcw'], 'L0_attn_qcb': _L0_attn_in['qcb'], 'L0_attn_kcw': _L0_attn_in['kcw'], 'L0_attn_kcb': _L0_attn_in['kcb'], 'L0_attn_vcw': _L0_attn_in['vcw'], 'L0_attn_vcb': _L0_attn_in['vcb'], 'L0_attn_ln_w': _L0_attn_in['ln_w'], 'L0_attn_ln_b': _L0_attn_in['ln_b'], 'L0_ffn_gate_w': _L0_ffn_in['gate_w'], 'L0_ffn_up_w': _L0_ffn_in['up_w'], 'L0_ffn_down_w': _L0_ffn_in['down_w'], 'L0_ffn_gate_s': _L0_ffn_in['gate_s'], 'L0_ffn_up_s': _L0_ffn_in['up_s'], 'L0_ffn_down_s': _L0_ffn_in['down_s'], 'L1_attn_a_param': _L1_attn_in['a_param'], 'L1_attn_ig_w': _L1_attn_in['ig_w'], 'L1_attn_ig_b': _L1_attn_in['ig_b'], 'L1_attn_ag_w': _L1_attn_in['ag_w'], 'L1_attn_ag_b': _L1_attn_in['ag_b'], 'L1_ffn_gate_W_packed': _L1_ffn_in['gate_W_packed'], 'L1_ffn_gate_scales': _L1_ffn_in['gate_scales'], 'L1_ffn_up_W_packed': _L1_ffn_in['up_W_packed'], 'L1_ffn_up_scales': _L1_ffn_in['up_scales'], 'L1_ffn_down_W_packed': _L1_ffn_in['down_W_packed'], 'L1_ffn_down_scales': _L1_ffn_in['down_scales']}
    _x0 = _d['L0_attn_x']
    _d['L0_attn_x'] = jax.random.normal(jax.random.fold_in(jax.random.key(seed), 1), (2, 1024, 512), dtype=_x0.dtype)
    del _x0
    return _d

def reference(L0_attn_x, L0_attn_Wq, L0_attn_Wk, L0_attn_Wv, L0_attn_Wa, L0_attn_ba, L0_attn_Wb, L0_attn_bb, L0_attn_Wg, L0_attn_Wo, L0_attn_qcw, L0_attn_qcb, L0_attn_kcw, L0_attn_kcb, L0_attn_vcw, L0_attn_vcb, L0_attn_ln_w, L0_attn_ln_b, L0_ffn_gate_w, L0_ffn_up_w, L0_ffn_down_w, L0_ffn_gate_s, L0_ffn_up_s, L0_ffn_down_s, L1_attn_a_param, L1_attn_ig_w, L1_attn_ig_b, L1_attn_ag_w, L1_attn_ag_b, L1_ffn_gate_W_packed, L1_ffn_gate_scales, L1_ffn_up_W_packed, L1_ffn_up_scales, L1_ffn_down_W_packed, L1_ffn_down_scales):

    def _L0_attn_ref(x, Wq, Wk, Wv, Wa, ba, Wb, bb, Wg, Wo, qcw, qcb, kcw, kcb, vcw, vcb, ln_w, ln_b):
        import jax, jax.numpy as jnp
        import numpy as np
        H = 16
        DK = 128
        DV = 128
        HID = 512
        KS = 4

        def _causal_dwconv(x, w, b):
            xc = jnp.transpose(x, (0, 2, 1))
            out = jax.lax.conv_general_dilated(xc, w[:, None, :], window_strides=(1,), padding=[(KS - 1, 0)], feature_group_count=xc.shape[1], dimension_numbers=('NCH', 'OIH', 'NCH'))
            out = out + b[None, :, None]
            return jnp.transpose(out, (0, 2, 1))

        def _forward(x, Wq, Wk, Wv, Wa, ba, Wb, bb, Wg, Wo, qcw, qcb, kcw, kcb, vcw, vcb, ln_w, ln_b):
            B, T, _ = x.shape
            q = jax.nn.silu(_causal_dwconv(x @ Wq, qcw, qcb))
            k = jax.nn.silu(_causal_dwconv(x @ Wk, kcw, kcb))
            v = jax.nn.silu(_causal_dwconv(x @ Wv, vcw, vcb))
            q = q.reshape(B, T, H, DK)
            k = k.reshape(B, T, H, DK) * DK ** (-0.5)
            v = v.reshape(B, T, H, DV)
            alpha = jax.nn.sigmoid(x @ Wa + ba)
            beta = jax.nn.sigmoid(x @ Wb + bb)
            qT = jnp.transpose(q, (1, 0, 2, 3))
            kT = jnp.transpose(k, (1, 0, 2, 3))
            vT = jnp.transpose(v, (1, 0, 2, 3))
            aT = jnp.transpose(alpha, (1, 0, 2))
            bT = jnp.transpose(beta, (1, 0, 2))

            def step(S, inps):
                qt, kt, vt, at, bt = inps
                Sk = jnp.einsum('bhvk,bhk->bhv', S, kt)
                err = Sk - vt
                S = at[..., None, None] * S - bt[..., None, None] * (err[..., None] * kt[:, :, None, :])
                ot = jnp.einsum('bhvk,bhk->bhv', S, qt)
                return (S, ot)
            S0 = jnp.zeros((B, H, DV, DK), x.dtype)
            _, oT = jax.lax.scan(step, S0, (qT, kT, vT, aT, bT))
            o = jnp.transpose(oT, (1, 0, 2, 3))
            mu = jnp.mean(o, axis=-1, keepdims=True)
            var = jnp.mean(jnp.square(o - mu), axis=-1, keepdims=True)
            o = (o - mu) * jax.lax.rsqrt(var + 1e-05) * ln_w + ln_b
            g = jax.nn.sigmoid(x @ Wg).reshape(B, T, H, DV)
            o = (o * g).reshape(B, T, H * DV)
            return o @ Wo
        return _forward(x, Wq, Wk, Wv, Wa, ba, Wb, bb, Wg, Wo, qcw, qcb, kcw, kcb, vcw, vcb, ln_w, ln_b)

    def _L0_ffn_ref(x, gate_w, up_w, down_w, gate_s, up_s, down_s):
        import jax, jax.numpy as jnp
        import numpy as np
        HIDDEN = 512
        INTER = 1408
        B, S = (2, 512)

        def _ternary(key, shape):
            return jax.random.randint(key, shape, -1, 2).astype(jnp.float32)
        b, s, h = x.shape
        xf = x.reshape(b * s, h)
        g = jnp.einsum('th,ih->ti', xf, gate_w) * gate_s
        u = jnp.einsum('th,ih->ti', xf, up_w) * up_s
        hdn = jax.nn.silu(g) * u
        out = jnp.einsum('ti,hi->th', hdn, down_w) * down_s
        return out.reshape(b, s, -1)

    def _L1_attn_ref(x, a_param, ig_w, ig_b, ag_w, ag_b):
        import jax, jax.numpy as jnp
        import numpy as np
        _MAX_SQRT_GRADIENT = 1000.0

        @jax.custom_vjp
        def sqrt_bound_derivative(x):
            return jnp.sqrt(x)

        def _sqrt_fwd(x):
            return (jnp.sqrt(x), x)

        def _sqrt_bwd(x, g):
            clipped_x_times_4 = jnp.clip(4.0 * x, 1.0 / _MAX_SQRT_GRADIENT ** 2)
            return (g / jnp.sqrt(clipped_x_times_4),)
        sqrt_bound_derivative.defvjp(_sqrt_fwd, _sqrt_bwd)

        def block_diagonal_linear(x, w, b):
            B, L, W = x.shape
            H = w.shape[0]
            xh = x.reshape(B, L, H, W // H)
            y = jnp.einsum('blhi,hij->blhj', xh, w) + b
            return y.reshape(B, L, W)

        def _reference_tuple_inner(x, a_param, ig_w, ig_b, ag_w, ag_b):
            B, L, W = x.shape
            gate_x = jax.nn.sigmoid(block_diagonal_linear(x, ig_w, ig_b))
            gate_a = jax.nn.sigmoid(block_diagonal_linear(x, ag_w, ag_b))
            log_a = -8.0 * gate_a * jax.nn.softplus(a_param)
            a = jnp.exp(log_a)
            a_square = jnp.exp(2.0 * log_a)
            gated_x = x * gate_x
            multiplier = sqrt_bound_derivative(1.0 - a_square)
            reset = (jnp.arange(L) == 0)[None, :, None]
            multiplier = jnp.where(reset, jnp.float32(1.0), multiplier)
            normalized_x = gated_x * multiplier.astype(x.dtype)
            h0 = jnp.zeros((B, W), dtype=jnp.float32)

            def step(h, inp):
                a_t, x_t = inp
                h = a_t.astype(jnp.float32) * h + x_t.astype(jnp.float32)
                return (h, h.astype(x.dtype))
            a_tl = jnp.swapaxes(a, 0, 1)
            x_tl = jnp.swapaxes(normalized_x, 0, 1)
            last_h, ys = jax.lax.scan(step, h0, (a_tl, x_tl))
            y = jnp.swapaxes(ys, 0, 1)
            return (y, last_h)
        return _reference_tuple_inner(x, a_param, ig_w, ig_b, ag_w, ag_b)[0]

    def _L1_ffn_ref(x, gate_W_packed, gate_scales, up_W_packed, up_scales, down_W_packed, down_scales):
        import jax, jax.numpy as jnp
        import numpy as np
        BLOCK_SIZE = 32
        HIDDEN_SIZE = 512
        MLP_DIM = 4096
        NVFP4_LUT = jnp.array([0.0, 0.5, 1.0, 1.5, 2.0, 3.0, 4.0, 6.0, 0.0, -0.5, -1.0, -1.5, -2.0, -3.0, -4.0, -6.0], dtype=jnp.float32)

        def dequant_nvfp4(W_packed, scales, block=BLOCK_SIZE):
            N = W_packed.shape[0]
            low = W_packed & 15
            high = W_packed >> 4 & 15
            idx = jnp.stack([low, high], axis=-1).reshape(N, -1)
            vals = NVFP4_LUT[idx]
            K = vals.shape[1]
            vals = vals.reshape(N, K // block, block) * scales[:, :, None]
            return vals.reshape(N, K)
        B, S, H = x.shape
        xt = x.reshape(B * S, H)
        Wg = dequant_nvfp4(gate_W_packed, gate_scales)
        Wu = dequant_nvfp4(up_W_packed, up_scales)
        Wd = dequant_nvfp4(down_W_packed, down_scales)
        gate = jnp.einsum('th,nh->tn', xt, Wg)
        up = jnp.einsum('th,nh->tn', xt, Wu)
        gelu = jnp.tanh(0.7978845608028654 * (gate + 0.044715 * gate ** 3)) * gate * 0.5 + gate * 0.5
        inter = gelu * up
        out = jnp.einsum('tn,hn->th', inter, Wd)
        return out.reshape(B, S, H)
    x = L0_attn_x
    xn = _layernorm(x, axis=-1)
    s = _L0_attn_ref(xn, L0_attn_Wq, L0_attn_Wk, L0_attn_Wv, L0_attn_Wa, L0_attn_ba, L0_attn_Wb, L0_attn_bb, L0_attn_Wg, L0_attn_Wo, L0_attn_qcw, L0_attn_qcb, L0_attn_kcw, L0_attn_kcb, L0_attn_vcw, L0_attn_vcb, L0_attn_ln_w, L0_attn_ln_b)
    g = _silu(_L0_ffn_ref(xn, L0_ffn_gate_w, L0_ffn_up_w, L0_ffn_down_w, L0_ffn_gate_s, L0_ffn_up_s, L0_ffn_down_s))
    x = x + s * g
    xn = _layernorm(x, axis=-1)
    s = _L1_attn_ref(xn, L1_attn_a_param, L1_attn_ig_w, L1_attn_ig_b, L1_attn_ag_w, L1_attn_ag_b)
    g = _silu(_L1_ffn_ref(xn, L1_ffn_gate_W_packed, L1_ffn_gate_scales, L1_ffn_up_W_packed, L1_ffn_up_scales, L1_ffn_down_W_packed, L1_ffn_down_scales))
    x = x + s * g
    return x

_drawn_inputs = setup_inputs


def setup_inputs(seed=0):
    import zlib

    import numpy as np

    out = dict(_drawn_inputs(seed))
    spreads = {'L0_attn_ba': (0.0, 0.673),
     'L0_attn_bb': (0.0, 0.487),
     'L0_attn_qcb': (0.0, 0.1),
     'L0_attn_kcb': (0.0, 0.1),
     'L0_attn_vcb': (0.0, 0.1),
     'L0_attn_ln_w': (1.0, 0.2),
     'L0_attn_ln_b': (0.0, 0.1),
     'L1_attn_ig_b': (0.0, 0.1),
     'L1_attn_ag_b': (0.0, 0.614)}
    factors = {}
    for name, (base, spread) in spreads.items():
        noise = np.random.default_rng([zlib.crc32(name.encode()), seed]).standard_normal(out[name].shape)
        drawn = base * np.exp(spread * noise) if base else spread * noise
        out[name] = jnp.asarray(drawn.astype(out[name].dtype))
    for name, factor in factors.items():
        out[name] = (out[name] * factor).astype(out[name].dtype)
    return out
```

```python
from contextlib import ExitStack

import numpy as np

import concourse.bass as bass
from concourse import mybir

F32 = mybir.dt.float32
F32R = mybir.dt.float32r
F16 = mybir.dt.float16
I32 = mybir.dt.int32
ALU = mybir.AluOpType
ACT = mybir.ActivationFunctionType

T = 2048
H = 16
EPS = 1e-5

C_ID, C_CM, C_J, C_M16, C_OFF, C_FLAG, C_N = 0, 128, 256, 384, 416, 448, 450


class Tok:

    __slots__ = ("sem", "val", "used")

    def __init__(self, sem, val=None):
        self.sem, self.val, self.used = sem, val, False


class Queues:

    ENG = ("tensor", "vector", "scalar", "gpsimd", "sync")

    def __init__(self, nc, ctx):
        self.nc = nc
        self.q = {e: [] for e in self.ENG}
        self.sem = {e: ctx.enter_context(nc.semaphore("s_" + e)) for e in self.ENG}
        self.ctx = ctx
        self.count = {}
        self.last = {}

    def op(self, eng, fn, *after):
        t = Tok(eng)
        self.q[eng].append((fn, flat(after), t))
        self.last[eng] = t
        return t

    def dma(self, eng, name, out, in_, *after):
        if name not in self.sem:
            self.sem[name] = self.ctx.enter_context(self.nc.semaphore("d_" + name))
            self.count[name] = 0
        self.count[name] += 16
        t = Tok(name, self.count[name])
        self.q[eng].append((lambda e: e.dma_start(out, in_), flat(after), t))
        return t

    def everything(self):
        return list(self.last.values()) + [Tok(n, c) for n, c in self.count.items()]

    def emit(self, block):
        for items in self.q.values():
            for _, after, _ in items:
                for a in after:
                    a.used = True
        for items in self.q.values():
            n = 0
            for _, _, t in items:
                if t.val is None and t.used:
                    n += 1
                    t.val = n
                elif t.val is None:
                    t.val = 0
        for name in self.ENG:
            hook = {"tensor": block.tensor, "vector": block.vector, "scalar": block.scalar,
                            "gpsimd": block.gpsimd, "sync": block.sync}[name]

            def body(e, name=name):
                met = {}
                for fn, after, t in self.q[name]:
                    need = {}
                    for a in after:
                        need[a.sem] = max(need.get(a.sem, 0), a.val)
                    for s, v in need.items():
                        if v > met.get(s, 0):
                            e.wait_ge(self.sem[s], v)
                            met[s] = v
                    ins = fn(e)
                    if ins is not None and t.used:
                        ins.then_inc(self.sem[t.sem], 16 if t.sem in self.count else 1)
                    elif ins is not None and t.sem in self.count:
                        ins.then_inc(self.sem[t.sem], 16)

            hook(body)


def flat(xs):
    out = []
    for x in xs:
        if x is None:
            continue
        if isinstance(x, (list, tuple)):
            out += flat(x)
        else:
            out.append(x)
    return out


class Ring:

    def __init__(self, slots):
        self.slots, self.free, self.n = slots, [[] for _ in slots], -1

    def take(self):
        self.n = (self.n + 1) % len(self.slots)
        return self.n, self.slots[self.n], self.free[self.n]

    def hold(self, i, *users):
        self.free[i] = flat(users)


def mm3(e, out, pairs, first=True, last=True):
    n = len(pairs)
    for k, (wh, wl, xh, xl) in enumerate(pairs):
        e.matmul(out, wh, xh, start=first and k == 0, stop=False)
        e.matmul(out, wh, xl, start=False, stop=False)
        m = e.matmul(out, wl, xh, start=False, stop=last and k == n - 1)
    return m


def f32(ap):
    return ap.bitcast(F32)


def program(nc, io, out, scratch, stages=99):
    with ExitStack() as ctx:
        Q = Queues(nc, ctx)
        V = lambda fn, *a: Q.op("vector", fn, *a)
        A = lambda fn, *a: Q.op("scalar", fn, *a)
        P = lambda fn, *a: Q.op("tensor", fn, *a)
        G = lambda fn, *a: Q.op("gpsimd", fn, *a)

        def sb(c, name, shape, dt=F32):
            return c.enter_context(nc.sbuf_tensor("b_" + name, shape, dt))

        bank = [ctx.enter_context(nc.psum_tensor(f"bank{i}", [128, 512], F32)) for i in range(8)]
        cst = sb(ctx, "cst", [128, C_N])
        ident, cmat, jmat = cst[:, 0:128], cst[:, C_CM:C_CM + 128], cst[:, C_J:C_J + 128]
        eps = sb(ctx, "eps", [128, 1])
        one = sb(ctx, "one", [128, 1])
        t_cst = Q.dma("sync", "cst", cst[:, :], io["consts"])
        t_eps = V(lambda e: e.memset(eps[:, :], EPS))
        t_one = V(lambda e: e.memset(one[:, :], 1.0))

        def split(src, hi, lo, after, free=(), src_is_psum=False, low_eng="vector"):
            th = A(lambda e: e.copy(hi, src), after, free)
            tl = Q.op(low_eng, lambda e: e.tensor_tensor(lo, src, f32(hi), ALU.subtract), th, after, free)
            return [th, tl]

        def norm_rows(x, xn, c, tag, after):
            st = sb(c, "st" + tag, [128, 16, 6])
            mv = sb(c, "mv" + tag, [128, 16, 2])
            sd = sb(c, "sd" + tag, [128, 16])
            rs = sb(c, "rs" + tag, [128, 16])
            for i in range(16):
                t = V(lambda e, i=i: e.bn_stats(st[:, i, :], x[:, i, :]), after[i])
                t = V(lambda e, i=i: e.bn_aggr(mv[:, i, :], st[:, i, :]), t)
            t = A(lambda e: e.activation(sd[:, :], mv[:, :, 1], ACT.Sqrt, bias=eps[:, 0:1]), t, t_eps)
            t = V(lambda e: e.reciprocal(rs[:, :], sd[:, :]), t)
            return [V(lambda e, i=i: e.tensor_scalar(xn[:, i, :], x[:, i, :], mv[:, i, 0:1], rs[:, i:i + 1],
                                                     ALU.subtract, ALU.mult), t) for i in range(16)]

        def turned(xn, i, order, bk, after, free):
            def go(e):
                for k in range(4):
                    m = e.transpose(bk[:, k * 128:(k + 1) * 128], order(xn, i, k), ident)
                return m
            return P(go, after, free, t_cst)

        plain = lambda xn, i, k: xn[:, i, k * 128:(k + 1) * 128]
        byparity = lambda xn, i, k: xn[:, i, 256 * (k // 2) + k % 2:256 * (k // 2) + 256:2]

        layer = ctx.enter_context(ExitStack())
        XH = sb(layer, "XH", [128, 4, T], F32R)
        XL = sb(layer, "XL", [128, 4, T], F32R)
        coef = sb(layer, "coef", [128, 16, 3, 16])
        GC = sb(layer, "GC", [128, 16, 16])
        with ExitStack() as c:
            x = sb(c, "x0", [128, 16, 512])
            xn = sb(c, "xn0", [128, 16, 512])
            tx = [Q.dma("sync", f"x{i % 4}", x[:, i * 4:i * 4 + 4, :],
                        io["x"].rearrange("(i p) d -> p i d", p=128)[:, i * 4:i * 4 + 4, :]) for i in range(4)]
            tn = norm_rows(x, xn, c, "0", [tx[i // 4] for i in range(16)])
            wab = sb(c, "wab", [128, 4, 128])
            wabh = sb(c, "wabh", [128, 4, 128], F32R)
            wabl = sb(c, "wabl", [128, 4, 128], F32R)
            bab = sb(c, "bab", [128, 1])
            t_wab = Q.dma("sync", "wab", wab[:, :, :], io["Wab"].rearrange("(k p) n -> p k n", p=128))
            t_bab = Q.dma("sync", "bab", bab[:, :], io["bab"])
            t_ws = split(wab[:, :, :], wabh[:, :, :], wabl[:, :, :], t_wab)
            tb = [None] * 8
            tX = []
            for i in range(16):
                b = i % 4
                t = turned(xn, i, plain, bank[b], tn[i], tb[b])
                src = bank[b][:, :].rearrange("p (k t) -> p k t", k=4)
                tb[b] = split(src, XH[:, :, i * 128:(i + 1) * 128], XL[:, :, i * 128:(i + 1) * 128], t)
                tX.append(tb[b])
            S = sb(c, "S", [128, T])
            SG = sb(c, "SG", [128, T])
            Gm = sb(c, "Gm", [128, T])
            TB = sb(c, "TB", [128, T])
            BT = sb(c, "BT", [128, T])
            zero = sb(c, "zero", [128, 128])
            gc16 = sb(c, "gc16", [16, 16])
            t_z = V(lambda e: e.memset(zero[:, :], 0.0))
            t_tb = V(lambda e: e.memset(TB[:, :], 0.0))
            tS = []
            for n in range(4):
                sl = slice(n * 512, n * 512 + 512)
                t = P(lambda e, n=n, sl=sl: mm3(e, bank[4 + n][:, :], [
                    (wabh[:, k, :], wabl[:, k, :], XH[:, k, sl], XL[:, k, sl]) for k in range(4)]),
                    t_ws, tX[4 * n:4 * n + 4])
                tS.append(A(lambda e, n=n, sl=sl: e.activation(S[:, sl], bank[4 + n][:, :], ACT.Sigmoid,
                                                               bias=bab[:, 0:1]), t, t_bab))
            t1 = V(lambda e: e.memset(SG[0:16, :].rearrange("p (c t) -> p c t", t=128)[:, :, 127:128], 1.0))
            tg = []
            for ch in range(16):
                o = ch * 128
                a = V(lambda e, o=o: e.tensor_tensor_scan(Gm[0:16, o:o + 128], S[0:16, o:o + 128], zero[0:16, :],
                                                          1.0, ALU.mult, ALU.add), tS[ch // 4], t_z)
                lo = o - 1 if o else None
                b = V(lambda e, o=o: e.tensor_tensor_scan(SG[0:16, o:o + 127][:, ::-1], S[0:16, o + 1:o + 128][:, ::-1],
                                                          zero[0:16, 0:127], 1.0, ALU.mult, ALU.add), t1)
                tg += [a, b]
            t2 = V(lambda e: e.tensor_scalar(TB[0:16, 1:T], Gm[0:16, 0:T - 1], -1.0, None, ALU.mult), tg, t_tb)
            t2 = V(lambda e: e.memset(TB[0:16, :].rearrange("p (c t) -> p c t", t=128)[:, :, 0:1], -1.0), t2)
            t3 = V(lambda e: e.tensor_copy(TB[32:48, :], S[32:48, :]), tS, t_tb)
            t4 = V(lambda e: e.tensor_copy(BT[0:16, :], S[32:48, :]), tS)
            t5 = V(lambda e: e.tensor_tensor(TB[64:80, :], BT[0:16, :], SG[0:16, :], ALU.mult), t4, tg, t_tb)
            t6 = V(lambda e: e.tensor_copy(gc16[:, :], Gm[0:16, :].rearrange("p (c t) -> p c t", t=128)[:, :, 127]), tg)
            d1 = Q.dma("sync", "ad", scratch["a"], S[0:16, :], tS)
            d2 = Q.dma("sync", "gd", scratch["g"], Gm[0:16, :], tg)
            d3 = Q.dma("sync", "gcd", scratch["gc"].rearrange("(h c) -> h c", h=16), gc16[:, :], t6)
            t_gc = Q.dma("sync", "gcl", GC[:, :, :].rearrange("p h c -> p (h c)"),
                         scratch["gc"].partition_broadcast(128), d3)
            t_coef = []
            for i in range(16):
                b = i % 4
                t = P(lambda e, i=i, b=b: e.transpose(bank[b][:, 0:128], TB[:, i * 128:(i + 1) * 128], ident),
                      [t2, t3, t5], tb[b], t_cst)
                tb[b] = A(lambda e, i=i, b=b: e.copy(
                    coef[:, i, :, :], bank[b][:, 0:96].rearrange("p (q r) -> p q r", q=3)[:, :, 0:16]), t)
                t_coef.append(tb[b])
            t_scr = [d1, d2]
            done = Q.everything()
        if stages == 0:
            Q.dma("sync", "dbg", out["d0"], XH[:, :, :].bitcast(F32), done)
            Q.dma("sync", "dbg", out["d1"], XL[:, :, :].bitcast(F32), done)
            Q.dma("sync", "dbg", out["d2"], coef[:, :, :, :], done)
            Q.dma("sync", "dbg", out["d3"], GC[:, :, :], done)
        if stages >= 1:
            done = ffn0(nc, Q, sb, io, scratch, bank, split, XH, XL, done)
        if stages >= 2:
            done = attn0(nc, Q, sb, io, scratch, bank, split, XH, XL, coef, GC, cst, eps, done)
        layer.close()
        if stages >= 3:
            done = mix0(nc, Q, sb, io, scratch, bank, split, cst, done)
        if stages >= 4:
            lay = ctx.enter_context(ExitStack())
            YH = sb(lay, "XH1", [128, 4, T], F32R)
            YL = sb(lay, "XL1", [128, 4, T], F32R)
            with ExitStack() as c:
                x1 = sb(c, "x1", [128, 16, 512])
                t = Q.dma("sync", "x0", x1[:, :, :], scratch["x1"].rearrange("(i p) d -> p i d", p=128), done)
                tn = norm_rows(x1, x1, c, "1", [t] * 16)
                XN = sb(c, "XN", [128, 4, T])
                tb = [done] * 8
                for i in range(16):
                    b = i % 4
                    t = turned(x1, i, byparity, bank[b], tn[i], tb[b])
                    src = bank[b][:, :].rearrange("p (k t) -> p k t", k=4)
                    tb[b] = split(src, YH[:, :, i * 128:(i + 1) * 128], YL[:, :, i * 128:(i + 1) * 128], t)
                    t = turned(x1, i, plain, bank[4 + b], tn[i], tb[4 + b])
                    tb[4 + b] = A(lambda e, i=i, b=b: e.copy(XN[:, :, i * 128:(i + 1) * 128], bank[4 + b][:, :]
                                                             .rearrange("p (k t) -> p k t", k=4)), t)
                done = Q.everything()
                done = attn1(nc, Q, sb, io, scratch, bank, XN, one, done)
            done = ffn1(nc, Q, sb, io, scratch, bank, split, YH, YL, done)
            lay.close()
            final(nc, Q, sb, io, scratch, bank, cst, out, done)
        Q.op("sync", lambda e: None, Q.everything())
        block = ctx.enter_context(nc.Block())
        Q.emit(block)


def final(nc, Q, sb, io, scratch, bank, cst, out, done):
    with ExitStack() as c:
        x1 = Ring([sb(c, f"fx{i}", [128, 512]) for i in range(3)])
        s1 = Ring([sb(c, f"fs{i}", [128, 4, 128]) for i in range(3)])
        g1 = Ring([sb(c, f"fg{i}", [128, 4, 128]) for i in range(3)])
        pr = Ring([sb(c, f"fp{i}", [128, 4, 128]) for i in range(3)])
        oo = Ring([sb(c, f"fo{i}", [128, 512]) for i in range(3)])
        bk = Ring(bank)
        for i in range(16):
            sl = slice(i * 128, (i + 1) * 128)
            n, xt, f = x1.take()
            tx = Q.dma("sync", f"fx{n}", xt[:, :], scratch["x1"][sl, :], f, done)
            m, st, f = s1.take()
            ts = Q.dma("sync", f"fs{m}", st[:, :, :], scratch["s1"].rearrange("(k p) t -> p k t", p=128)[:, :, sl], f, done)
            m, gt, f = g1.take()
            tg = Q.dma("scalar", f"fg{m}", gt[:, :, :], scratch["g1"].rearrange("(k p) t -> p k t", p=128)[:, :, sl], f, done)
            m2, pt, f = pr.take()
            tp = Q.op("vector", lambda e, pt=pt, st=st, gt=gt: e.tensor_tensor(pt[:, :, :], st[:, :, :], gt[:, :, :],
                                                                               ALU.mult), ts, tg, f)
            s1.hold(m, tp)
            g1.hold(m, tp)
            b, bt, f = bk.take()

            def go(e, bt=bt, pt=pt):
                for k in range(4):
                    r = e.transpose(bt[:, k * 128:(k + 1) * 128], pt[:, k, :], cst[:, 0:128])
                return r
            t = Q.op("tensor", go, tp, f, done)
            pr.hold(m2, t)
            m3, ot, f = oo.take()
            t = Q.op("vector", lambda e, ot=ot, bt=bt, xt=xt: e.tensor_tensor(ot[:, :], bt[:, :], xt[:, :], ALU.add), t, tx, f)
            bk.hold(b, t)
            x1.hold(n, t)
            oo.hold(m3, Q.dma("scalar", f"fo{m3}", out["y"][sl, :], ot[:, :], t))


def ffn0(nc, Q, sb, io, scratch, bank, split, XH, XL, done):
    V = lambda fn, *a: Q.op("vector", fn, *a)
    A = lambda fn, *a: Q.op("scalar", fn, *a)
    P = lambda fn, *a: Q.op("tensor", fn, *a)
    with ExitStack() as c:
        raw = Ring([sb(c, f"fr{i}", [128, 4, 128]) for i in range(3)])
        wh = Ring([sb(c, f"fwh{i}", [128, 4, 128], F32R) for i in range(4)])
        wl = [sb(c, f"fwl{i}", [128, 4, 128], F32R) for i in range(4)]
        HH = sb(c, "HH", [128, 4, T], F32R)
        HL = sb(c, "HL", [128, 4, T], F32R)
        ACC = sb(c, "ACC", [128, 4, T])
        sil = Ring([sb(c, f"sil{i}", [128, 512]) for i in range(2)])
        hd = Ring([sb(c, f"hd{i}", [128, 512]) for i in range(2)])
        sc = sb(c, "fsc", [128, 26])
        t_sc = Q.dma("sync", "fsc", sc[:, :], io["ffn0_s"], done)
        bk = Ring(bank)
        for i in range(8):
            bk.hold(i, done)
        for r in (raw, wh, sil, hd):
            for i in range(len(r.slots)):
                r.hold(i, done)

        def weight(src):
            n, r, f = raw.take()
            t = Q.dma("sync", f"fr{n}", r[:, :, :], src, f)
            m, w, f = wh.take()
            ts = split(r[:, :, :], w[:, :, :], wl[m][:, :, :], t, f, low_eng="gpsimd")
            raw.hold(n, ts)
            return m, w, wl[m], ts

        gw = io["gate_wT"].rearrange("(k p) n -> p k n", p=128)
        uw = io["up_wT"].rearrange("(k p) n -> p k n", p=128)
        dw = io["down_wT"]
        tH = [[done for _ in range(4)] for _ in range(4)]
        tA = {}
        for g0, g1 in ((0, 4), (4, 8), (8, 11)):
            hs = {}
            for it in range(g0, g1):
                ng, wg, wgl, tg = weight(gw[:, :, it * 128:(it + 1) * 128])
                nu, wu, wul, tu = weight(uw[:, :, it * 128:(it + 1) * 128])
                for n in range(4):
                    sl = slice(n * 512, n * 512 + 512)
                    b1, k1, f1 = bk.take()
                    t1 = P(lambda e, k1=k1, wg=wg, wgl=wgl, sl=sl: mm3(e, k1[:, :], [
                        (wg[:, k, :], wgl[:, k, :], XH[:, k, sl], XL[:, k, sl]) for k in range(4)]), tg, f1)
                    b2, k2, f2 = bk.take()
                    t2 = P(lambda e, k2=k2, wu=wu, wul=wul, sl=sl: mm3(e, k2[:, :], [
                        (wu[:, k, :], wul[:, k, :], XH[:, k, sl], XL[:, k, sl]) for k in range(4)]), tu, f2)
                    m, s, f = sil.take()
                    ts = A(lambda e, s=s, k1=k1, it=it: e.activation(s[:, :], k1[:, :], ACT.Silu,
                                                                     scale=sc[:, it:it + 1]), t1, f, t_sc)
                    bk.hold(b1, ts)
                    m2, h, f = hd.take()
                    th = V(lambda e, h=h, k2=k2, s=s, it=it: e.scalar_tensor_tensor(
                        out=h[:, :], in0=k2[:, :], scalar=sc[:, 11 + it:12 + it], in1=s[:, :],
                        op0=ALU.mult, op1=ALU.mult), t2, ts, f)
                    bk.hold(b2, th)
                    sil.hold(m, th)
                    q = it - g0
                    tt = split(h[:, :], HH[:, q, sl], HL[:, q, sl], th, tH[q][n], low_eng="gpsimd")
                    hd.hold(m2, tt)
                    hs[(q, n)] = tt
                wh.hold(ng, t1)
                wh.hold(nu, t2)
            ws = []
            for it in range(g0, g1):
                ws.append(weight(dw[it * 128:(it + 1) * 128, :].rearrange("p (k n) -> p k n", k=4)))
            for o in range(4):
                for n in range(4):
                    sl = slice(n * 512, n * 512 + 512)
                    b, kb, f = bk.take()
                    t = P(lambda e, kb=kb, o=o, sl=sl, ws=ws: mm3(e, kb[:, :], [
                        (w[:, o, :], wlo[:, o, :], HH[:, q, sl], HL[:, q, sl])
                        for q, (_, w, wlo, _) in enumerate(ws)]),
                        [w[3] for w in ws], [hs[(q, n)] for q in range(g1 - g0)], f)
                    if g0 == 0:
                        ta = A(lambda e, kb=kb, o=o, sl=sl: e.copy(ACC[:, o, sl], kb[:, :]), t)
                    else:
                        ta = V(lambda e, kb=kb, o=o, sl=sl: e.tensor_tensor(ACC[:, o, sl], ACC[:, o, sl], kb[:, :],
                                                                            ALU.add), t, tA[(o, n)])
                    tA[(o, n)] = ta
                    bk.hold(b, ta)
                    tH[0][n] = t
            for n in range(4):
                for q in range(4):
                    tH[q][n] = tH[0][n]
            for w in ws:
                wh.hold(w[0], t)
        for o in range(4):
            for n in range(4):
                sl = slice(n * 512, n * 512 + 512)
                t = A(lambda e, o=o, sl=sl: e.activation(ACC[:, o, sl], ACC[:, o, sl], ACT.Silu,
                                                         scale=sc[:, 22 + o:23 + o]), tA[(o, n)])
            Q.dma("sync", "g0d", scratch["g0"][o * 128:(o + 1) * 128, :], ACC[:, o, :], t)
        return Q.everything()


def merged(*streams):
    lists = [(list_len, iter(gen)) for list_len, gen in streams]
    total = max(n for n, _ in lists)
    at = [0] * len(lists)
    for s in range(total):
        for k, (n, g) in enumerate(lists):
            while at[k] * total < (s + 1) * n:
                next(g, None)
                at[k] += 1
    for _, g in lists:
        for _ in g:
            pass


def attn0(nc, Q, sb, io, scratch, bank, split, XH, XL, coef, GC, cst, eps, done):
    V = lambda fn, *a: Q.op("vector", fn, *a)
    A = lambda fn, *a: Q.op("scalar", fn, *a)
    P = lambda fn, *a: Q.op("tensor", fn, *a)
    G = lambda fn, *a: Q.op("gpsimd", fn, *a)
    KS = 128.0 ** -0.5
    with ExitStack() as c:
        def ring(name, n, shape, dt=F32):
            r = Ring([sb(c, f"{name}{i}", shape, dt) for i in range(n)])
            for i in range(n):
                r.hold(i, done)
            return r

        ident, cmat, jmat = cst[:, 0:128], cst[:, C_CM:C_CM + 128], cst[:, C_J:C_J + 128]
        raw = ring("wr", 2, [128, 4, 128])
        wh = ring("wh", 5, [128, 4, 128], F32R)
        wl = [sb(c, f"wl{i}", [128, 4, 128], F32R) for i in range(5)]
        cw = sb(c, "cw", [128, 16, 3, 5])
        lnw = sb(c, "lnw", [128, 2])
        t_cw = Q.dma("sync", "cw", cw[:, :, :, :], io["cw"], done)
        t_ln = Q.dma("sync", "lnw", lnw[:, :], io["ln"], done)
        rawx = ring("rx", 2, [128, 515])
        zt = ring("zt", 2, [128, 512])
        vt = ring("vt", 2, [128, 512])
        tails = sb(c, "tails", [128, 3, 2, 3])
        abc = ring("abc", 2, [128, 512])
        gbc = ring("gbc", 1, [128, 512])
        KQA = sb(c, "KQA", [128, 3, 2, 4, 128])
        KQ = Ring([0, 1])
        QG = ring("QG", 2, [128, 2, 4, 128])
        KD = ring("KD", 2, [128, 2, 4, 128])
        VC = ring("VC", 2, [128, 2, 4, 128])
        XPA = sb(c, "XPA", [128, 3, 8, 128])
        XP = Ring([1, 2])
        for r in (KQ, XP):
            for i in range(2):
                r.hold(i, done)
        q_all, X = KQA[:, 2], XPA[:, 0]

        def pair(ap, step, n=128):
            return bass.AP(tensor=ap.tensor, offset=ap.offset, ap=[list(ap.ap[0]), [step, 2], [1, n]])

        MF = ring("MF", 2, [128, 8, 128])
        D = ring("D", 3, [128, 130])
        XD = sb(c, "XD", [128, 16, 32])
        UN = sb(c, "UN", [128, 1024])
        XM = UN[:, 0:512].rearrange("p (m t) -> p m t", m=16)
        YY = UN[:, 512:1024].rearrange("p (m t) -> p m t", m=16)
        E1 = UN[:, :].rearrange("p (w a s b) -> p w a s b", w=2, a=16, s=2)
        XO = sb(c, "XO", [128, 8, 32])
        A16 = sb(c, "A16", [128, 16, 16])
        T16 = sb(c, "T16", [128, 16, 16])
        PR = sb(c, "PR", [128, 64])
        MN = sb(c, "MN", [128, 2, 16, 32])
        ZS = sb(c, "ZS", [128, 8, 32])
        ZT = sb(c, "ZT", [128, 8, 32])
        NF = sb(c, "NF", [64, 8, 64])
        Z2 = sb(c, "Z2", [128, 8, 64])
        ST = sb(c, "ST", [128, 2, 128])
        R = ring("R", 2, [128, 2, 128])
        WS = ring("WS", 2, [128, 2, 128])
        OS = ring("OS", 1, [128, 2, 4, 128])
        sq = ring("sq", 1, [128, 512])
        rs = ring("rstd", 2, [128, 512])
        gg = ring("gg", 1, [128, 512])
        bk = Ring(bank[0:4])
        for i in range(4):
            bk.hold(i, done)
        fb = {n: [done] for n in (4, 5, 6, 7)}
        t_i = []
        t_i.append(V(lambda e: e.memset(XD[:, :, :], 0.0), done))
        t_i.append(V(lambda e: e.memset(NF[:, :, :], 0.0), done))
        for m in MF.slots:
            t_i.append(V(lambda e, m=m: e.memset(m[:, :, :], 0.0), done))
        for d in D.slots:
            t_i.append(V(lambda e, d=d: e.memset(d[:, 0:1], 0.0), done))

        wsrc = {p: io[p].rearrange("(k p) n -> p k n", p=128) for p in ("Wq", "Wk", "Wv", "Wg")}

        def weight(p, h):
            n, r, f = raw.take()
            t = Q.dma("sync", f"wr{n}", r[:, :, :], wsrc[p][:, :, h * 128:(h + 1) * 128], f)
            m, w, f = wh.take()
            ts = split(r[:, :, :], w[:, :, :], wl[m][:, :, :], t, f, low_eng="gpsimd")
            raw.hold(n, ts)
            return m, w, wl[m], ts

        def project(w, n):
            m, wt, wlo, tw = w
            b, kb, f = bk.take()
            sl = slice(n * 512, n * 512 + 512)
            t = P(lambda e, kb=kb: mm3(e, kb[:, :], [
                (wt[:, k, :], wlo[:, k, :], XH[:, k, sl], XL[:, k, sl]) for k in range(4)]), tw, f)
            return b, kb, t

        W = {}
        t_tail = {}
        unit = {}

        def stage_a(u):
            h, half = divmod(u, 2)
            if half == 0:
                for p in ("Wk", "Wv", "Wq"):
                    W[p] = weight(p, h)
            s = {}
            unit[u] = s
            kqn, kq, kqf = KQ.take()
            qgn, qg, qgf = QG.take()
            kdn, kd, kdf = KD.take()
            vcn, vc, vcf = VC.take()
            xpn, xp, xpf = XP.take()
            mfn, mf, mff = MF.take()
            s.update(kqn=kqn, kq=KQA[:, kq], slot=(kq, xp), qgn=qgn, qg=qg, kdn=kdn, kd=kd, vcn=vcn, vc=vc, xpn=xpn, xp=XPA[:, xp], mfn=mfn, mf=mf)
            k_slot, p_slot = kq, xp
            kq, xp = KQA[:, kq], XPA[:, xp]
            inv = s_prev.get("inv")
            s["t_kd"], s["t_vc"], s["t_xp"], s["t_kq"] = {}, {}, {}, {}
            ready = {}

            def conv(pi, p, b):
                n = 2 * b + half
                kbn, kb, t = project(W[p], n)
                rn, rx, rf = rawx.take()
                zn, z, zf = zt.take()
                tr = A(lambda e: e.copy(rx[:, 3:515], kb[:, :]), t, rf)
                tz = A(lambda e: e.activation(z[:, :], kb[:, :], ACT.Copy, scale=cw[:, h, pi, 3:4]), t, zf, t_cw)
                bk.hold(kbn, tr, tz)
                if half == 0:
                    th = G(lambda e: e.memset(rx[:, 0:3], 0.0), rf)
                    tt = G(lambda e: e.tensor_copy(tails[:, pi, b, :], rx[:, 512:515]), tr, t_tail.get((pi, b)))
                    t_tail[pi, b] = tt
                else:
                    th = G(lambda e: e.tensor_copy(rx[:, 0:3], tails[:, pi, b, :]), rf, t_tail[pi, b])
                    t_tail[pi, b] = th
                    tt = th
                for j in (2, 1, 0):
                    tz = V(lambda e, j=j: e.scalar_tensor_tensor(out=z[:, :], in0=rx[:, j:j + 512],
                                                                 scalar=cw[:, h, pi, j:j + 1], in1=z[:, :],
                                                                 op0=ALU.mult, op1=ALU.add), tz, tr, th)
                rawx.hold(rn, tz, tt)
                bias = cw[:, h, pi, 4:5]
                v4 = lambda ap: ap.rearrange("p (c t) -> p c t", c=4)
                if p == "Wk":
                    ta = A(lambda e: e.activation(z[:, :], z[:, :], ACT.Silu, bias=bias), tz)
                    ta = to = G(lambda e: e.tensor_scalar(kq[:, b, :, :], v4(z[:, :]), KS, None, ALU.mult), ta, kqf)
                elif p == "Wq":
                    ta = to = A(lambda e: e.activation(q_all[:, b, :, :], v4(z[:, :]), ACT.Silu, bias=bias), tz,
                                s_prev.get("q"))
                    gn, g, gf = gbc.take()
                    tl = Q.dma("sync", f"gb{gn}", g[:, :],
                               scratch["g"][h:h + 1, n * 512:n * 512 + 512].rearrange("a t -> (a t)").partition_broadcast(128), gf)
                    tg = G(lambda e: e.tensor_tensor(qg[:, b, :, :], q_all[:, b, :, :], v4(g[:, :]), ALU.mult),
                           ta, tl, qgf)
                    gbc.hold(gn, tg)
                    s["t_qg", b] = tg
                else:
                    vn, v, vf = vt.take()
                    ta = to = A(lambda e: e.activation(v[:, :], z[:, :], ACT.Silu, bias=bias), tz, vf)
                    ready["v", b] = (vn, v)
                zt.hold(zn, ta)
                ready[p, b] = to
                s["t_kq"][b] = [ready.get(("Wk", b)), ready.get(("Wq", b))]

            def turn_kv(b, c0):
                vn, v = ready["v", b]
                bn, kb, f = bk.take()

                def go(e):
                    for x in range(2):
                        e.transpose(kb[:, x * 256:x * 256 + 128], kq[:, b, c0 + x, :], ident)
                        m = e.matmul(kb[:, x * 256 + 128:x * 256 + 256], v[:, (c0 + x) * 128:(c0 + x + 1) * 128],
                                     cmat, start=True, stop=True)
                    return m
                t = P(go, ready["Wk", b], ready["Wv", b], f)
                for x in range(2):
                    i = b * 8 + half * 4 + c0 + x
                    s["t_kd"][b, c0 + x] = A(lambda e, x=x, i=i: e.activation(
                        kd[:, b, c0 + x, :], kb[:, x * 256:x * 256 + 128], ACT.Copy, scale=coef[:, i, 2, h:h + 1]), t, kdf)
                tv = A(lambda e: e.copy(vc[:, b, c0:c0 + 2, :],
                                        kb[:, :].rearrange("p (x a t) -> p x a t", x=2, a=2)[:, :, 1, :]), t, vcf)
                bk.hold(bn, s["t_kd"][b, c0], s["t_kd"][b, c0 + 1], tv)
                s["t_vc"][b, c0] = s["t_vc"][b, c0 + 1] = tv
                if c0 == 2:
                    vt.hold(vn, t)

            def scores(b, c0, an):
                bn, kb, f = bk.take()

                def go(e):
                    for x in range(2):
                        m = e.matmul(kb[:, x * 256:x * 256 + 256], kq[:, b, c0 + x, :],
                                     pair(kq[:, b, c0 + x, :], (2 - k_slot) * 1024), start=True, stop=True)
                    return m
                t = P(go, ready["Wk", b], ready["Wq", b], f)
                s_prev["q"] = [t, s["t_qg", 0], s.get(("t_qg", 1))]
                ts = []
                for x in range(2):
                    i = b * 8 + half * 4 + c0 + x
                    dn, d, df = D.take()
                    td = V(lambda e, x=x, d=d: e.tensor_tensor_scan(
                        d[:, 1:129], abc.slots[an[0]][:, (c0 + x) * 128:(c0 + x + 1) * 128], ident, 0.0,
                        ALU.mult, ALU.add), an[1], df, t_i)
                    tx = V(lambda e, x=x, d=d, i=i: e.scalar_tensor_tensor(
                        out=pair(X[:, b * 4 + c0 + x, :], p_slot * 1024), in0=kb[:, x * 256:x * 256 + 256].rearrange("p (a t) -> p a t", a=2),
                        scalar=coef[:, i, 1, h:h + 1], in1=pair(d[:, 0:128], 1), op0=ALU.mult, op1=ALU.mult), t, td, xpf, inv)
                    D.hold(dn, tx)
                    s["t_xp"][b, c0 + x] = tx
                    ts.append(tx)
                    s["t_scan"] = td
                bk.hold(bn, ts)

            def decays(b):
                n = 2 * b + half
                an, a, af = abc.take()
                tl = Q.dma("sync", f"ab{an}", a[:, :],
                           scratch["a"][h:h + 1, n * 512:n * 512 + 512].rearrange("a t -> (a t)").partition_broadcast(128), af)
                return an, tl

            for b in range(2):
                an = decays(b)
                for pi, p in ((1, "Wk"), (2, "Wv"), (0, "Wq")):
                    conv(pi, p, b)
                    yield
                    if b == 1 and p == "Wk":
                        turn_kv(0, 0)
                        turn_kv(0, 2)
                        yield
                    if b == 1 and p == "Wv":
                        scores(0, 0, an0)
                        scores(0, 2, an0)
                        abc.hold(an0[0], s["t_scan"])
                        yield
                an0 = an if b == 0 else an0
            if half == 1:
                for p in ("Wk", "Wv", "Wq"):
                    wh.hold(W[p][0], Q.last["tensor"])
            turn_kv(1, 0)
            turn_kv(1, 2)
            yield
            scores(1, 0, an)
            scores(1, 2, an)
            abc.hold(an[0], s["t_scan"])
            yield
            tx = list(s["t_xp"].values())
            prev = s_prev.get("inv")
            t = []
            for q in range(4):
                qs = slice(32 * q, 32 * q + 32)
                t.append(A(lambda e, qs=qs: e.copy(XD[qs, 0:8, :], X[qs, :, qs]), tx, prev, t_i))
            tm = V(lambda e: e.tensor_tensor(XM[:, :, :], XD[:, :, :], cst[:, C_M16:C_M16 + 32].unsqueeze(1)
                                             .to_broadcast([128, 16, 32]), ALU.mult), t, prev)
            to = G(lambda e: e.tensor_tensor(XO[:, :, :], XD[:, 0:8, :], cst[:, C_OFF:C_OFF + 32].unsqueeze(1)
                                             .to_broadcast([128, 8, 32]), ALU.mult), t, prev)
            t = V(lambda e: e.transpose(YY[:, :, :], XM[:, :, :].rearrange("p m (s t) -> p t s m", s=2)), tm, prev)
            ta = V(lambda e: e.tensor_tensor(A16[:, :, :], YY[:, :, 0:16], YY[:, :, 16:32], ALU.add), t)
            tt = G(lambda e: e.memset(T16[:, :, :], 0.0), prev)
            tt = G(lambda e: e.memset(T16[:, :, :].rearrange("p a b -> p (a b)")[:, 0:256:17], 1.0), tt)
            for l in range(15):
                n = 15 - l
                pr = PR[:, 0:n * (l + 1)].rearrange("p (a b) -> p a b", a=n)
                tp = V(lambda e, l=l, n=n, pr=pr: e.tensor_tensor(
                    pr, A16[:, l + 1:16, l:l + 1].to_broadcast([128, n, l + 1]),
                    T16[:, l:l + 1, 0:l + 1].to_broadcast([128, n, l + 1]), ALU.mult), ta, tt)
                tt = V(lambda e, l=l, pr=pr: e.tensor_tensor(T16[:, l + 1:16, 0:l + 1], T16[:, l + 1:16, 0:l + 1],
                                                             pr, ALU.add), tp)
            te = []
            for s2 in range(2):
                fl = cst[:, C_FLAG + s2:C_FLAG + s2 + 1]
                te.append(A(lambda e, s2=s2, fl=fl: e.activation(E1[:, 0, :, s2, :], T16[:, :, :], ACT.Copy, scale=fl), tt, prev))
                te.append(A(lambda e, s2=s2, fl=fl: e.activation(E1[:, 1, :, s2, :], T16[:, :, :].rearrange("p t j -> p j t"),
                                                                 ACT.Copy, scale=fl), tt, prev))
            tn = [V(lambda e, w=w: e.transpose(MN[:, w, :, :].rearrange("p m (s t) -> p t s m", s=2),
                                               E1[:, w, :, :, :].rearrange("p a s b -> p a (s b)")), te, prev) for w in range(2)]
            yield
            zb = [bk.take() for _ in range(4)]
            tz = []
            for q in range(4):
                qs = slice(32 * q, 32 * q + 32)
                bn, kb, f = zb[q]

                def go(e, qs=qs, kb=kb):
                    for m in range(8):
                        r = e.matmul(kb[qs, m * 32:m * 32 + 32], XO[qs, m, :], MN[qs, 1, m, :], start=True, stop=True)
                    return r
                t = P(go, to, tn, f)
                tz.append(A(lambda e, qs=qs, kb=kb: e.copy(ZS[qs, :, :], kb[qs, 0:256].rearrange("p (m t) -> p m t", m=8)),
                            t, prev))
                bk.hold(bn, tz[-1])
            yield
            zb = [bk.take() for _ in range(4)]
            tmn = []
            for q in range(4):
                qs = slice(32 * q, 32 * q + 32)
                bn, kb, f = zb[q]

                def go(e, qs=qs, kb=kb):
                    for m in range(8):
                        e.matmul(kb[qs, m * 32:m * 32 + 32], ZS[qs, m, :], MN[qs, 0, m, :], start=True, stop=True)
                        r = e.matmul(kb[qs, 256 + m * 32:288 + m * 32], MN[qs, 0, m, :], ZS[qs, m, :], start=True, stop=True)
                    return r
                t = P(go, tz[q], f)
                tmn.append(V(lambda e, qs=qs, kb=kb: e.tensor_tensor(
                    MN[qs, :, 0:8, :], MN[qs, :, 0:8, :], kb[qs, :].rearrange("p (a m t) -> p a m t", a=2, m=8), ALU.add), t))
                bk.hold(bn, tmn[-1])
            tmf = []
            for q in range(4):
                qs = slice(32 * q, 32 * q + 32)
                tmf.append(A(lambda e, qs=qs: e.copy(mf[qs, :, qs], MN[qs, 0, 0:8, :]), tmn[q], mff, t_i))
            for q in range(2):
                qs = slice(32 * q, 32 * q + 32)
                tmf.append(A(lambda e, qs=qs: e.copy(NF[qs, :, qs], MN[qs, 1, 0:8, :]), tmn[q], prev, t_i))
            yield
            zb = [bk.take() for _ in range(2)]
            tz = []
            for p in range(2):
                sa, sb_ = slice(64 * p, 64 * p + 32), slice(64 * p + 32, 64 * p + 64)
                bn, kb, f = zb[p]

                def go(e, sa=sa, sb_=sb_, kb=kb):
                    for m in range(8):
                        r = e.matmul(kb[sb_, m * 32:m * 32 + 32], X[sa, m, sb_], MN[sa, 1, m, :], start=True, stop=True)
                    return r
                t = P(go, tmn, f, tx)
                tz.append(A(lambda e, sb_=sb_, kb=kb: e.activation(
                    ZT[sb_, :, :], kb[sb_, 0:256].rearrange("p (m t) -> p m t", m=8), ACT.Copy, scale=-1.0), t, prev))
                bk.hold(bn, tz[-1])
            yield
            zb = [bk.take() for _ in range(2)]
            for p in range(2):
                sa, sb_ = slice(64 * p, 64 * p + 32), slice(64 * p + 32, 64 * p + 64)
                bn, kb, f = zb[p]

                def go(e, sa=sa, sb_=sb_, kb=kb, p=p):
                    for m in range(8):
                        r = e.matmul(kb[sa, m * 32:m * 32 + 32], ZT[sb_, m, :], MN[sb_, 0, m, :], start=True, stop=True)
                        if p == 0:
                            r = e.matmul(kb[sb_, 256 + m * 32:288 + m * 32], MN[sb_, 0, m, :], ZT[sb_, m, :],
                                         start=True, stop=True)
                    return r
                t = P(go, tz[p], f)
                ts = [V(lambda e, sa=sa, sb_=sb_, kb=kb: e.tensor_copy(
                    mf[sa, :, sb_], kb[sa, 0:256].rearrange("p (m t) -> p m t", m=8)), t, mff)]
                if p == 0:
                    ts.append(V(lambda e, kb=kb: e.tensor_copy(
                        NF[32:64, :, 0:32], kb[32:64, 256:512].rearrange("p (m t) -> p m t", m=8)), t, tmf))
                tmf += ts
                bk.hold(bn, ts)
            yield
            bn, kb, f = bk.take()

            def go(e, kb=kb):
                for m in range(8):
                    r = e.matmul(kb[64:128, m * 64:m * 64 + 64], X[0:64, m, 64:128], NF[0:64, m, :], start=True, stop=True)
                return r
            t = P(go, tmf, f)
            tz = A(lambda e, kb=kb: e.activation(Z2[64:128, :, :], kb[64:128, :].rearrange("p (m t) -> p m t", m=8),
                                                 ACT.Copy, scale=-1.0), t, prev)
            bk.hold(bn, tz)
            yield
            bn, kb, f = bk.take()

            def go(e, kb=kb):
                for m in range(8):
                    r = e.matmul(kb[0:64, m * 64:m * 64 + 64], Z2[64:128, m, :], mf[64:128, m, 64:128], start=True, stop=True)
                return r
            t = P(go, tz, tmf, f)
            tl = V(lambda e, kb=kb: e.tensor_copy(mf[0:64, :, 64:128], kb[0:64, :].rearrange("p (m t) -> p m t", m=8)), t)
            bk.hold(bn, tl)
            s["t_mf"] = [tl, tmf]
            s_prev["inv"] = [t, tl, tmf, tn, tmn]
            yield

        s_prev = {}
        st = {"S": [done]}

        def stage_b(u):
            h, half = divmod(u, 2)
            s = unit[u]
            kq, qg, kd, vc, xp, mf = (s[k] for k in ("kq", "qg", "kd", "vc", "xp", "mf"))
            if half == 0:
                W["g"] = weight("Wg", h)
            osn, os_, osf = OS.take()
            to = []
            wait_s = st["S"]
            for ch in range(4):
                first = half == 0 and ch == 0
                if not first:
                    def go(e, ch=ch):
                        for b in range(2):
                            r = e.matmul(bank[4][:, b * 128:b * 128 + 128], kq[:, b, ch, :], ST[:, b, :],
                                         start=True, stop=True)
                        return r
                    t = P(go, wait_s, fb[4])
                    rn, r_, rf = R.take()
                    tr = []
                    for b in range(2):
                        i = b * 8 + half * 4 + ch
                        tr.append(V(lambda e, b=b, i=i, ch=ch, r_=r_: e.scalar_tensor_tensor(
                            out=r_[:, b, :], in0=bank[4][:, b * 128:b * 128 + 128], scalar=coef[:, i, 0, h:h + 1],
                            in1=vc[:, b, ch, :], op0=ALU.mult, op1=ALU.add), t, rf, s["t_vc"][b, ch]))
                    fb[4] = tr
                    right = r_
                    rhs = lambda b, r_=r_: r_[:, b, :]
                else:
                    tr = [s["t_vc"][0, ch], s["t_vc"][1, ch]]
                    rhs = lambda b: vc[:, b, 0, :]

                def go(e, ch=ch, rhs=rhs):
                    for b in range(2):
                        r = e.matmul(bank[5][:, b * 128:b * 128 + 128], mf[:, b * 4 + ch, :], rhs(b), start=True, stop=True)
                    return r
                tw = P(go, tr, s["t_mf"], fb[5])
                if not first:
                    R.hold(rn, tw)
                wn, ws, wf = WS.take()
                tws = A(lambda e, ws=ws: e.copy(ws[:, :, :], bank[5][:, 0:256].rearrange("p (b t) -> p b t", b=2)), tw, wf)
                fb[5] = [tws]

                def go(e, ch=ch, ws=ws):
                    for b in range(2):
                        r = e.matmul(bank[6][:, b * 128:b * 128 + 128], kd[:, b, ch, :], ws[:, b, :], start=True, stop=True)
                    return r
                tds = P(go, tws, fb[6])

                def go(e, ch=ch, ws=ws, first=first):
                    for b in range(2):
                        o = bank[7][:, b * 128:b * 128 + 128]
                        if not first:
                            e.matmul(o, ST[:, b, :], qg[:, b, ch, :], start=True, stop=False)
                        r = e.matmul(o, ws[:, b, :], xp[:, b * 4 + ch, :], start=first, stop=True)
                    return r
                tp = P(go, fb[7], s["t_qg", 0], s["t_qg", 1])
                WS.hold(wn, tp)
                ts = []
                for b in range(2):
                    i = b * 8 + half * 4 + ch
                    if first:
                        ts.append(V(lambda e, b=b: e.tensor_copy(ST[:, b, :], bank[6][:, b * 128:b * 128 + 128]), tds, wait_s, tp))
                    else:
                        ts.append(V(lambda e, b=b, i=i: e.scalar_tensor_tensor(
                            out=ST[:, b, :], in0=ST[:, b, :], scalar=GC[:, h, i:i + 1],
                            in1=bank[6][:, b * 128:b * 128 + 128], op0=ALU.mult, op1=ALU.add), tds, tp))
                fb[6] = ts
                wait_s = ts
                toc = A(lambda e, ch=ch, os_=os_: e.copy(os_[:, :, ch, :], bank[7][:, 0:256].rearrange("p (b t) -> p b t", b=2)),
                        tp, osf)
                fb[7] = [toc]
                to.append(toc)
                yield
            st["S"] = wait_s + [tp]
            for r, k in ((KQ, "kqn"), (QG, "qgn"), (KD, "kdn"), (VC, "vcn"), (XP, "xpn"), (MF, "mfn")):
                r.hold(s[k], tp, ts)
            for b in range(2):
                gbn, gb, t = project(W["g"], 2 * b + half)
                gn, g, gf = gg.take()
                tg = A(lambda e, g=g, gb=gb: e.activation(g[:, :], gb[:, :], ACT.Sigmoid), t, gf)
                bk.hold(gbn, tg)
                if half == 1 and b == 1:
                    wh.hold(W["g"][0], t)
                yield
                o = os_[:, b, :, :].rearrange("p c t -> p (c t)")
                qn, q_, qf = sq.take()
                tq = A(lambda e, o=o, q_=q_: e.activation(q_[:, :], o, ACT.Square), to, qf)
                vbn, vb, f = bk.take()
                t = P(lambda e, vb=vb, q_=q_: e.matmul(vb[:, :], jmat, q_[:, :], start=True, stop=True), tq, f)
                sq.hold(qn, t)
                rn, r_, rf = rs.take()
                t = A(lambda e, vb=vb, r_=r_: e.activation(r_[:, :], vb[:, :], ACT.Sqrt, bias=eps[:, 0:1]), t, rf)
                bk.hold(vbn, t)
                t = V(lambda e, r_=r_: e.reciprocal(r_[:, :], r_[:, :]), t)
                t = V(lambda e, r_=r_, o=o: e.tensor_tensor(r_[:, :], r_[:, :], o, ALU.mult), t)
                tos = t
                t = V(lambda e, r_=r_: e.tensor_scalar(r_[:, :], r_[:, :], lnw[:, 0:1], lnw[:, 1:2], ALU.mult, ALU.add), t, t_ln)
                t = V(lambda e, r_=r_, g=g: e.tensor_tensor(r_[:, :], r_[:, :], g[:, :], ALU.mult), t, tg)
                gg.hold(gn, t)
                t = Q.dma("sync", f"og{rn}", scratch["og"][h * 128:(h + 1) * 128, b * 1024 + half * 512:b * 1024 + half * 512 + 512],
                          r_[:, :], t)
                rs.hold(rn, t)
                yield
            OS.hold(osn, tos)

        NU = 2 * H
        for _ in stage_a(0):
            pass
        for u in range(1, NU):
            merged((16, stage_a(u)), (7, stage_b(u - 1)))
        for _ in stage_b(NU - 1):
            pass
        return Q.everything()


def mix0(nc, Q, sb, io, scratch, bank, split, cst, done):
    V = lambda fn, *a: Q.op("vector", fn, *a)
    A = lambda fn, *a: Q.op("scalar", fn, *a)
    P = lambda fn, *a: Q.op("tensor", fn, *a)
    with ExitStack() as c:
        def ring(name, n, shape, dt=F32):
            r = Ring([sb(c, f"{name}{i}", shape, dt) for i in range(n)])
            for i in range(n):
                r.hold(i, done)
            return r
        WOH = sb(c, "WOH", [128, 16, 512], F32R)
        WOL = sb(c, "WOL", [128, 16, 512], F32R)
        raw = ring("mr", 3, [128, 512])
        og = ring("mo", 4, [128, 512])
        oh = ring("moh", 3, [128, 512], F32R)
        ol = ring("mol", 3, [128, 512], F32R)
        g0 = ring("mg", 2, [128, 4, 512])
        xT = ring("mx", 2, [128, 4, 512])
        xr = ring("mxr", 3, [128, 512])
        bk = Ring(bank)
        for i in range(8):
            bk.hold(i, done)
        tw = []
        pend = []

        def rows(n, x1, tx1, nx):
            for q in range(4):
                i = n * 4 + q
                b, kb, f = bk.take()

                def go(e, q=q, kb=kb):
                    for k in range(4):
                        m = e.transpose(kb[:, k * 128:(k + 1) * 128], x1[:, k, q * 128:(q + 1) * 128], cst[:, 0:128])
                    return m
                t = P(go, tx1, f)
                m, r, f = xr.take()
                t2 = A(lambda e, kb=kb, r=r: e.copy(r[:, :], kb[:, :]), t, f)
                bk.hold(b, t2)
                xr.hold(m, Q.dma("scalar", f"mxr{m}", scratch["x1"][i * 128:(i + 1) * 128, :], r[:, :], t2))
            xT.hold(nx, t)

        for n in range(4):
            sl = slice(n * 512, n * 512 + 512)
            ng, g, f = g0.take()
            tg = Q.dma("scalar", f"mg{ng}", g[:, :, :], scratch["g0"].rearrange("(k p) t -> p k t", p=128)[:, :, sl], f)
            nx, x, f = xT.take()
            tx = Q.dma("scalar", f"mx{nx}", x[:, :, :], io["xT"].rearrange("(k p) t -> p k t", p=128)[:, :, sl], f)
            bks = [bk.take() for _ in range(4)]
            for k in range(16):
                if n == 0:
                    m, r, f = raw.take()
                    t = Q.dma("sync", f"mr{m}", r[:, :], io["Wo"][k * 128:(k + 1) * 128, :], f)
                    ts = split(r[:, :], WOH[:, k, :], WOL[:, k, :], t, done, low_eng="gpsimd")
                    raw.hold(m, ts)
                    tw.append(ts)
                m, o, f = og.take()
                t = Q.dma("sync", f"mo{m}", o[:, :], scratch["og"][k * 128:(k + 1) * 128, sl], f)
                mh, h, fh = oh.take()
                ml, l, fl = ol.take()
                ts = split(o[:, :], h[:, :], l[:, :], t, [fh, fl], low_eng="vector")
                og.hold(m, ts)
                for j in range(4):
                    tp = P(lambda e, j=j, k=k, h=h, l=l, kb=bks[j][1]: mm3(e, kb[:, :], [
                        (WOH[:, k, j * 128:(j + 1) * 128], WOL[:, k, j * 128:(j + 1) * 128], h[:, :], l[:, :])],
                        first=k == 0, last=k == 15), ts, tw[k], bks[j][2])
                oh.hold(mh, tp)
                ol.hold(ml, tp)
                if k == 3 and pend:
                    rows(*pend.pop())
            tv = []
            for j in range(4):
                t = V(lambda e, j=j, kb=bks[j][1], g=g: e.tensor_tensor(g[:, j, :], g[:, j, :], kb[:, :], ALU.mult), tp, tg)
                bk.hold(bks[j][0], t)
                tv.append(V(lambda e, j=j, g=g, x=x: e.tensor_tensor(x[:, j, :], x[:, j, :], g[:, j, :], ALU.add), t, tx))
            g0.hold(ng, tv)
            pend.append((n, x, tv, nx))
        rows(*pend.pop())
        return Q.everything()


def attn1(nc, Q, sb, io, scratch, bank, XN, one, done):
    V = lambda fn, *a: Q.op("vector", fn, *a)
    A = lambda fn, *a: Q.op("scalar", fn, *a)
    P = lambda fn, *a: Q.op("tensor", fn, *a)
    G = lambda fn, *a: Q.op("gpsimd", fn, *a)
    with ExitStack() as c:
        v = sb(c, "l1v", [128, 4, 3])
        wi = sb(c, "wi", [128, 4, 128])
        wa = sb(c, "wa", [128, 4, 128])
        t_v = Q.dma("sync", "l1v", v[:, :, :], io["l1v"], done)
        t_wi = Q.dma("sync", "l1wi", wi[:, :, :], io["ig_w"].rearrange("k p n -> p k n"), done)
        t_wa = Q.dma("sync", "l1wa", wa[:, :, :], io["ag_w"].rearrange("k p n -> p k n"), done)
        sp = sb(c, "sp", [128, 8, 4])
        row = lambda i: sp[:, i, :]
        p = v[:, :, 2]
        t = A(lambda e: e.activation(row(0), p, ACT.Abs), t_v)
        t = A(lambda e: e.activation(row(1), row(0), ACT.Exp, scale=-1.0), t)
        t = V(lambda e: e.tensor_scalar(row(2), row(1), 2.0, None, ALU.add), t)
        t = V(lambda e: e.reciprocal(row(3), row(2)), t)
        t = V(lambda e: e.tensor_tensor(row(2), row(1), row(3), ALU.mult), t)
        t = V(lambda e: e.tensor_tensor(row(4), row(2), row(2), ALU.mult), t)
        t = V(lambda e: e.tensor_scalar(row(5), row(4), 2.0 / 17, 2.0 / 15, ALU.mult, ALU.add), t)
        for k in (13, 11, 9, 7, 5, 3, 1):
            t = V(lambda e: e.tensor_tensor(row(5), row(5), row(4), ALU.mult), t)
            t = V(lambda e, k=k: e.tensor_scalar(row(5), row(5), 2.0 / k, None, ALU.add), t)
        t = V(lambda e: e.tensor_tensor(row(5), row(5), row(2), ALU.mult), t)
        t = V(lambda e: e.tensor_scalar(row(6), p, 0.0, None, ALU.max), t)
        t = V(lambda e: e.tensor_tensor(row(6), row(6), row(5), ALU.add), t)
        t1 = V(lambda e: e.tensor_scalar(row(5), row(6), -8.0, None, ALU.mult), t)
        t_sp = V(lambda e: e.tensor_scalar(row(7), row(6), -16.0, None, ALU.mult), t1)
        gx = [sb(c, f"gx{i}", [128, T]) for i in range(2)]
        ga = [sb(c, f"ga{i}", [128, T]) for i in range(2)]
        am = [sb(c, f"am{i}", [128, T]) for i in range(1)]
        free = [[done], [done]]
        fam = [done]
        fb = [[done] for _ in range(8)]
        for k in range(4):
            s = k % 2
            X, Y, M = gx[s], ga[s], am[0]
            tg = []
            for n in range(4):
                sl = slice(n * 512, n * 512 + 512)
                t = P(lambda e, n=n, sl=sl, k=k: e.matmul(bank[n][:, :], wi[:, k, :], XN[:, k, sl], start=True, stop=True),
                      t_wi, fb[n], done)
                fb[n] = [A(lambda e, n=n, sl=sl, k=k, X=X: e.activation(X[:, sl], bank[n][:, :], ACT.Sigmoid,
                                                                        bias=v[:, k, 0:1]), t, free[s], t_v)]
                t = P(lambda e, n=n, sl=sl, k=k: e.matmul(bank[4 + n][:, :], wa[:, k, :], XN[:, k, sl], start=True, stop=True),
                      t_wa, fb[4 + n], done)
                fb[4 + n] = [A(lambda e, n=n, sl=sl, k=k, Y=Y: e.activation(Y[:, sl], bank[4 + n][:, :], ACT.Sigmoid,
                                                                            bias=v[:, k, 1:2]), t, free[s])]
                tg += [fb[n], fb[4 + n]]
            ta = A(lambda e, k=k, M=M, Y=Y: e.activation(M[:, :], Y[:, :], ACT.Exp, scale=sp[:, 7, k:k + 1]), tg, t_sp, fam)
            tb = A(lambda e, k=k, Y=Y: e.activation(Y[:, :], Y[:, :], ACT.Exp, scale=sp[:, 5, k:k + 1]), ta)
            ta = A(lambda e, M=M: e.activation(M[:, :], M[:, :], ACT.Sqrt, bias=one[:, 0:1], scale=-1.0), ta)
            ta = V(lambda e, M=M: e.memset(M[:, 0:T:1024], 1.0), ta)
            t = V(lambda e, X=X, k=k: e.tensor_tensor(X[:, :], X[:, :], XN[:, k, :], ALU.mult), tg)
            t = V(lambda e, X=X, M=M: e.tensor_tensor(X[:, :], X[:, :], M[:, :], ALU.mult), t, ta)
            fam = [t]
            tt = [V(lambda e, X=X, Y=Y, b=b: e.tensor_tensor_scan(
                X[:, b * 1024:b * 1024 + 1024], Y[:, b * 1024:b * 1024 + 1024], X[:, b * 1024:b * 1024 + 1024],
                0.0, ALU.mult, ALU.add), t, tb) for b in range(2)]
            free[s] = [Q.dma("sync", f"s1{s}", scratch["s1"][k * 128:(k + 1) * 128, :], X[:, :], tt)]
        return Q.everything()


def ffn1(nc, Q, sb, io, scratch, bank, split, XH, XL, done):
    V = lambda fn, *a: Q.op("vector", fn, *a)
    A = lambda fn, *a: Q.op("scalar", fn, *a)
    P = lambda fn, *a: Q.op("tensor", fn, *a)
    G = lambda fn, *a: Q.op("gpsimd", fn, *a)
    with ExitStack() as c:
        def ring(name, n, shape, dt=F32):
            r = Ring([sb(c, f"{name}{i}", shape, dt) for i in range(n)])
            for i in range(n):
                r.hold(i, done)
            return r
        pk = ring("pk", 2, [128, 512], I32)
        sc = ring("sc", 2, [128, 512])
        w1 = ring("w1", 1, [128, 512], I32)
        w2 = ring("w2", 1, [128, 512], I32)
        wf = ring("wf", 1, [128, 2, 512])
        wh = ring("qh", 4, [128, 2, 512], F32R)
        wl = [sb(c, f"ql{i}", [128, 2, 512], F32R) for i in range(4)]
        HH = sb(c, "QHH", [128, 2, T], F32R)
        HL = sb(c, "QHL", [128, 2, T], F32R)
        ACC = sb(c, "QACC", [128, 4, T])
        g2 = ring("g2", 2, [128, 512])
        hd = ring("qhd", 2, [128, 512])
        bk = Ring(bank)
        for i in range(8):
            bk.hold(i, done)

        def weight(pk_src, sc_src):
            n, r, f = pk.take()
            tp = [Q.dma("sync", f"pk{n}", r[:, a:b], s, f) for a, b, s in pk_src]
            m, s_, f = sc.take()
            ts = [Q.dma("sync", f"sc{m}", s_[p0:p0 + 128, a:b], s, f) for p0, a, b, s in sc_src]
            i1, a, f1 = w1.take()
            i2, b, f2 = w2.take()
            t = V(lambda e: e.tensor_scalar(a[:, :], r[:, :], 255, None, ALU.bitwise_and), tp, f1)
            pk.hold(n, t)
            t = V(lambda e: e.tensor_scalar(b[:, :], a[:, :], 12, None, ALU.logical_shift_left), t, f2)
            t = V(lambda e: e.tensor_tensor(a[:, :], a[:, :], b[:, :], ALU.bitwise_or), t)
            t = V(lambda e: e.tensor_scalar(b[:, :], a[:, :], 9, 0x0E000E00, ALU.logical_shift_left, ALU.bitwise_and), t)
            t = V(lambda e: e.tensor_scalar(a[:, :], a[:, :], 12, -0x7FFF8000, ALU.logical_shift_left, ALU.bitwise_and), t)
            t = V(lambda e: e.tensor_tensor(a[:, :], a[:, :], b[:, :], ALU.bitwise_or), t)
            w1.hold(i1, t)
            w2.hold(i2, t)
            i3, w, f3 = wf.take()
            half = a[:, :].bitcast(F16).rearrange("p (n s) -> p n s", s=2)
            tw = [V(lambda e, s2=s2: e.scalar_tensor_tensor(out=w[:, s2, :], in0=half[:, :, s2], scalar=16384.0,
                                                            in1=s_[:, :], op0=ALU.mult, op1=ALU.mult), t, ts, f3)
                  for s2 in range(2)]
            w1.hold(i1, tw)
            sc.hold(m, tw)
            i4, h, f4 = wh.take()
            th = split(w[:, :, :], h[:, :, :], wl[i4][:, :, :], tw, f4, low_eng="gpsimd")
            wf.hold(i3, th)
            return i4, h, wl[i4], th

        tH = [[done] for _ in range(4)]
        tA = {}
        Q.x = None
        prev_down = None

        def down(j, hs, wd):
            for o in range(4):
                for n in range(4):
                    sl = slice(n * 512, n * 512 + 512)
                    b, kb, f = bk.take()
                    i4, w, wlo, tw = wd
                    t = P(lambda e, kb=kb, o=o, sl=sl: mm3(e, kb[:, :], [
                        (w[:, s2, o * 128:(o + 1) * 128], wlo[:, s2, o * 128:(o + 1) * 128], HH[:, s2, sl], HL[:, s2, sl])
                        for s2 in range(2)]), tw, hs[n], f)
                    if j == 0:
                        ta = A(lambda e, kb=kb, o=o, sl=sl: e.copy(ACC[:, o, sl], kb[:, :]), t)
                    else:
                        ta = V(lambda e, kb=kb, o=o, sl=sl: e.tensor_tensor(ACC[:, o, sl], ACC[:, o, sl], kb[:, :],
                                                                            ALU.add), t, tA[(o, n)])
                    tA[(o, n)] = ta
                    bk.hold(b, ta)
                    tH[n] = [t]
            wh.hold(wd[0], t)

        def weights(j):
            out = []
            for p in ("gate", "up"):
                src = io[p + "_pk"]
                scs = io[p + "_sc"]
                cols = slice(j * 256, j * 256 + 256)
                out.append(weight(
                    [(q * 256, q * 256 + 256, src[q * 128:(q + 1) * 128, cols]) for q in range(2)],
                    [(0, q * 256, q * 256 + 256, scs[q * 8:q * 8 + 8, cols].unsqueeze(1).to_broadcast([8, 16, 256]))
                     for q in range(2)]))
            out.append(weight([(0, 512, io["down_pk"][j * 128:(j + 1) * 128, :])],
                              [(0, 0, 512, io["down_scT"][j * 8:j * 8 + 8, :].unsqueeze(1).to_broadcast([8, 16, 512]))]))
            return out

        wnext = weights(0)
        for j in range(16):
            wg, wu, wd = wnext
            hs = [[] for _ in range(4)]
            for s2 in range(2):
                cs = [(q * 256 + s2 * 128, q * 256 + s2 * 128 + 128) for q in range(2)]
                for n in range(4):
                    sl = slice(n * 512, n * 512 + 512)

                    def mats(w):
                        return [(w[1][:, par, cs[q][0]:cs[q][1]], w[2][:, par, cs[q][0]:cs[q][1]],
                                 XH[:, 2 * q + par, sl], XL[:, 2 * q + par, sl]) for q in range(2) for par in range(2)]
                    b1, k1, f1 = bk.take()
                    t1 = P(lambda e, k1=k1, m=mats(wg): mm3(e, k1[:, :], m), wg[3], f1)
                    b2, k2, f2 = bk.take()
                    t2 = P(lambda e, k2=k2, m=mats(wu): mm3(e, k2[:, :], m), wu[3], f2)
                    m, s, f = g2.take()
                    t = A(lambda e, s=s, k1=k1: e.activation(s[:, :], k1[:, :], ACT.Square), t1, f)
                    t = V(lambda e, s=s, k1=k1: e.scalar_tensor_tensor(out=s[:, :], in0=s[:, :], scalar=1.0 / 0.044715,
                                                                       in1=k1[:, :], op0=ALU.add, op1=ALU.mult), t)
                    t = A(lambda e, s=s: e.activation(s[:, :], s[:, :], ACT.Tanh, scale=0.7978845608028654 * 0.044715), t)
                    t = V(lambda e, s=s, k1=k1: e.scalar_tensor_tensor(out=s[:, :], in0=s[:, :], scalar=1.0,
                                                                       in1=k1[:, :], op0=ALU.add, op1=ALU.mult), t)
                    bk.hold(b1, t)
                    m2, h, f = hd.take()
                    th = V(lambda e, h=h, s=s, k2=k2: e.scalar_tensor_tensor(out=h[:, :], in0=s[:, :], scalar=0.5,
                                                                             in1=k2[:, :], op0=ALU.mult, op1=ALU.mult), t, t2, f)
                    bk.hold(b2, th)
                    g2.hold(m, th)
                    tt = split(h[:, :], HH[:, s2, sl], HL[:, s2, sl], th, tH[n], low_eng="gpsimd")
                    hd.hold(m2, tt)
                    hs[n] += tt
            wh.hold(wg[0], t1)
            wh.hold(wu[0], t2)
            if j < 15:
                wnext = weights(j + 1)
            down(j, hs, wd)
        sd = None
        for o in range(4):
            for n in range(4):
                sl = slice(n * 512, n * 512 + 512)
                t = A(lambda e, o=o, sl=sl: e.activation(ACC[:, o, sl], ACC[:, o, sl], ACT.Silu), tA[(o, n)])
            Q.dma("sync", "g1d", scratch["g1"][o * 128:(o + 1) * 128, :], ACC[:, o, :], t)
        return Q.everything()


def laid_out(inputs):
    g = {k: np.ascontiguousarray(np.asarray(v)) for k, v in inputs.items()}
    f = np.float32
    x = g["L0_attn_x"].reshape(T, 512)
    o = {"x": x, "xT": x.T}
    for n in ("Wq", "Wk", "Wv", "Wg", "Wo"):
        o[n] = g["L0_attn_" + n]
    wab = np.zeros((512, 128), f)
    wab[:, 0:16], wab[:, 32:48] = g["L0_attn_Wa"], g["L0_attn_Wb"]
    bab = np.zeros((128, 1), f)
    bab[0:16, 0], bab[32:48, 0] = g["L0_attn_ba"], g["L0_attn_bb"]
    o["Wab"], o["bab"] = wab, bab
    cw = np.zeros((128, 16, 3, 5), f)
    for i, n in enumerate("qkv"):
        cw[:, :, i, 0:4] = g[f"L0_attn_{n}cw"].reshape(16, 128, 4).transpose(1, 0, 2)
        cw[:, :, i, 4] = g[f"L0_attn_{n}cb"].reshape(16, 128).T
    o["cw"] = cw
    o["ln"] = np.stack([g["L0_attn_ln_w"], g["L0_attn_ln_b"]], 1)
    o["gate_wT"], o["up_wT"] = g["L0_ffn_gate_w"].T, g["L0_ffn_up_w"].T
    o["down_wT"] = g["L0_ffn_down_w"].T
    s = np.zeros((128, 26), f)
    s[:, 0:11] = g["L0_ffn_gate_s"].reshape(11, 128).T
    s[:, 11:22] = g["L0_ffn_up_s"].reshape(11, 128).T
    s[:, 22:26] = g["L0_ffn_down_s"].reshape(4, 128).T
    o["ffn0_s"] = s
    for n in ("ig", "ag"):
        w = np.zeros((4, 128, 128), f)
        for h in range(16):
            a = 32 * (h % 4)
            w[h // 4, a:a + 32, a:a + 32] = g[f"L1_attn_{n}_w"][h]
        o[n + "_w"] = w
    v = np.zeros((128, 4, 3), f)
    v[:, :, 0] = g["L1_attn_ig_b"].reshape(4, 128).T
    v[:, :, 1] = g["L1_attn_ag_b"].reshape(4, 128).T
    v[:, :, 2] = g["L1_attn_a_param"].reshape(4, 128).T
    o["l1v"] = v
    n = np.arange(4096).reshape(16, 128, 2).transpose(0, 2, 1).reshape(-1)
    for p in ("gate", "up"):
        o[p + "_pk"] = g[f"L1_ffn_{p}_W_packed"].T[:, n]
        o[p + "_sc"] = g[f"L1_ffn_{p}_scales"].T[:, n]
    o["down_pk"] = g["L1_ffn_down_W_packed"].T
    o["down_scT"] = g["L1_ffn_down_scales"].T
    c = np.zeros((128, C_N), f)
    c[:, 0:128] = np.eye(128)
    c[:, C_CM:C_CM + 128] = np.eye(128) - 1.0 / 128
    c[:, C_J:C_J + 128] = 1.0 / 128
    r = np.arange(128) % 32 // 16
    cc = np.arange(32) // 16
    c[:, C_M16:C_M16 + 32] = -1.0 * (r[:, None] == cc[None, :])
    c[:, C_OFF:C_OFF + 32] = -1.0 * ((r[:, None] == 0) & (cc[None, :] == 1))
    c[:, C_FLAG] = r == 0
    c[:, C_FLAG + 1] = r == 1
    o["consts"] = c
    return {k: np.ascontiguousarray(a) for k, a in o.items()}


SCRATCH = {"a": [16, T], "g": [16, T], "gc": [256], "g0": [512, T], "og": [2048, T], "x1": [T, 512],
           "s1": [512, T], "g1": [512, T]}


def kernel(**inputs):
    import concourse.bacc as _bacc
    from concourse.bass_utils import run_bass_kernel_spmd as _run

    nc = _bacc.Bacc("TRN2", target_bir_lowering=False, num_devices=1)
    arrays, io = {}, {}
    for name, a in laid_out(inputs).items():
        arrays["in_" + name] = a
        io[name] = nc.dram_tensor("in_" + name, a.shape, mybir.dt.from_np(a.dtype), kind="ExternalInput").ap()
    out = {"y": nc.dram_tensor("out_y", [T, 512], F32, kind="ExternalOutput").ap()}
    scratch = {n: nc.dram_tensor("tmp_" + n, s, F32).ap() for n, s in SCRATCH.items()}
    program(nc, io, out, scratch)
    r = _run(nc, [arrays], core_ids=[0])
    return r.results[0]["out_y"].reshape(2, 1024, 512)
```

```python
from contextlib import ExitStack

import numpy as np

import concourse.bass as bass
from concourse import mybir

F32 = mybir.dt.float32
F32R = mybir.dt.float32r
F16 = mybir.dt.float16
I32 = mybir.dt.int32
ALU = mybir.AluOpType
ACT = mybir.ActivationFunctionType

T = 2048
H = 16
EPS = 1e-5

C_ID, C_CM, C_J, C_M16, C_OFF, C_FLAG, C_N = 0, 128, 256, 384, 416, 448, 450


class Tok:

    __slots__ = ("sem", "val", "used")

    def __init__(self, sem, val=None):
        self.sem, self.val, self.used = sem, val, False


class Queues:

    ENG = ("tensor", "vector", "scalar", "gpsimd", "sync")

    def __init__(self, nc, ctx):
        self.nc = nc
        self.q = {e: [] for e in self.ENG}
        self.sem = {e: ctx.enter_context(nc.semaphore("s_" + e)) for e in self.ENG}
        self.ctx = ctx
        self.count = {}
        self.last = {}

    def op(self, eng, fn, *after):
        t = Tok(eng)
        self.q[eng].append((fn, flat(after), t))
        self.last[eng] = t
        return t

    def dma(self, eng, name, out, in_, *after):
        if name not in self.sem:
            self.sem[name] = self.ctx.enter_context(self.nc.semaphore("d_" + name))
            self.count[name] = 0
        self.count[name] += 16
        t = Tok(name, self.count[name])
        self.q[eng].append((lambda e: e.dma_start(out, in_), flat(after), t))
        return t

    def everything(self):
        return list(self.last.values()) + [Tok(n, c) for n, c in self.count.items()]

    def emit(self, block):
        for items in self.q.values():
            for _, after, _ in items:
                for a in after:
                    a.used = True
        for items in self.q.values():
            n = 0
            for _, _, t in items:
                if t.val is None and t.used:
                    n += 1
                    t.val = n
                elif t.val is None:
                    t.val = 0
        for name in self.ENG:
            hook = {"tensor": block.tensor, "vector": block.vector, "scalar": block.scalar,
                            "gpsimd": block.gpsimd, "sync": block.sync}[name]

            def body(e, name=name):
                met = {}
                for fn, after, t in self.q[name]:
                    need = {}
                    for a in after:
                        need[a.sem] = max(need.get(a.sem, 0), a.val)
                    for s, v in need.items():
                        if v > met.get(s, 0):
                            e.wait_ge(self.sem[s], v)
                            met[s] = v
                    ins = fn(e)
                    if ins is not None and t.used:
                        ins.then_inc(self.sem[t.sem], 16 if t.sem in self.count else 1)
                    elif ins is not None and t.sem in self.count:
                        ins.then_inc(self.sem[t.sem], 16)

            hook(body)


def flat(xs):
    out = []
    for x in xs:
        if x is None:
            continue
        if isinstance(x, (list, tuple)):
            out += flat(x)
        else:
            out.append(x)
    return out


class Ring:

    def __init__(self, slots):
        self.slots, self.free, self.n = slots, [[] for _ in slots], -1

    def take(self):
        self.n = (self.n + 1) % len(self.slots)
        return self.n, self.slots[self.n], self.free[self.n]

    def hold(self, i, *users):
        self.free[i] = flat(users)


def mm3(e, out, pairs, first=True, last=True):
    n = len(pairs)
    for k, (wh, wl, xh, xl) in enumerate(pairs):
        e.matmul(out, wh, xh, start=first and k == 0, stop=False)
        e.matmul(out, wh, xl, start=False, stop=False)
        m = e.matmul(out, wl, xh, start=False, stop=last and k == n - 1)
    return m


def f32(ap):
    return ap.bitcast(F32)


def program(nc, io, out, scratch, stages=99):
    with ExitStack() as ctx:
        Q = Queues(nc, ctx)
        V = lambda fn, *a: Q.op("vector", fn, *a)
        A = lambda fn, *a: Q.op("scalar", fn, *a)
        P = lambda fn, *a: Q.op("tensor", fn, *a)
        G = lambda fn, *a: Q.op("gpsimd", fn, *a)

        def sb(c, name, shape, dt=F32):
            return c.enter_context(nc.sbuf_tensor("b_" + name, shape, dt))

        bank = [ctx.enter_context(nc.psum_tensor(f"bank{i}", [128, 512], F32)) for i in range(8)]
        cst = sb(ctx, "cst", [128, C_N])
        ident, cmat, jmat = cst[:, 0:128], cst[:, C_CM:C_CM + 128], cst[:, C_J:C_J + 128]
        eps = sb(ctx, "eps", [128, 1])
        one = sb(ctx, "one", [128, 1])
        t_cst = Q.dma("sync", "cst", cst[:, :], io["consts"])
        t_eps = V(lambda e: e.memset(eps[:, :], EPS))
        t_one = V(lambda e: e.memset(one[:, :], 1.0))

        def split(src, hi, lo, after, free=(), src_is_psum=False, low_eng="vector"):
            th = A(lambda e: e.copy(hi, src), after, free)
            tl = Q.op(low_eng, lambda e: e.tensor_tensor(lo, src, f32(hi), ALU.subtract), th, after, free)
            return [th, tl]

        def norm_rows(x, xn, c, tag, after):
            st = sb(c, "st" + tag, [128, 16, 6])
            mv = sb(c, "mv" + tag, [128, 16, 2])
            sd = sb(c, "sd" + tag, [128, 16])
            rs = sb(c, "rs" + tag, [128, 16])
            for i in range(16):
                t = V(lambda e, i=i: e.bn_stats(st[:, i, :], x[:, i, :]), after[i])
                t = V(lambda e, i=i: e.bn_aggr(mv[:, i, :], st[:, i, :]), t)
            t = A(lambda e: e.activation(sd[:, :], mv[:, :, 1], ACT.Sqrt, bias=eps[:, 0:1]), t, t_eps)
            t = V(lambda e: e.reciprocal(rs[:, :], sd[:, :]), t)
            return [V(lambda e, i=i: e.tensor_scalar(xn[:, i, :], x[:, i, :], mv[:, i, 0:1], rs[:, i:i + 1],
                                                     ALU.subtract, ALU.mult), t) for i in range(16)]

        def turned(xn, i, order, bk, after, free):
            def go(e):
                for k in range(4):
                    m = e.transpose(bk[:, k * 128:(k + 1) * 128], order(xn, i, k), ident)
                return m
            return P(go, after, free, t_cst)

        plain = lambda xn, i, k: xn[:, i, k * 128:(k + 1) * 128]
        byparity = lambda xn, i, k: xn[:, i, 256 * (k // 2) + k % 2:256 * (k // 2) + 256:2]

        layer = ctx.enter_context(ExitStack())
        XH = sb(layer, "XH", [128, 4, T], F32R)
        XL = sb(layer, "XL", [128, 4, T], F32R)
        coef = sb(layer, "coef", [128, 16, 3, 16])
        GC = sb(layer, "GC", [128, 16, 16])
        with ExitStack() as c:
            x = sb(c, "x0", [128, 16, 512])
            xn = sb(c, "xn0", [128, 16, 512])
            tx = [Q.dma("sync", f"x{i % 4}", x[:, i * 4:i * 4 + 4, :],
                        io["x"].rearrange("(i p) d -> p i d", p=128)[:, i * 4:i * 4 + 4, :]) for i in range(4)]
            tn = norm_rows(x, xn, c, "0", [tx[i // 4] for i in range(16)])
            wab = sb(c, "wab", [128, 4, 128])
            wabh = sb(c, "wabh", [128, 4, 128], F32R)
            wabl = sb(c, "wabl", [128, 4, 128], F32R)
            bab = sb(c, "bab", [128, 1])
            t_wab = Q.dma("sync", "wab", wab[:, :, :], io["Wab"].rearrange("(k p) n -> p k n", p=128))
            t_bab = Q.dma("sync", "bab", bab[:, :], io["bab"])
            t_ws = split(wab[:, :, :], wabh[:, :, :], wabl[:, :, :], t_wab)
            tb = [None] * 8
            tX = []
            for i in range(16):
                b = i % 4
                t = turned(xn, i, plain, bank[b], tn[i], tb[b])
                src = bank[b][:, :].rearrange("p (k t) -> p k t", k=4)
                tb[b] = split(src, XH[:, :, i * 128:(i + 1) * 128], XL[:, :, i * 128:(i + 1) * 128], t)
                tX.append(tb[b])
            S = sb(c, "S", [128, T])
            SG = sb(c, "SG", [128, T])
            Gm = sb(c, "Gm", [128, T])
            TB = sb(c, "TB", [128, T])
            BT = sb(c, "BT", [128, T])
            zero = sb(c, "zero", [128, 128])
            gc16 = sb(c, "gc16", [16, 16])
            t_z = V(lambda e: e.memset(zero[:, :], 0.0))
            t_tb = V(lambda e: e.memset(TB[:, :], 0.0))
            tS = []
            for n in range(4):
                sl = slice(n * 512, n * 512 + 512)
                t = P(lambda e, n=n, sl=sl: mm3(e, bank[4 + n][:, :], [
                    (wabh[:, k, :], wabl[:, k, :], XH[:, k, sl], XL[:, k, sl]) for k in range(4)]),
                    t_ws, tX[4 * n:4 * n + 4])
                tS.append(A(lambda e, n=n, sl=sl: e.activation(S[:, sl], bank[4 + n][:, :], ACT.Sigmoid,
                                                               bias=bab[:, 0:1]), t, t_bab))
            t1 = V(lambda e: e.memset(SG[0:16, :].rearrange("p (c t) -> p c t", t=128)[:, :, 127:128], 1.0))
            tg = []
            for ch in range(16):
                o = ch * 128
                a = V(lambda e, o=o: e.tensor_tensor_scan(Gm[0:16, o:o + 128], S[0:16, o:o + 128], zero[0:16, :],
                                                          1.0, ALU.mult, ALU.add), tS[ch // 4], t_z)
                lo = o - 1 if o else None
                b = V(lambda e, o=o: e.tensor_tensor_scan(SG[0:16, o:o + 127][:, ::-1], S[0:16, o + 1:o + 128][:, ::-1],
                                                          zero[0:16, 0:127], 1.0, ALU.mult, ALU.add), t1)
                tg += [a, b]
            t2 = V(lambda e: e.tensor_scalar(TB[0:16, 1:T], Gm[0:16, 0:T - 1], -1.0, None, ALU.mult), tg, t_tb)
            t2 = V(lambda e: e.memset(TB[0:16, :].rearrange("p (c t) -> p c t", t=128)[:, :, 0:1], -1.0), t2)
            t3 = V(lambda e: e.tensor_copy(TB[32:48, :], S[32:48, :]), tS, t_tb)
            t4 = V(lambda e: e.tensor_copy(BT[0:16, :], S[32:48, :]), tS)
            t5 = V(lambda e: e.tensor_tensor(TB[64:80, :], BT[0:16, :], SG[0:16, :], ALU.mult), t4, tg, t_tb)
            t6 = V(lambda e: e.tensor_copy(gc16[:, :], Gm[0:16, :].rearrange("p (c t) -> p c t", t=128)[:, :, 127]), tg)
            d1 = Q.dma("sync", "ad", scratch["a"], S[0:16, :], tS)
            d2 = Q.dma("sync", "gd", scratch["g"], Gm[0:16, :], tg)
            d3 = Q.dma("sync", "gcd", scratch["gc"].rearrange("(h c) -> h c", h=16), gc16[:, :], t6)
            t_gc = Q.dma("sync", "gcl", GC[:, :, :].rearrange("p h c -> p (h c)"),
                         scratch["gc"].partition_broadcast(128), d3)
            t_coef = []
            for i in range(16):
                b = i % 4
                t = P(lambda e, i=i, b=b: e.transpose(bank[b][:, 0:128], TB[:, i * 128:(i + 1) * 128], ident),
                      [t2, t3, t5], tb[b], t_cst)
                tb[b] = A(lambda e, i=i, b=b: e.copy(
                    coef[:, i, :, :], bank[b][:, 0:96].rearrange("p (q r) -> p q r", q=3)[:, :, 0:16]), t)
                t_coef.append(tb[b])
            t_scr = [d1, d2]
            done = Q.everything()
        if stages == 0:
            Q.dma("sync", "dbg", out["d0"], XH[:, :, :].bitcast(F32), done)
            Q.dma("sync", "dbg", out["d1"], XL[:, :, :].bitcast(F32), done)
            Q.dma("sync", "dbg", out["d2"], coef[:, :, :, :], done)
            Q.dma("sync", "dbg", out["d3"], GC[:, :, :], done)
        if stages >= 1:
            done = ffn0(nc, Q, sb, io, scratch, bank, split, XH, XL, done)
        if stages >= 2:
            done = attn0(nc, Q, sb, io, scratch, bank, split, XH, XL, coef, GC, cst, eps, done)
        layer.close()
        if stages >= 3:
            done = mix0(nc, Q, sb, io, scratch, bank, split, cst, done)
        if stages >= 4:
            lay = ctx.enter_context(ExitStack())
            YH = sb(lay, "XH1", [128, 4, T], F32R)
            YL = sb(lay, "XL1", [128, 4, T], F32R)
            with ExitStack() as c:
                x1 = sb(c, "x1", [128, 16, 512])
                t = Q.dma("sync", "x0", x1[:, :, :], scratch["x1"].rearrange("(i p) d -> p i d", p=128), done)
                tn = norm_rows(x1, x1, c, "1", [t] * 16)
                XN = sb(c, "XN", [128, 4, T])
                tb = [done] * 8
                for i in range(16):
                    b = i % 4
                    t = turned(x1, i, byparity, bank[b], tn[i], tb[b])
                    src = bank[b][:, :].rearrange("p (k t) -> p k t", k=4)
                    tb[b] = split(src, YH[:, :, i * 128:(i + 1) * 128], YL[:, :, i * 128:(i + 1) * 128], t)
                    t = turned(x1, i, plain, bank[4 + b], tn[i], tb[4 + b])
                    tb[4 + b] = A(lambda e, i=i, b=b: e.copy(XN[:, :, i * 128:(i + 1) * 128], bank[4 + b][:, :]
                                                             .rearrange("p (k t) -> p k t", k=4)), t)
                done = Q.everything()
                done = attn1(nc, Q, sb, io, scratch, bank, XN, one, done)
            done = ffn1(nc, Q, sb, io, scratch, bank, split, YH, YL, done)
            lay.close()
            final(nc, Q, sb, io, scratch, bank, cst, out, done)
        Q.op("sync", lambda e: None, Q.everything())
        block = ctx.enter_context(nc.Block())
        Q.emit(block)


def final(nc, Q, sb, io, scratch, bank, cst, out, done):
    with ExitStack() as c:
        x1 = Ring([sb(c, f"fx{i}", [128, 512]) for i in range(3)])
        s1 = Ring([sb(c, f"fs{i}", [128, 4, 128]) for i in range(3)])
        g1 = Ring([sb(c, f"fg{i}", [128, 4, 128]) for i in range(3)])
        pr = Ring([sb(c, f"fp{i}", [128, 4, 128]) for i in range(3)])
        oo = Ring([sb(c, f"fo{i}", [128, 512]) for i in range(3)])
        bk = Ring(bank)
        for i in range(16):
            sl = slice(i * 128, (i + 1) * 128)
            n, xt, f = x1.take()
            tx = Q.dma("sync", f"fx{n}", xt[:, :], scratch["x1"][sl, :], f, done)
            m, st, f = s1.take()
            ts = Q.dma("sync", f"fs{m}", st[:, :, :], scratch["s1"].rearrange("(k p) t -> p k t", p=128)[:, :, sl], f, done)
            m, gt, f = g1.take()
            tg = Q.dma("scalar", f"fg{m}", gt[:, :, :], scratch["g1"].rearrange("(k p) t -> p k t", p=128)[:, :, sl], f, done)
            m2, pt, f = pr.take()
            tp = Q.op("vector", lambda e, pt=pt, st=st, gt=gt: e.tensor_tensor(pt[:, :, :], st[:, :, :], gt[:, :, :],
                                                                               ALU.mult), ts, tg, f)
            s1.hold(m, tp)
            g1.hold(m, tp)
            b, bt, f = bk.take()

            def go(e, bt=bt, pt=pt):
                for k in range(4):
                    r = e.transpose(bt[:, k * 128:(k + 1) * 128], pt[:, k, :], cst[:, 0:128])
                return r
            t = Q.op("tensor", go, tp, f, done)
            pr.hold(m2, t)
            m3, ot, f = oo.take()
            t = Q.op("vector", lambda e, ot=ot, bt=bt, xt=xt: e.tensor_tensor(ot[:, :], bt[:, :], xt[:, :], ALU.add), t, tx, f)
            bk.hold(b, t)
            x1.hold(n, t)
            oo.hold(m3, Q.dma("scalar", f"fo{m3}", out["y"][sl, :], ot[:, :], t))


def ffn0(nc, Q, sb, io, scratch, bank, split, XH, XL, done):
    V = lambda fn, *a: Q.op("vector", fn, *a)
    A = lambda fn, *a: Q.op("scalar", fn, *a)
    P = lambda fn, *a: Q.op("tensor", fn, *a)
    with ExitStack() as c:
        raw = Ring([sb(c, f"fr{i}", [128, 4, 128]) for i in range(3)])
        wh = Ring([sb(c, f"fwh{i}", [128, 4, 128], F32R) for i in range(4)])
        wl = [sb(c, f"fwl{i}", [128, 4, 128], F32R) for i in range(4)]
        HH = sb(c, "HH", [128, 4, T], F32R)
        HL = sb(c, "HL", [128, 4, T], F32R)
        ACC = sb(c, "ACC", [128, 4, T])
        sil = Ring([sb(c, f"sil{i}", [128, 512]) for i in range(2)])
        hd = Ring([sb(c, f"hd{i}", [128, 512]) for i in range(2)])
        sc = sb(c, "fsc", [128, 26])
        t_sc = Q.dma("sync", "fsc", sc[:, :], io["ffn0_s"], done)
        bk = Ring(bank)
        for i in range(8):
            bk.hold(i, done)
        for r in (raw, wh, sil, hd):
            for i in range(len(r.slots)):
                r.hold(i, done)

        def weight(src):
            n, r, f = raw.take()
            t = Q.dma("sync", f"fr{n}", r[:, :, :], src, f)
            m, w, f = wh.take()
            ts = split(r[:, :, :], w[:, :, :], wl[m][:, :, :], t, f, low_eng="gpsimd")
            raw.hold(n, ts)
            return m, w, wl[m], ts

        gw = io["gate_wT"].rearrange("(k p) n -> p k n", p=128)
        uw = io["up_wT"].rearrange("(k p) n -> p k n", p=128)
        dw = io["down_wT"]
        tH = [[done for _ in range(4)] for _ in range(4)]
        tA = {}
        for g0, g1 in ((0, 4), (4, 8), (8, 11)):
            hs = {}
            for it in range(g0, g1):
                ng, wg, wgl, tg = weight(gw[:, :, it * 128:(it + 1) * 128])
                nu, wu, wul, tu = weight(uw[:, :, it * 128:(it + 1) * 128])
                for n in range(4):
                    sl = slice(n * 512, n * 512 + 512)
                    b1, k1, f1 = bk.take()
                    t1 = P(lambda e, k1=k1, wg=wg, wgl=wgl, sl=sl: mm3(e, k1[:, :], [
                        (wg[:, k, :], wgl[:, k, :], XH[:, k, sl], XL[:, k, sl]) for k in range(4)]), tg, f1)
                    b2, k2, f2 = bk.take()
                    t2 = P(lambda e, k2=k2, wu=wu, wul=wul, sl=sl: mm3(e, k2[:, :], [
                        (wu[:, k, :], wul[:, k, :], XH[:, k, sl], XL[:, k, sl]) for k in range(4)]), tu, f2)
                    m, s, f = sil.take()
                    ts = A(lambda e, s=s, k1=k1, it=it: e.activation(s[:, :], k1[:, :], ACT.Silu,
                                                                     scale=sc[:, it:it + 1]), t1, f, t_sc)
                    bk.hold(b1, ts)
                    m2, h, f = hd.take()
                    th = V(lambda e, h=h, k2=k2, s=s, it=it: e.scalar_tensor_tensor(
                        out=h[:, :], in0=k2[:, :], scalar=sc[:, 11 + it:12 + it], in1=s[:, :],
                        op0=ALU.mult, op1=ALU.mult), t2, ts, f)
                    bk.hold(b2, th)
                    sil.hold(m, th)
                    q = it - g0
                    tt = split(h[:, :], HH[:, q, sl], HL[:, q, sl], th, tH[q][n], low_eng="gpsimd")
                    hd.hold(m2, tt)
                    hs[(q, n)] = tt
                wh.hold(ng, t1)
                wh.hold(nu, t2)
            ws = []
            for it in range(g0, g1):
                ws.append(weight(dw[it * 128:(it + 1) * 128, :].rearrange("p (k n) -> p k n", k=4)))
            for o in range(4):
                for n in range(4):
                    sl = slice(n * 512, n * 512 + 512)
                    b, kb, f = bk.take()
                    t = P(lambda e, kb=kb, o=o, sl=sl, ws=ws: mm3(e, kb[:, :], [
                        (w[:, o, :], wlo[:, o, :], HH[:, q, sl], HL[:, q, sl])
                        for q, (_, w, wlo, _) in enumerate(ws)]),
                        [w[3] for w in ws], [hs[(q, n)] for q in range(g1 - g0)], f)
                    if g0 == 0:
                        ta = A(lambda e, kb=kb, o=o, sl=sl: e.copy(ACC[:, o, sl], kb[:, :]), t)
                    else:
                        ta = V(lambda e, kb=kb, o=o, sl=sl: e.tensor_tensor(ACC[:, o, sl], ACC[:, o, sl], kb[:, :],
                                                                            ALU.add), t, tA[(o, n)])
                    tA[(o, n)] = ta
                    bk.hold(b, ta)
                    tH[0][n] = t
            for n in range(4):
                for q in range(4):
                    tH[q][n] = tH[0][n]
            for w in ws:
                wh.hold(w[0], t)
        for o in range(4):
            for n in range(4):
                sl = slice(n * 512, n * 512 + 512)
                t = A(lambda e, o=o, sl=sl: e.activation(ACC[:, o, sl], ACC[:, o, sl], ACT.Silu,
                                                         scale=sc[:, 22 + o:23 + o]), tA[(o, n)])
            Q.dma("sync", "g0d", scratch["g0"][o * 128:(o + 1) * 128, :], ACC[:, o, :], t)
        return Q.everything()


def merged(*streams):
    lists = [list(x) for x in streams]
    order = sorted((((i + 0.5) / len(x), k, i) for k, x in enumerate(lists) for i in range(len(x))))
    for _, k, i in order:
        lists[k][i]()


def attn0(nc, Q, sb, io, scratch, bank, split, XH, XL, coef, GC, cst, eps, done):
    V = lambda fn, *a: Q.op("vector", fn, *a)
    A = lambda fn, *a: Q.op("scalar", fn, *a)
    P = lambda fn, *a: Q.op("tensor", fn, *a)
    G = lambda fn, *a: Q.op("gpsimd", fn, *a)
    KS = 128.0 ** -0.5
    with ExitStack() as c:
        def ring(name, n, shape, dt=F32):
            r = Ring([sb(c, f"{name}{i}", shape, dt) for i in range(n)])
            for i in range(n):
                r.hold(i, done)
            return r

        ident, cmat, jmat = cst[:, 0:128], cst[:, C_CM:C_CM + 128], cst[:, C_J:C_J + 128]
        raw = ring("wr", 2, [128, 4, 128])
        wh = ring("wh", 5, [128, 4, 128], F32R)
        wl = [sb(c, f"wl{i}", [128, 4, 128], F32R) for i in range(5)]
        cw = sb(c, "cw", [128, 16, 3, 5])
        lnw = sb(c, "lnw", [128, 2])
        t_cw = Q.dma("sync", "cw", cw[:, :, :, :], io["cw"], done)
        t_ln = Q.dma("sync", "lnw", lnw[:, :], io["ln"], done)
        rawx = ring("rx", 2, [128, 515])
        zt = ring("zt", 2, [128, 512])
        vt = ring("vt", 2, [128, 512])
        tails = sb(c, "tails", [128, 3, 2, 3])
        abc = ring("abc", 2, [128, 512])
        gbc = ring("gbc", 1, [128, 512])
        KQA = sb(c, "KQA", [128, 3, 2, 4, 128])
        KQ = Ring([0, 1])
        QG = ring("QG", 2, [128, 2, 4, 128])
        KD = ring("KD", 2, [128, 2, 4, 128])
        VC = ring("VC", 2, [128, 2, 4, 128])
        XPA = sb(c, "XPA", [128, 3, 8, 128])
        XP = Ring([1, 2])
        for r in (KQ, XP):
            for i in range(2):
                r.hold(i, done)
        q_all, X = KQA[:, 2], XPA[:, 0]

        def pair(ap, step, n=128):
            return bass.AP(tensor=ap.tensor, offset=ap.offset, ap=[list(ap.ap[0]), [step, 2], [1, n]])

        MF = ring("MF", 2, [128, 8, 128])
        D = ring("D", 3, [128, 130])
        XD = sb(c, "XD", [128, 16, 32])
        UN = sb(c, "UN", [128, 1024])
        XM = UN[:, 0:512].rearrange("p (m t) -> p m t", m=16)
        YY = UN[:, 512:1024].rearrange("p (m t) -> p m t", m=16)
        E1 = UN[:, :].rearrange("p (w a s b) -> p w a s b", w=2, a=16, s=2)
        XO = sb(c, "XO", [128, 8, 32])
        A16 = sb(c, "A16", [128, 16, 16])
        T16 = sb(c, "T16", [128, 16, 16])
        PR = sb(c, "PR", [128, 64])
        MN = sb(c, "MN", [128, 2, 16, 32])
        ZS = sb(c, "ZS", [128, 8, 32])
        ZT = sb(c, "ZT", [128, 8, 32])
        NF = sb(c, "NF", [64, 8, 64])
        Z2 = sb(c, "Z2", [128, 8, 64])
        ST = sb(c, "ST", [128, 2, 128])
        R = ring("R", 2, [128, 2, 128])
        WS = ring("WS", 2, [128, 2, 128])
        OS = ring("OS", 1, [128, 2, 4, 128])
        sq = sb(c, "sq", [128, 128])
        ss = sb(c, "ss", [128, 3, 8])
        DG = ring("DG", 2, [128, 128])
        rs = ring("rstd", 2, [128, 512])
        gg = ring("gg", 1, [128, 512])
        bk = Ring(bank[0:4])
        for i in range(4):
            bk.hold(i, done)
        pbk = Ring([bank[5], bank[6]])
        for i in range(2):
            pbk.hold(i, done)
        fb = {n: [done] for n in (4, 7)}
        t_i = []
        t_i.append(V(lambda e: e.memset(XD[:, :, :], 0.0), done))
        t_i.append(V(lambda e: e.memset(NF[:, :, :], 0.0), done))
        for m in MF.slots:
            t_i.append(V(lambda e, m=m: e.memset(m[:, :, :], 0.0), done))
        for d in D.slots:
            t_i.append(V(lambda e, d=d: e.memset(d[:, 0:1], 0.0), done))

        wsrc = {p: io[p].rearrange("(k p) n -> p k n", p=128) for p in ("Wq", "Wk", "Wv", "Wg")}

        loading = {}

        def load(p, h):
            if h < H:
                n, r, f = raw.take()
                loading[p] = (n, r, Q.dma("sync", f"wr{n}", r[:, :, :], wsrc[p][:, :, h * 128:(h + 1) * 128], f))

        def cut(p, h):
            if h < H:
                n, r, t = loading[p]
                m, w, f = wh.take()
                ts = split(r[:, :, :], w[:, :, :], wl[m][:, :, :], t, f, low_eng="gpsimd")
                raw.hold(n, ts)
                W[p, h % 2] = (m, w, wl[m], ts)

        def project(w, n):
            m, wt, wlo, tw = w
            got = {}
            sl = slice(n * 512, n * 512 + 512)

            def part(k0, k1):
                def go():
                    if k0 == 0:
                        got["b"], got["kb"], got["f"] = pbk.take()
                    kb = got["kb"]
                    got["t"] = P(lambda e: mm3(e, kb[:, :], [
                        (wt[:, k, :], wlo[:, k, :], XH[:, k, sl], XL[:, k, sl]) for k in range(k0, k1)],
                        first=k0 == 0, last=k1 == 4), tw, got["f"])
                return go
            return got, [part(0, 2), part(2, 4)]

        W = {}
        t_tail = {}
        unit = {}
        s_prev = {}
        st = {"S": [done]}

        def begin(u):
            s = unit.setdefault(u, {})
            for name, r in (("kq", KQ), ("qg", QG), ("kd", KD), ("vc", VC), ("xp", XP), ("mf", MF)):
                s[name + "n"], s[name], s[name + "f"] = r.take()
            s["k_slot"], s["p_slot"] = s["kq"], s["xp"]
            s["kq"], s["xp"] = KQA[:, s["kq"]], XPA[:, s["xp"]]
            s["t_kd"], s["t_vc"], s["t_xp"] = {}, {}, {}
            return s

        def conv(u, pi, p, b):
            h, half = divmod(u, 2)
            s = unit.setdefault(u, {})
            n = 2 * b + half
            g = {}
            v4 = lambda ap: ap.rearrange("p (c t) -> p c t", c=4)
            pre, mats = {}, [None, None]

            def first():
                pre["got"], pre["steps"] = project(W[p, h % 2], n)
                pre["steps"][0]()
                if p == "Wq":
                    g["gn"], g["g"], gf = gbc.take()
                    g["tl"] = Q.dma("sync", f"gb{g['gn']}", g["g"][:, :], scratch["g"][h:h + 1, n * 512:n * 512 + 512]
                                    .rearrange("a t -> (a t)").partition_broadcast(128), gf)

            def second():
                pre["steps"][1]()
                got = pre["got"]
                kb, t = got["kb"], got["t"]
                s["t_proj", p, b] = t
                rn, rx, rf = rawx.take()
                zn, z, zf = zt.take()
                tr = A(lambda e: e.copy(rx[:, 3:515], kb[:, :]), t, rf)
                tz = A(lambda e: e.activation(z[:, :], kb[:, :], ACT.Copy, scale=cw[:, h, pi, 3:4]), t, zf, t_cw)
                pbk.hold(got["b"], tr, tz)
                if half == 0:
                    th = G(lambda e: e.memset(rx[:, 0:3], 0.0), rf)
                    tt = G(lambda e: e.tensor_copy(tails[:, pi, b, :], rx[:, 512:515]), tr, t_tail.get((pi, b)))
                    t_tail[pi, b] = tt
                else:
                    th = tt = G(lambda e: e.tensor_copy(rx[:, 0:3], tails[:, pi, b, :]), rf, t_tail[pi, b])
                    t_tail[pi, b] = th
                for j in (2, 1, 0):
                    tz = V(lambda e, j=j: e.scalar_tensor_tensor(out=z[:, :], in0=rx[:, j:j + 512],
                                                                 scalar=cw[:, h, pi, j:j + 1], in1=z[:, :],
                                                                 op0=ALU.mult, op1=ALU.add), tz, tr, th)
                rawx.hold(rn, tz, tt)
                g["z"], g["zn"], g["tz"] = z, zn, tz

            def finish():
                z, zn, tz = g["z"], g["zn"], g["tz"]
                bias = cw[:, h, pi, 4:5]
                if p == "Wk":
                    ta = A(lambda e: e.activation(z[:, :], z[:, :], ACT.Silu, bias=bias), tz)
                    ta = G(lambda e: e.tensor_scalar(s["kq"][:, b, :, :], v4(z[:, :]), KS, None, ALU.mult), ta, s["kqf"])
                    s["t_k", b] = ta
                elif p == "Wq":
                    ta = A(lambda e: e.activation(q_all[:, b, :, :], v4(z[:, :]), ACT.Silu, bias=bias), tz,
                           s_prev.get("q"))
                    s["t_q", b] = ta
                    gg_, gn = g["g"], g["gn"]
                    tg = G(lambda e: e.tensor_tensor(s["qg"][:, b, :, :], q_all[:, b, :, :], v4(gg_[:, :]), ALU.mult),
                           ta, g["tl"], s["qgf"])
                    gbc.hold(gn, tg)
                    s["t_qg", b] = tg
                else:
                    vn, v, vf = vt.take()
                    ta = A(lambda e: e.activation(v[:, :], z[:, :], ACT.Silu, bias=bias), tz, vf)
                    s["v", b], s["t_v", b] = (vn, v), ta
                zt.hold(zn, ta)
            return [first, second], finish

        def decays(u, b):
            def go():
                h, half = divmod(u, 2)
                n = 2 * b + half
                an, a, af = abc.take()
                unit[u]["a", b] = (an, Q.dma("sync", f"ab{an}", a[:, :], scratch["a"][h:h + 1, n * 512:n * 512 + 512]
                                             .rearrange("a t -> (a t)").partition_broadcast(128), af))
            return go

        def turn_kv(u, b, c0):
            def steps():
                h, half = divmod(u, 2)
                s = unit[u]
                kq, kd, vc = s["kq"], s["kd"], s["vc"]
                vn, v = s["v", b]
                bn, kb, f = bk.take()

                def go(e):
                    for x in range(2):
                        e.transpose(kb[:, x * 256:x * 256 + 128], kq[:, b, c0 + x, :], ident)
                        m = e.matmul(kb[:, x * 256 + 128:x * 256 + 256], v[:, (c0 + x) * 128:(c0 + x + 1) * 128],
                                     cmat, start=True, stop=True)
                    return m
                t = P(go, s["t_k", b], s["t_v", b], f)
                for x in range(2):
                    i = b * 8 + half * 4 + c0 + x
                    s["t_kd"][b, c0 + x] = A(lambda e, x=x, i=i: e.activation(
                        kd[:, b, c0 + x, :], kb[:, x * 256:x * 256 + 128], ACT.Copy, scale=coef[:, i, 2, h:h + 1]),
                        t, s["kdf"])
                tv = A(lambda e: e.copy(vc[:, b, c0:c0 + 2, :],
                                        kb[:, :].rearrange("p (x a t) -> p x a t", x=2, a=2)[:, :, 1, :]), t, s["vcf"])
                bk.hold(bn, s["t_kd"][b, c0], s["t_kd"][b, c0 + 1], tv)
                s["t_vc"][b, c0] = s["t_vc"][b, c0 + 1] = tv
                if c0 == 2:
                    vt.hold(vn, t)
            return steps

        def scores(u, b, c0):
            def steps():
                h, half = divmod(u, 2)
                s = unit[u]
                kq = s["kq"]
                an, ta = s["a", b]
                bn, kb, f = bk.take()

                def go(e):
                    for x in range(2):
                        m = e.matmul(kb[:, x * 256:x * 256 + 256], kq[:, b, c0 + x, :],
                                     pair(kq[:, b, c0 + x, :], (2 - s["k_slot"]) * 1024), start=True, stop=True)
                    return m
                t = P(go, s["t_k", b], s["t_q", b], f)
                s_prev["q"] = [t, s["t_qg", 0], s.get(("t_qg", 1))]
                ts = []
                for x in range(2):
                    i = b * 8 + half * 4 + c0 + x
                    dn, d, df = D.take()
                    td = V(lambda e, x=x, d=d: e.tensor_tensor_scan(
                        d[:, 1:129], abc.slots[an][:, (c0 + x) * 128:(c0 + x + 1) * 128], ident, 0.0,
                        ALU.mult, ALU.add), ta, df, t_i)
                    tx = V(lambda e, x=x, d=d, i=i: e.scalar_tensor_tensor(
                        out=pair(X[:, b * 4 + c0 + x, :], s["p_slot"] * 1024),
                        in0=kb[:, x * 256:x * 256 + 256].rearrange("p (a t) -> p a t", a=2),
                        scalar=coef[:, i, 1, h:h + 1], in1=pair(d[:, 0:128], 1), op0=ALU.mult, op1=ALU.mult),
                        t, td, s["xpf"], s_prev.get("inv"))
                    D.hold(dn, tx)
                    s["t_xp"][b, c0 + x] = tx
                    ts.append(tx)
                bk.hold(bn, ts)
                if c0 == 2:
                    abc.hold(an, td)
            return steps

        def head_part(u):
            if u >= 2 * H:
                return []
            h, half = divmod(u, 2)
            (k0, fk), (v0, fv), (q0, fq) = (conv(u, i, p, 0) for i, p in ((1, "Wk"), (2, "Wv"), (0, "Wq")))

            def with_(a, b):
                return lambda: (a(), b())
            extra = (lambda: load("Wg", h), lambda: cut("Wg", h)) if half == 0 else (lambda: None, lambda: None)
            return [with_(lambda: begin(u), with_(decays(u, 0), k0[0])), k0[1],
                    v0[0], with_(fk, v0[1]), with_(extra[0], q0[0]), with_(fv, with_(extra[1], q0[1]))], fq

        def rest_part(u, fq):
            h, half = divmod(u, 2)
            (k1, fk1), (v1, fv1), (q1, fq1) = (conv(u, i, p, 1) for i, p in ((1, "Wk"), (2, "Wv"), (0, "Wq")))
            nop = lambda: None
            o = half == 1
            ld = lambda p: (lambda: load(p, h + 1)) if o else nop
            ct = lambda p: (lambda: cut(p, h + 1)) if o else nop

            def seq(*fs):
                def go():
                    for f in fs:
                        f()
                return go

            def free(p):
                return (lambda: wh.hold(W[p, h % 2][0], unit[u]["t_proj", p, 1])) if o else nop
            return [seq(fq, decays(u, 1), ld("Wk"), k1[0]), k1[1],
                    seq(ct("Wk"), turn_kv(u, 0, 0)), seq(free("Wk"), ld("Wv"), v1[0]), seq(fk1, v1[1]),
                    turn_kv(u, 0, 2), seq(scores(u, 0, 0), ct("Wv")), seq(free("Wv"), ld("Wq"), q1[0]),
                    seq(fv1, q1[1]), seq(scores(u, 0, 2), ct("Wq"), free("Wq")), turn_kv(u, 1, 0), seq(fq1, turn_kv(u, 1, 2)),
                    scores(u, 1, 0), scores(u, 1, 2)]

        def inverse(u):
            L = {}

            def s0():
                s = unit[u]
                tx = L["tx"] = list(s["t_xp"].values())
                prev = L["prev"] = s_prev.get("inv")
                t = []
                for q in range(4):
                    qs = slice(32 * q, 32 * q + 32)
                    t.append(A(lambda e, qs=qs: e.copy(XD[qs, 0:8, :], X[qs, :, qs]), tx, prev, t_i))
                tm = V(lambda e: e.tensor_tensor(XM, XD[:, :, :], cst[:, C_M16:C_M16 + 32].unsqueeze(1)
                                                 .to_broadcast([128, 16, 32]), ALU.mult), t, prev)
                L["to"] = G(lambda e: e.tensor_tensor(XO[:, :, :], XD[:, 0:8, :], cst[:, C_OFF:C_OFF + 32].unsqueeze(1)
                                                      .to_broadcast([128, 8, 32]), ALU.mult), t, prev)
                t = V(lambda e: e.transpose(YY, XM.rearrange("p m (s t) -> p t s m", s=2)), tm, prev)
                L["ta"] = V(lambda e: e.tensor_tensor(A16[:, :, :], YY[:, :, 0:16], YY[:, :, 16:32], ALU.add), t)
                tt = G(lambda e: e.memset(T16[:, :, :], 0.0), prev)
                L["tt"] = G(lambda e: e.memset(T16[:, :, :].rearrange("p a b -> p (a b)")[:, 0:256:17], 1.0), tt)

            def rows(l0, l1):
                def go():
                    tt = L["tt"]
                    for l in range(l0, l1):
                        n = 15 - l
                        pr = PR[:, 0:n * (l + 1)].rearrange("p (a b) -> p a b", a=n)
                        tp = V(lambda e, l=l, n=n, pr=pr: e.tensor_tensor(
                            pr, A16[:, l + 1:16, l:l + 1].to_broadcast([128, n, l + 1]),
                            T16[:, l:l + 1, 0:l + 1].to_broadcast([128, n, l + 1]), ALU.mult), L["ta"], tt)
                        tt = V(lambda e, l=l, pr=pr: e.tensor_tensor(T16[:, l + 1:16, 0:l + 1],
                                                                     T16[:, l + 1:16, 0:l + 1], pr, ALU.add), tp)
                    L["tt"] = tt
                return go

            def s2():
                te = []
                for f in range(2):
                    fl = cst[:, C_FLAG + f:C_FLAG + f + 1]
                    te.append(A(lambda e, f=f, fl=fl: e.activation(E1[:, 0, :, f, :], T16[:, :, :], ACT.Copy, scale=fl),
                                L["tt"], L["prev"]))
                    te.append(A(lambda e, f=f, fl=fl: e.activation(
                        E1[:, 1, :, f, :], T16[:, :, :].rearrange("p t j -> p j t"), ACT.Copy, scale=fl), L["tt"], L["prev"]))
                L["tn"] = [V(lambda e, w=w: e.transpose(MN[:, w, :, :].rearrange("p m (s t) -> p t s m", s=2),
                                                        E1[:, w, :, :, :].rearrange("p a s b -> p a (s b)")),
                             te, L["prev"]) for w in range(2)]

            def s3():
                zb = [bk.take() for _ in range(4)]
                L["tz"] = []
                for q in range(4):
                    qs = slice(32 * q, 32 * q + 32)
                    bn, kb, f = zb[q]

                    def go(e, qs=qs, kb=kb):
                        for m in range(8):
                            r = e.matmul(kb[qs, m * 32:m * 32 + 32], XO[qs, m, :], MN[qs, 1, m, :], start=True, stop=True)
                        return r
                    t = P(go, L["to"], L["tn"], f)
                    L["tz"].append(A(lambda e, qs=qs, kb=kb: e.copy(
                        ZS[qs, :, :], kb[qs, 0:256].rearrange("p (m t) -> p m t", m=8)), t, L["prev"]))
                    bk.hold(bn, L["tz"][-1])

            def s4():
                s = unit[u]
                mf = s["mf"]
                zb = [bk.take() for _ in range(4)]
                tmn = []
                for q in range(4):
                    qs = slice(32 * q, 32 * q + 32)
                    bn, kb, f = zb[q]

                    def go(e, qs=qs, kb=kb):
                        for m in range(8):
                            e.matmul(kb[qs, m * 32:m * 32 + 32], ZS[qs, m, :], MN[qs, 0, m, :], start=True, stop=True)
                            r = e.matmul(kb[qs, 256 + m * 32:288 + m * 32], MN[qs, 0, m, :], ZS[qs, m, :],
                                         start=True, stop=True)
                        return r
                    t = P(go, L["tz"][q], f)
                    tmn.append(V(lambda e, qs=qs, kb=kb: e.tensor_tensor(
                        MN[qs, :, 0:8, :], MN[qs, :, 0:8, :], kb[qs, :].rearrange("p (a m t) -> p a m t", a=2, m=8),
                        ALU.add), t))
                    bk.hold(bn, tmn[-1])
                L["tmn"] = tmn
                L["tmf"] = []
                for q in range(4):
                    qs = slice(32 * q, 32 * q + 32)
                    L["tmf"].append(A(lambda e, qs=qs: e.copy(mf[qs, :, qs], MN[qs, 0, 0:8, :]), tmn[q], s["mff"], t_i))
                for q in range(2):
                    qs = slice(32 * q, 32 * q + 32)
                    L["tmf"].append(A(lambda e, qs=qs: e.copy(NF[qs, :, qs], MN[qs, 1, 0:8, :]), tmn[q], L["prev"], t_i))

            def s5():
                zb = [bk.take() for _ in range(2)]
                L["tz"] = []
                for p in range(2):
                    ra, rb = slice(64 * p, 64 * p + 32), slice(64 * p + 32, 64 * p + 64)
                    bn, kb, f = zb[p]

                    def go(e, ra=ra, rb=rb, kb=kb):
                        for m in range(8):
                            r = e.matmul(kb[rb, m * 32:m * 32 + 32], X[ra, m, rb], MN[ra, 1, m, :], start=True, stop=True)
                        return r
                    t = P(go, L["tmn"], f, L["tx"])
                    L["tz"].append(A(lambda e, rb=rb, kb=kb: e.activation(
                        ZT[rb, :, :], kb[rb, 0:256].rearrange("p (m t) -> p m t", m=8), ACT.Copy, scale=-1.0), t, L["prev"]))
                    bk.hold(bn, L["tz"][-1])

            def s6():
                s = unit[u]
                mf = s["mf"]
                zb = [bk.take() for _ in range(2)]
                for p in range(2):
                    ra, rb = slice(64 * p, 64 * p + 32), slice(64 * p + 32, 64 * p + 64)
                    bn, kb, f = zb[p]

                    def go(e, ra=ra, rb=rb, kb=kb, p=p):
                        for m in range(8):
                            r = e.matmul(kb[ra, m * 32:m * 32 + 32], ZT[rb, m, :], MN[rb, 0, m, :], start=True, stop=True)
                            if p == 0:
                                r = e.matmul(kb[rb, 256 + m * 32:288 + m * 32], MN[rb, 0, m, :], ZT[rb, m, :],
                                             start=True, stop=True)
                        return r
                    t = P(go, L["tz"][p], f)
                    ts = [V(lambda e, ra=ra, rb=rb, kb=kb: e.tensor_copy(
                        mf[ra, :, rb], kb[ra, 0:256].rearrange("p (m t) -> p m t", m=8)), t, s["mff"])]
                    if p == 0:
                        ts.append(V(lambda e, kb=kb: e.tensor_copy(
                            NF[32:64, :, 0:32], kb[32:64, 256:512].rearrange("p (m t) -> p m t", m=8)), t, L["tmf"]))
                    L["tmf"] += ts
                    bk.hold(bn, ts)

            def s7():
                bn, kb, f = bk.take()

                def go(e, kb=kb):
                    for m in range(8):
                        r = e.matmul(kb[64:128, m * 64:m * 64 + 64], X[0:64, m, 64:128], NF[0:64, m, :],
                                     start=True, stop=True)
                    return r
                t = P(go, L["tmf"], f)
                L["tz"] = A(lambda e, kb=kb: e.activation(
                    Z2[64:128, :, :], kb[64:128, :].rearrange("p (m t) -> p m t", m=8), ACT.Copy, scale=-1.0), t, L["prev"])
                bk.hold(bn, L["tz"])

            def s8():
                s = unit[u]
                mf = s["mf"]
                bn, kb, f = bk.take()

                def go(e, kb=kb):
                    for m in range(8):
                        r = e.matmul(kb[0:64, m * 64:m * 64 + 64], Z2[64:128, m, :], mf[64:128, m, 64:128],
                                     start=True, stop=True)
                    return r
                t = P(go, L["tz"], L["tmf"], f)
                tl = V(lambda e, kb=kb: e.tensor_copy(mf[0:64, :, 64:128],
                                                      kb[0:64, :].rearrange("p (m t) -> p m t", m=8)), t)
                bk.hold(bn, tl)
                s["t_mf"] = [tl, L["tmf"]]
                s_prev["inv"] = [t, tl, L["tmf"], L["tn"], L["tmn"]]
            return [s0, rows(0, 5), rows(5, 10), rows(10, 15), s2, s3, s4, s5, s6, s7, s8]

        def chain(u):
            h, half = divmod(u, 2)
            steps = []
            L = {}

            def start():
                osn, L["os"], osf = OS.take()
                L["osn"], L["osf"], L["to"] = osn, osf, []
                unit[u]["os"] = L
            for ch in range(4):
                first = half == 0 and ch == 0

                def p1(ch=ch, first=first):
                    s = unit[u]
                    kq, vc = s["kq"], s["vc"]
                    if ch == 0:
                        start()
                    if first:
                        L["tr"] = [s["t_vc"][0, ch], s["t_vc"][1, ch]]
                        L["rhs"] = lambda b: vc[:, b, 0, :]
                        return

                    def go(e):
                        for b in range(2):
                            r = e.matmul(bank[4][:, b * 128:b * 128 + 128], kq[:, b, ch, :], ST[:, b, :],
                                         start=True, stop=True)
                        return r
                    t = P(go, st["S"], fb[4])
                    L["rn"], r_, rf = R.take()
                    tr = []
                    for b in range(2):
                        i = b * 8 + half * 4 + ch
                        tr.append(V(lambda e, b=b, i=i: e.scalar_tensor_tensor(
                            out=r_[:, b, :], in0=bank[4][:, b * 128:b * 128 + 128], scalar=coef[:, i, 0, h:h + 1],
                            in1=vc[:, b, ch, :], op0=ALU.mult, op1=ALU.add), t, rf, s["t_vc"][b, ch]))
                    fb[4] = tr
                    L["tr"] = tr
                    L["rhs"] = lambda b: r_[:, b, :]

                def p2(ch=ch, first=first):
                    s = unit[u]
                    mf, qg = s["mf"], s["qg"]
                    rhs = L["rhs"]

                    def go(e):
                        for b in range(2):
                            r = e.matmul(bank[4][:, b * 128:b * 128 + 128], mf[:, b * 4 + ch, :], rhs(b), start=True, stop=True)
                        return r
                    tw = P(go, L["tr"], s["t_mf"], fb[4])
                    if not first:
                        R.hold(L["rn"], tw)
                    L["wn"], ws, wf = WS.take()
                    L["ws"] = ws
                    L["tws"] = A(lambda e: e.copy(ws[:, :, :], bank[4][:, 0:256].rearrange("p (b t) -> p b t", b=2)), tw, wf)
                    fb[4] = [L["tws"]]

                def p3(ch=ch, first=first):
                    s = unit[u]
                    kd, xp, qg = s["kd"], s["xp"], s["qg"]
                    ws = L["ws"]

                    def go(e):
                        for b in range(2):
                            r = e.matmul(bank[4][:, b * 128:b * 128 + 128], kd[:, b, ch, :], ws[:, b, :], start=True, stop=True)
                        return r
                    tds = P(go, L["tws"], fb[4])

                    def go(e):
                        for b in range(2):
                            o = bank[7][:, b * 128:b * 128 + 128]
                            if not first:
                                e.matmul(o, qg[:, b, ch, :], ST[:, b, :], start=True, stop=False)
                            r = e.matmul(o, xp[:, b * 4 + ch, :], ws[:, b, :], start=first, stop=True)
                        return r
                    tp = P(go, fb[7], s["t_qg", 0], s["t_qg", 1])
                    WS.hold(L["wn"], tp)
                    ts = []
                    for b in range(2):
                        i = b * 8 + half * 4 + ch
                        if first:
                            ts.append(V(lambda e, b=b: e.tensor_copy(ST[:, b, :], bank[4][:, b * 128:b * 128 + 128]),
                                        tds, st["S"], tp))
                        else:
                            ts.append(V(lambda e, b=b, i=i: e.scalar_tensor_tensor(
                                out=ST[:, b, :], in0=ST[:, b, :], scalar=GC[:, h, i:i + 1],
                                in1=bank[4][:, b * 128:b * 128 + 128], op0=ALU.mult, op1=ALU.add), tds, tp))
                    fb[4] = ts
                    st["S"] = ts + [tp]
                    os_ = L["os"]
                    toc = A(lambda e: e.copy(os_[:, :, ch, :], bank[7][:, 0:256].rearrange("p (b t) -> p b t", b=2)),
                            tp, L["osf"])
                    fb[7] = [toc]
                    L["to"].append(toc)
                    if ch == 3:
                        for r, k in ((KQ, "kqn"), (QG, "qgn"), (KD, "kdn"), (VC, "vcn"), (XP, "xpn"), (MF, "mfn")):
                            r.hold(s[k], tp, ts)
                steps += [p1, p2, p3]
            return steps

        def tail(u):
            h, half = divmod(u, 2)
            L = {}

            def sums():
                o = unit[u]["os"]
                os_ = o["os"]
                tq = s_prev.get("sq")
                ts = []
                for b in range(2):
                    for ch in range(4):
                        tq = A(lambda e, b=b, ch=ch: e.activation(sq[:, :], os_[:, b, ch, :], ACT.Square,
                                                                  accum_out=ss[:, 0, b * 4 + ch:b * 4 + ch + 1]),
                               o["to"], tq, s_prev.get("ss"))
                        ts.append(tq)
                s_prev["sq"] = tq
                t = A(lambda e: e.activation(ss[:, 1, :], ss[:, 0, :], ACT.Sqrt, bias=eps[:, 0:1], scale=1.0 / 128), ts)
                L["tr"] = V(lambda e: e.reciprocal(ss[:, 2, :], ss[:, 1, :]), t)

            def gate(b):
                def first():
                    L["got"], L["steps"] = project(W["Wg", h % 2], 2 * b + half)
                    L["steps"][0]()

                def second():
                    L["steps"][1]()
                    kb, t = L["got"]["kb"], L["got"]["t"]
                    gn, g, gf = gg.take()
                    L["g"] = (gn, g, A(lambda e: e.activation(g[:, :], kb[:, :], ACT.Sigmoid), t, gf))
                    pbk.hold(L["got"]["b"], L["g"][2])
                    if half == 1 and b == 1:
                        wh.hold(W["Wg", h % 2][0], t)
                return [first, second]

            def turn(b):
                def go_():
                    o = unit[u]["os"]
                    os_ = o["os"]
                    gn, g, tg = L["g"]
                    bn, kb, f = bk.take()
                    tl = []
                    for ch in range(4):
                        dn, d, df = DG.take()
                        k = b * 4 + ch
                        t = V(lambda e, k=k, d=d: e.tensor_scalar(d[:, :], ident, ss[:, 2, k:k + 1], None, ALU.mult),
                              L["tr"], df)
                        t = P(lambda e, ch=ch, d=d: e.matmul(kb[:, ch * 128:ch * 128 + 128], os_[:, b, ch, :], d[:, :],
                                                             start=True, stop=True), t, f if ch == 0 else None, o["to"])
                        DG.hold(dn, t)
                    rn, r_, rf = rs.take()
                    t2 = A(lambda e: e.activation(r_[:, :], kb[:, :], ACT.Identity, scale=lnw[:, 0:1], bias=lnw[:, 1:2]),
                           t, rf, t_ln)
                    bk.hold(bn, t2)
                    t3 = G(lambda e: e.tensor_tensor(r_[:, :], r_[:, :], g[:, :], ALU.mult), t2, tg)
                    gg.hold(gn, t3)
                    a = b * 1024 + half * 512
                    rs.hold(rn, Q.dma("gpsimd", f"og{rn}", scratch["og"][h * 128:(h + 1) * 128, a:a + 512], r_[:, :], t3))
                    if b == 1:
                        OS.hold(o["osn"], t)
                        s_prev["ss"] = t
                return go_
            return [sums] + gate(0) + [turn(0)] + gate(1) + [turn(1)]

        NU = 2 * H
        for p in ("Wk", "Wv", "Wq"):
            load(p, 0)
            cut(p, 0)
        steps, fq = head_part(0)
        merged(steps)
        for u in range(NU):
            merged(rest_part(u, fq), chain(u - 1) if u else [])
            if u + 1 < NU:
                steps, fq = head_part(u + 1)
            else:
                steps = []
            merged(inverse(u), tail(u - 1) if u else [], steps)
        merged(chain(NU - 1))
        merged(tail(NU - 1))
        return Q.everything()



def mix0(nc, Q, sb, io, scratch, bank, split, cst, done):
    V = lambda fn, *a: Q.op("vector", fn, *a)
    A = lambda fn, *a: Q.op("scalar", fn, *a)
    P = lambda fn, *a: Q.op("tensor", fn, *a)
    with ExitStack() as c:
        def ring(name, n, shape, dt=F32):
            r = Ring([sb(c, f"{name}{i}", shape, dt) for i in range(n)])
            for i in range(n):
                r.hold(i, done)
            return r
        WOH = sb(c, "WOH", [128, 16, 512], F32R)
        WOL = sb(c, "WOL", [128, 16, 512], F32R)
        raw = ring("mr", 3, [128, 512])
        og = ring("mo", 4, [128, 512])
        oh = ring("moh", 3, [128, 512], F32R)
        ol = ring("mol", 3, [128, 512], F32R)
        g0 = ring("mg", 2, [128, 4, 512])
        xT = ring("mx", 2, [128, 4, 512])
        xr = ring("mxr", 3, [128, 512])
        bk = Ring(bank)
        for i in range(8):
            bk.hold(i, done)
        tw = []
        pend = []

        def rows(n, x1, tx1, nx):
            for q in range(4):
                i = n * 4 + q
                b, kb, f = bk.take()

                def go(e, q=q, kb=kb):
                    for k in range(4):
                        m = e.transpose(kb[:, k * 128:(k + 1) * 128], x1[:, k, q * 128:(q + 1) * 128], cst[:, 0:128])
                    return m
                t = P(go, tx1, f)
                m, r, f = xr.take()
                t2 = A(lambda e, kb=kb, r=r: e.copy(r[:, :], kb[:, :]), t, f)
                bk.hold(b, t2)
                xr.hold(m, Q.dma("scalar", f"mxr{m}", scratch["x1"][i * 128:(i + 1) * 128, :], r[:, :], t2))
            xT.hold(nx, t)

        for n in range(4):
            sl = slice(n * 512, n * 512 + 512)
            ng, g, f = g0.take()
            tg = Q.dma("scalar", f"mg{ng}", g[:, :, :], scratch["g0"].rearrange("(k p) t -> p k t", p=128)[:, :, sl], f)
            nx, x, f = xT.take()
            tx = Q.dma("scalar", f"mx{nx}", x[:, :, :], io["xT"].rearrange("(k p) t -> p k t", p=128)[:, :, sl], f)
            bks = [bk.take() for _ in range(4)]
            for k in range(16):
                if n == 0:
                    m, r, f = raw.take()
                    t = Q.dma("sync", f"mr{m}", r[:, :], io["Wo"][k * 128:(k + 1) * 128, :], f)
                    ts = split(r[:, :], WOH[:, k, :], WOL[:, k, :], t, done, low_eng="gpsimd")
                    raw.hold(m, ts)
                    tw.append(ts)
                m, o, f = og.take()
                t = Q.dma("sync", f"mo{m}", o[:, :], scratch["og"][k * 128:(k + 1) * 128, sl], f)
                mh, h, fh = oh.take()
                ml, l, fl = ol.take()
                ts = split(o[:, :], h[:, :], l[:, :], t, [fh, fl], low_eng="vector")
                og.hold(m, ts)
                for j in range(4):
                    tp = P(lambda e, j=j, k=k, h=h, l=l, kb=bks[j][1]: mm3(e, kb[:, :], [
                        (WOH[:, k, j * 128:(j + 1) * 128], WOL[:, k, j * 128:(j + 1) * 128], h[:, :], l[:, :])],
                        first=k == 0, last=k == 15), ts, tw[k], bks[j][2])
                oh.hold(mh, tp)
                ol.hold(ml, tp)
                if k == 3 and pend:
                    rows(*pend.pop())
            tv = []
            for j in range(4):
                t = V(lambda e, j=j, kb=bks[j][1], g=g: e.tensor_tensor(g[:, j, :], g[:, j, :], kb[:, :], ALU.mult), tp, tg)
                bk.hold(bks[j][0], t)
                tv.append(V(lambda e, j=j, g=g, x=x: e.tensor_tensor(x[:, j, :], x[:, j, :], g[:, j, :], ALU.add), t, tx))
            g0.hold(ng, tv)
            pend.append((n, x, tv, nx))
        rows(*pend.pop())
        return Q.everything()


def attn1(nc, Q, sb, io, scratch, bank, XN, one, done):
    V = lambda fn, *a: Q.op("vector", fn, *a)
    A = lambda fn, *a: Q.op("scalar", fn, *a)
    P = lambda fn, *a: Q.op("tensor", fn, *a)
    G = lambda fn, *a: Q.op("gpsimd", fn, *a)
    with ExitStack() as c:
        v = sb(c, "l1v", [128, 4, 3])
        wi = sb(c, "wi", [128, 4, 128])
        wa = sb(c, "wa", [128, 4, 128])
        t_v = Q.dma("sync", "l1v", v[:, :, :], io["l1v"], done)
        t_wi = Q.dma("sync", "l1wi", wi[:, :, :], io["ig_w"].rearrange("k p n -> p k n"), done)
        t_wa = Q.dma("sync", "l1wa", wa[:, :, :], io["ag_w"].rearrange("k p n -> p k n"), done)
        sp = sb(c, "sp", [128, 8, 4])
        row = lambda i: sp[:, i, :]
        p = v[:, :, 2]
        t = A(lambda e: e.activation(row(0), p, ACT.Abs), t_v)
        t = A(lambda e: e.activation(row(1), row(0), ACT.Exp, scale=-1.0), t)
        t = V(lambda e: e.tensor_scalar(row(2), row(1), 2.0, None, ALU.add), t)
        t = V(lambda e: e.reciprocal(row(3), row(2)), t)
        t = V(lambda e: e.tensor_tensor(row(2), row(1), row(3), ALU.mult), t)
        t = V(lambda e: e.tensor_tensor(row(4), row(2), row(2), ALU.mult), t)
        t = V(lambda e: e.tensor_scalar(row(5), row(4), 2.0 / 17, 2.0 / 15, ALU.mult, ALU.add), t)
        for k in (13, 11, 9, 7, 5, 3, 1):
            t = V(lambda e: e.tensor_tensor(row(5), row(5), row(4), ALU.mult), t)
            t = V(lambda e, k=k: e.tensor_scalar(row(5), row(5), 2.0 / k, None, ALU.add), t)
        t = V(lambda e: e.tensor_tensor(row(5), row(5), row(2), ALU.mult), t)
        t = V(lambda e: e.tensor_scalar(row(6), p, 0.0, None, ALU.max), t)
        t = V(lambda e: e.tensor_tensor(row(6), row(6), row(5), ALU.add), t)
        t1 = V(lambda e: e.tensor_scalar(row(5), row(6), -8.0, None, ALU.mult), t)
        t_sp = V(lambda e: e.tensor_scalar(row(7), row(6), -16.0, None, ALU.mult), t1)
        gx = [sb(c, f"gx{i}", [128, T]) for i in range(2)]
        ga = [sb(c, f"ga{i}", [128, T]) for i in range(2)]
        am = [sb(c, f"am{i}", [128, T]) for i in range(1)]
        free = [[done], [done]]
        fam = [done]
        fb = [[done] for _ in range(8)]
        for k in range(4):
            s = k % 2
            X, Y, M = gx[s], ga[s], am[0]
            tg = []
            for n in range(4):
                sl = slice(n * 512, n * 512 + 512)
                t = P(lambda e, n=n, sl=sl, k=k: e.matmul(bank[n][:, :], wi[:, k, :], XN[:, k, sl], start=True, stop=True),
                      t_wi, fb[n], done)
                fb[n] = [A(lambda e, n=n, sl=sl, k=k, X=X: e.activation(X[:, sl], bank[n][:, :], ACT.Sigmoid,
                                                                        bias=v[:, k, 0:1]), t, free[s], t_v)]
                t = P(lambda e, n=n, sl=sl, k=k: e.matmul(bank[4 + n][:, :], wa[:, k, :], XN[:, k, sl], start=True, stop=True),
                      t_wa, fb[4 + n], done)
                fb[4 + n] = [A(lambda e, n=n, sl=sl, k=k, Y=Y: e.activation(Y[:, sl], bank[4 + n][:, :], ACT.Sigmoid,
                                                                            bias=v[:, k, 1:2]), t, free[s])]
                tg += [fb[n], fb[4 + n]]
            ta = A(lambda e, k=k, M=M, Y=Y: e.activation(M[:, :], Y[:, :], ACT.Exp, scale=sp[:, 7, k:k + 1]), tg, t_sp, fam)
            tb = A(lambda e, k=k, Y=Y: e.activation(Y[:, :], Y[:, :], ACT.Exp, scale=sp[:, 5, k:k + 1]), ta)
            ta = A(lambda e, M=M: e.activation(M[:, :], M[:, :], ACT.Sqrt, bias=one[:, 0:1], scale=-1.0), ta)
            ta = V(lambda e, M=M: e.memset(M[:, 0:T:1024], 1.0), ta)
            t = V(lambda e, X=X, k=k: e.tensor_tensor(X[:, :], X[:, :], XN[:, k, :], ALU.mult), tg)
            t = V(lambda e, X=X, M=M: e.tensor_tensor(X[:, :], X[:, :], M[:, :], ALU.mult), t, ta)
            fam = [t]
            tt = [V(lambda e, X=X, Y=Y, b=b: e.tensor_tensor_scan(
                X[:, b * 1024:b * 1024 + 1024], Y[:, b * 1024:b * 1024 + 1024], X[:, b * 1024:b * 1024 + 1024],
                0.0, ALU.mult, ALU.add), t, tb) for b in range(2)]
            free[s] = [Q.dma("sync", f"s1{s}", scratch["s1"][k * 128:(k + 1) * 128, :], X[:, :], tt)]
        return Q.everything()


def ffn1(nc, Q, sb, io, scratch, bank, split, XH, XL, done):
    V = lambda fn, *a: Q.op("vector", fn, *a)
    A = lambda fn, *a: Q.op("scalar", fn, *a)
    P = lambda fn, *a: Q.op("tensor", fn, *a)
    G = lambda fn, *a: Q.op("gpsimd", fn, *a)
    with ExitStack() as c:
        def ring(name, n, shape, dt=F32):
            r = Ring([sb(c, f"{name}{i}", shape, dt) for i in range(n)])
            for i in range(n):
                r.hold(i, done)
            return r
        pk = ring("pk", 2, [128, 512], I32)
        sc = ring("sc", 2, [128, 512])
        w1 = ring("w1", 1, [128, 512], I32)
        w2 = ring("w2", 1, [128, 512], I32)
        wf = ring("wf", 1, [128, 2, 512])
        wh = ring("qh", 4, [128, 2, 512], F32R)
        wl = [sb(c, f"ql{i}", [128, 2, 512], F32R) for i in range(4)]
        HH = sb(c, "QHH", [128, 2, T], F32R)
        HL = sb(c, "QHL", [128, 2, T], F32R)
        ACC = sb(c, "QACC", [128, 4, T])
        g2 = ring("g2", 2, [128, 512])
        hd = ring("qhd", 2, [128, 512])
        bk = Ring(bank)
        for i in range(8):
            bk.hold(i, done)

        def weight(pk_src, sc_src):
            n, r, f = pk.take()
            tp = [Q.dma("sync", f"pk{n}", r[:, a:b], s, f) for a, b, s in pk_src]
            m, s_, f = sc.take()
            ts = [Q.dma("sync", f"sc{m}", s_[p0:p0 + 128, a:b], s, f) for p0, a, b, s in sc_src]
            i1, a, f1 = w1.take()
            i2, b, f2 = w2.take()
            t = V(lambda e: e.tensor_scalar(a[:, :], r[:, :], 255, None, ALU.bitwise_and), tp, f1)
            pk.hold(n, t)
            t = V(lambda e: e.tensor_scalar(b[:, :], a[:, :], 12, None, ALU.logical_shift_left), t, f2)
            t = V(lambda e: e.tensor_tensor(a[:, :], a[:, :], b[:, :], ALU.bitwise_or), t)
            t = V(lambda e: e.tensor_scalar(b[:, :], a[:, :], 9, 0x0E000E00, ALU.logical_shift_left, ALU.bitwise_and), t)
            t = V(lambda e: e.tensor_scalar(a[:, :], a[:, :], 12, -0x7FFF8000, ALU.logical_shift_left, ALU.bitwise_and), t)
            t = V(lambda e: e.tensor_tensor(a[:, :], a[:, :], b[:, :], ALU.bitwise_or), t)
            w1.hold(i1, t)
            w2.hold(i2, t)
            i3, w, f3 = wf.take()
            half = a[:, :].bitcast(F16).rearrange("p (n s) -> p n s", s=2)
            tw = [V(lambda e, s2=s2: e.scalar_tensor_tensor(out=w[:, s2, :], in0=half[:, :, s2], scalar=16384.0,
                                                            in1=s_[:, :], op0=ALU.mult, op1=ALU.mult), t, ts, f3)
                  for s2 in range(2)]
            w1.hold(i1, tw)
            sc.hold(m, tw)
            i4, h, f4 = wh.take()
            th = split(w[:, :, :], h[:, :, :], wl[i4][:, :, :], tw, f4, low_eng="gpsimd")
            wf.hold(i3, th)
            return i4, h, wl[i4], th

        tH = [[done] for _ in range(4)]
        tA = {}
        Q.x = None
        prev_down = None

        def down(j, hs, wd):
            for o in range(4):
                for n in range(4):
                    sl = slice(n * 512, n * 512 + 512)
                    b, kb, f = bk.take()
                    i4, w, wlo, tw = wd
                    t = P(lambda e, kb=kb, o=o, sl=sl: mm3(e, kb[:, :], [
                        (w[:, s2, o * 128:(o + 1) * 128], wlo[:, s2, o * 128:(o + 1) * 128], HH[:, s2, sl], HL[:, s2, sl])
                        for s2 in range(2)]), tw, hs[n], f)
                    if j == 0:
                        ta = A(lambda e, kb=kb, o=o, sl=sl: e.copy(ACC[:, o, sl], kb[:, :]), t)
                    else:
                        ta = V(lambda e, kb=kb, o=o, sl=sl: e.tensor_tensor(ACC[:, o, sl], ACC[:, o, sl], kb[:, :],
                                                                            ALU.add), t, tA[(o, n)])
                    tA[(o, n)] = ta
                    bk.hold(b, ta)
                    tH[n] = [t]
            wh.hold(wd[0], t)

        def weights(j):
            out = []
            for p in ("gate", "up"):
                src = io[p + "_pk"]
                scs = io[p + "_sc"]
                cols = slice(j * 256, j * 256 + 256)
                out.append(weight(
                    [(q * 256, q * 256 + 256, src[q * 128:(q + 1) * 128, cols]) for q in range(2)],
                    [(0, q * 256, q * 256 + 256, scs[q * 8:q * 8 + 8, cols].unsqueeze(1).to_broadcast([8, 16, 256]))
                     for q in range(2)]))
            out.append(weight([(0, 512, io["down_pk"][j * 128:(j + 1) * 128, :])],
                              [(0, 0, 512, io["down_scT"][j * 8:j * 8 + 8, :].unsqueeze(1).to_broadcast([8, 16, 512]))]))
            return out

        wnext = weights(0)
        for j in range(16):
            wg, wu, wd = wnext
            hs = [[] for _ in range(4)]
            for s2 in range(2):
                cs = [(q * 256 + s2 * 128, q * 256 + s2 * 128 + 128) for q in range(2)]
                for n in range(4):
                    sl = slice(n * 512, n * 512 + 512)

                    def mats(w):
                        return [(w[1][:, par, cs[q][0]:cs[q][1]], w[2][:, par, cs[q][0]:cs[q][1]],
                                 XH[:, 2 * q + par, sl], XL[:, 2 * q + par, sl]) for q in range(2) for par in range(2)]
                    b1, k1, f1 = bk.take()
                    t1 = P(lambda e, k1=k1, m=mats(wg): mm3(e, k1[:, :], m), wg[3], f1)
                    b2, k2, f2 = bk.take()
                    t2 = P(lambda e, k2=k2, m=mats(wu): mm3(e, k2[:, :], m), wu[3], f2)
                    m, s, f = g2.take()
                    t = A(lambda e, s=s, k1=k1: e.activation(s[:, :], k1[:, :], ACT.Square), t1, f)
                    t = V(lambda e, s=s, k1=k1: e.scalar_tensor_tensor(out=s[:, :], in0=s[:, :], scalar=1.0 / 0.044715,
                                                                       in1=k1[:, :], op0=ALU.add, op1=ALU.mult), t)
                    t = A(lambda e, s=s: e.activation(s[:, :], s[:, :], ACT.Tanh, scale=0.7978845608028654 * 0.044715), t)
                    t = V(lambda e, s=s, k1=k1: e.scalar_tensor_tensor(out=s[:, :], in0=s[:, :], scalar=1.0,
                                                                       in1=k1[:, :], op0=ALU.add, op1=ALU.mult), t)
                    bk.hold(b1, t)
                    m2, h, f = hd.take()
                    th = V(lambda e, h=h, s=s, k2=k2: e.scalar_tensor_tensor(out=h[:, :], in0=s[:, :], scalar=0.5,
                                                                             in1=k2[:, :], op0=ALU.mult, op1=ALU.mult), t, t2, f)
                    bk.hold(b2, th)
                    g2.hold(m, th)
                    tt = split(h[:, :], HH[:, s2, sl], HL[:, s2, sl], th, tH[n], low_eng="gpsimd")
                    hd.hold(m2, tt)
                    hs[n] += tt
            wh.hold(wg[0], t1)
            wh.hold(wu[0], t2)
            if j < 15:
                wnext = weights(j + 1)
            down(j, hs, wd)
        sd = None
        for o in range(4):
            for n in range(4):
                sl = slice(n * 512, n * 512 + 512)
                t = A(lambda e, o=o, sl=sl: e.activation(ACC[:, o, sl], ACC[:, o, sl], ACT.Silu), tA[(o, n)])
            Q.dma("sync", "g1d", scratch["g1"][o * 128:(o + 1) * 128, :], ACC[:, o, :], t)
        return Q.everything()


def laid_out(inputs):
    g = {k: np.ascontiguousarray(np.asarray(v)) for k, v in inputs.items()}
    f = np.float32
    x = g["L0_attn_x"].reshape(T, 512)
    o = {"x": x, "xT": x.T}
    for n in ("Wq", "Wk", "Wv", "Wg", "Wo"):
        o[n] = g["L0_attn_" + n]
    wab = np.zeros((512, 128), f)
    wab[:, 0:16], wab[:, 32:48] = g["L0_attn_Wa"], g["L0_attn_Wb"]
    bab = np.zeros((128, 1), f)
    bab[0:16, 0], bab[32:48, 0] = g["L0_attn_ba"], g["L0_attn_bb"]
    o["Wab"], o["bab"] = wab, bab
    cw = np.zeros((128, 16, 3, 5), f)
    for i, n in enumerate("qkv"):
        cw[:, :, i, 0:4] = g[f"L0_attn_{n}cw"].reshape(16, 128, 4).transpose(1, 0, 2)
        cw[:, :, i, 4] = g[f"L0_attn_{n}cb"].reshape(16, 128).T
    o["cw"] = cw
    o["ln"] = np.stack([g["L0_attn_ln_w"], g["L0_attn_ln_b"]], 1)
    o["gate_wT"], o["up_wT"] = g["L0_ffn_gate_w"].T, g["L0_ffn_up_w"].T
    o["down_wT"] = g["L0_ffn_down_w"].T
    s = np.zeros((128, 26), f)
    s[:, 0:11] = g["L0_ffn_gate_s"].reshape(11, 128).T
    s[:, 11:22] = g["L0_ffn_up_s"].reshape(11, 128).T
    s[:, 22:26] = g["L0_ffn_down_s"].reshape(4, 128).T
    o["ffn0_s"] = s
    for n in ("ig", "ag"):
        w = np.zeros((4, 128, 128), f)
        for h in range(16):
            a = 32 * (h % 4)
            w[h // 4, a:a + 32, a:a + 32] = g[f"L1_attn_{n}_w"][h]
        o[n + "_w"] = w
    v = np.zeros((128, 4, 3), f)
    v[:, :, 0] = g["L1_attn_ig_b"].reshape(4, 128).T
    v[:, :, 1] = g["L1_attn_ag_b"].reshape(4, 128).T
    v[:, :, 2] = g["L1_attn_a_param"].reshape(4, 128).T
    o["l1v"] = v
    n = np.arange(4096).reshape(16, 128, 2).transpose(0, 2, 1).reshape(-1)
    for p in ("gate", "up"):
        o[p + "_pk"] = g[f"L1_ffn_{p}_W_packed"].T[:, n]
        o[p + "_sc"] = g[f"L1_ffn_{p}_scales"].T[:, n]
    o["down_pk"] = g["L1_ffn_down_W_packed"].T
    o["down_scT"] = g["L1_ffn_down_scales"].T
    c = np.zeros((128, C_N), f)
    c[:, 0:128] = np.eye(128)
    c[:, C_CM:C_CM + 128] = np.eye(128) - 1.0 / 128
    c[:, C_J:C_J + 128] = 1.0 / 128
    r = np.arange(128) % 32 // 16
    cc = np.arange(32) // 16
    c[:, C_M16:C_M16 + 32] = -1.0 * (r[:, None] == cc[None, :])
    c[:, C_OFF:C_OFF + 32] = -1.0 * ((r[:, None] == 0) & (cc[None, :] == 1))
    c[:, C_FLAG] = r == 0
    c[:, C_FLAG + 1] = r == 1
    o["consts"] = c
    return {k: np.ascontiguousarray(a) for k, a in o.items()}


SCRATCH = {"a": [16, T], "g": [16, T], "gc": [256], "g0": [512, T], "og": [2048, T], "x1": [T, 512],
           "s1": [512, T], "g1": [512, T]}


def kernel(**inputs):
    import concourse.bacc as _bacc
    from concourse.bass_utils import run_bass_kernel_spmd as _run

    nc = _bacc.Bacc("TRN2", target_bir_lowering=False, num_devices=1)
    arrays, io = {}, {}
    for name, a in laid_out(inputs).items():
        arrays["in_" + name] = a
        io[name] = nc.dram_tensor("in_" + name, a.shape, mybir.dt.from_np(a.dtype), kind="ExternalInput").ap()
    out = {"y": nc.dram_tensor("out_y", [T, 512], F32, kind="ExternalOutput").ap()}
    scratch = {n: nc.dram_tensor("tmp_" + n, s, F32).ap() for n, s in SCRATCH.items()}
    program(nc, io, out, scratch)
    r = _run(nc, [arrays], core_ids=[0])
    return r.results[0]["out_y"].reshape(2, 1024, 512)
```

```python
from contextlib import ExitStack

import numpy as np

import concourse.bass as bass
from concourse import mybir

F32 = mybir.dt.float32
F32R = mybir.dt.float32r
F16 = mybir.dt.float16
I32 = mybir.dt.int32
ALU = mybir.AluOpType
ACT = mybir.ActivationFunctionType

T = 2048
H = 16
EPS = 1e-5

C_ID, C_CM, C_J, C_M16, C_OFF, C_FLAG, C_N = 0, 128, 256, 384, 416, 448, 450


class Tok:

    __slots__ = ("sem", "val", "used")

    def __init__(self, sem, val=None):
        self.sem, self.val, self.used = sem, val, False


class Queues:

    ENG = ("tensor", "vector", "scalar", "gpsimd", "sync")

    def __init__(self, nc, ctx):
        self.nc = nc
        self.q = {e: [] for e in self.ENG}
        self.sem = {e: ctx.enter_context(nc.semaphore("s_" + e)) for e in self.ENG}
        self.ctx = ctx
        self.count = {}
        self.last = {}

    def op(self, eng, fn, *after):
        t = Tok(eng)
        self.q[eng].append((fn, flat(after), t))
        self.last[eng] = t
        return t

    def dma(self, eng, name, out, in_, *after):
        if name not in self.sem:
            self.sem[name] = self.ctx.enter_context(self.nc.semaphore("d_" + name))
            self.count[name] = 0
        self.count[name] += 16
        t = Tok(name, self.count[name])
        self.q[eng].append((lambda e: e.dma_start(out, in_), flat(after), t))
        return t

    def everything(self):
        return list(self.last.values()) + [Tok(n, c) for n, c in self.count.items()]

    def emit(self, block):
        for items in self.q.values():
            for _, after, _ in items:
                for a in after:
                    a.used = True
        for items in self.q.values():
            n = 0
            for _, _, t in items:
                if t.val is None and t.used:
                    n += 1
                    t.val = n
                elif t.val is None:
                    t.val = 0
        for name in self.ENG:
            hook = {"tensor": block.tensor, "vector": block.vector, "scalar": block.scalar,
                            "gpsimd": block.gpsimd, "sync": block.sync}[name]

            def body(e, name=name):
                met = {}
                for fn, after, t in self.q[name]:
                    need = {}
                    for a in after:
                        need[a.sem] = max(need.get(a.sem, 0), a.val)
                    for s, v in need.items():
                        if v > met.get(s, 0):
                            e.wait_ge(self.sem[s], v)
                            met[s] = v
                    ins = fn(e)
                    if ins is not None and t.used:
                        ins.then_inc(self.sem[t.sem], 16 if t.sem in self.count else 1)
                    elif ins is not None and t.sem in self.count:
                        ins.then_inc(self.sem[t.sem], 16)

            hook(body)


def flat(xs):
    out = []
    for x in xs:
        if x is None:
            continue
        if isinstance(x, (list, tuple)):
            out += flat(x)
        else:
            out.append(x)
    return out


class Ring:

    def __init__(self, slots):
        self.slots, self.free, self.n = slots, [[] for _ in slots], -1

    def take(self):
        self.n = (self.n + 1) % len(self.slots)
        return self.n, self.slots[self.n], self.free[self.n]

    def hold(self, i, *users):
        self.free[i] = flat(users)


class Slots(Ring):

    def __init__(self, slots, users):
        super().__init__(slots)
        self.idle = []
        for i in range(len(slots)):
            self.hold(i, users)

    def take(self):
        i = self.idle.pop(0)
        return i, self.slots[i], self.free[i]

    def hold(self, i, *users):
        super().hold(i, *users)
        self.idle.append(i)


def mm3(e, out, pairs, first=True, last=True):
    n = len(pairs)
    for k, (wh, wl, xh, xl) in enumerate(pairs):
        e.matmul(out, wh, xh, start=first and k == 0, stop=False)
        e.matmul(out, wh, xl, start=False, stop=False)
        m = e.matmul(out, wl, xh, start=False, stop=last and k == n - 1)
    return m


def f32(ap):
    return ap.bitcast(F32)


def program(nc, io, out, scratch, stages=99):
    with ExitStack() as ctx:
        Q = Queues(nc, ctx)
        V = lambda fn, *a: Q.op("vector", fn, *a)
        A = lambda fn, *a: Q.op("scalar", fn, *a)
        P = lambda fn, *a: Q.op("tensor", fn, *a)
        G = lambda fn, *a: Q.op("gpsimd", fn, *a)

        def sb(c, name, shape, dt=F32):
            return c.enter_context(nc.sbuf_tensor("b_" + name, shape, dt))

        bank = [ctx.enter_context(nc.psum_tensor(f"bank{i}", [128, 512], F32)) for i in range(8)]
        cst = sb(ctx, "cst", [128, C_N])
        ident, cmat, jmat = cst[:, 0:128], cst[:, C_CM:C_CM + 128], cst[:, C_J:C_J + 128]
        eps = sb(ctx, "eps", [128, 1])
        t_cst = Q.dma("gpsimd", "cst", cst[:, :], io["consts"])
        t_eps = V(lambda e: e.memset(eps[:, :], EPS))

        def split(src, hi, lo, after, free=(), src_is_psum=False, low_eng="vector"):
            th = A(lambda e: e.copy(hi, src), after, free)
            tl = Q.op(low_eng, lambda e: e.tensor_tensor(lo, src, f32(hi), ALU.subtract), th, after, free)
            return [th, tl]

        def norm_rows(x, xn, c, tag, after):
            st = sb(c, "st" + tag, [128, 16, 6])
            mv = sb(c, "mv" + tag, [128, 16, 2])
            sd = sb(c, "sd" + tag, [128, 16])
            rs = sb(c, "rs" + tag, [128, 16])
            out, ready = [], []

            def stats(g):
                for i in range(g, g + 2):
                    t = V(lambda e, i=i: e.bn_stats(st[:, i, :], x[:, i, :]), after[i])
                    t = V(lambda e, i=i: e.bn_aggr(mv[:, i, :], st[:, i, :]), t)
                ready.append(A(lambda e: e.activation(sd[:, g:g + 2], mv[:, g:g + 2, 1], ACT.Sqrt, bias=eps[:, 0:1]),
                               t, t_eps))

            def scale(g):
                t = V(lambda e: e.reciprocal(rs[:, g:g + 2], sd[:, g:g + 2]), ready.pop(0))
                for i in range(g, g + 2):
                    out.append(V(lambda e, i=i: e.tensor_scalar(xn[:, i, :], x[:, i, :], mv[:, i, 0:1], rs[:, i:i + 1],
                                                                ALU.subtract, ALU.mult), t))
                return out[g:g + 2]
            return stats, scale

        def turned(xn, i, order, bk, after, free):
            def go(e):
                for k in range(4):
                    m = e.transpose(bk[:, k * 128:(k + 1) * 128], order(xn, i, k), ident)
                return m
            return P(go, after, free, t_cst)

        plain = lambda xn, i, k: xn[:, i, k * 128:(k + 1) * 128]

        layer = ctx.enter_context(ExitStack())
        XH = sb(layer, "XH", [128, 4, T], F32R)
        XL = sb(layer, "XL", [128, 4, T], F32R)
        coef = sb(layer, "coef", [128, 16, 3, 16])
        GC = sb(layer, "GC", [128, 16, 16])
        with ExitStack() as c:
            x = sb(c, "x0", [128, 16, 512])
            xn = sb(c, "xn0", [128, 16, 512])
            tx = [Q.dma("scalar" if i % 2 else "sync", f"x{i}", x[:, i * 2:i * 2 + 2, :],
                        io["x"].rearrange("(i p) d -> p i d", p=128)[:, i * 2:i * 2 + 2, :]) for i in range(8)]
            stats, scale = norm_rows(x, xn, c, "0", [tx[i // 2] for i in range(16)])
            wab = sb(c, "wab", [128, 4, 128])
            wabh = sb(c, "wabh", [128, 4, 128], F32R)
            wabl = sb(c, "wabl", [128, 4, 128], F32R)
            bab = sb(c, "bab", [128, 1])
            t_wab = Q.dma("sync", "wab", wab[:, :, :], io["Wab"].rearrange("(k p) n -> p k n", p=128))
            t_bab = Q.dma("sync", "bab", bab[:, :], io["bab"])
            tb = [None] * 8
            tX = []
            stats(0)
            stats(2)
            tn = {}
            late, tZ = [], []
            for i in range(16):
                b = i % 4
                if i % 2 == 0:
                    if i < 12:
                        stats(i + 4)
                    tn[i], tn[i + 1] = scale(i)
                t = turned(xn, i, plain, bank[b], tn[i], tb[b])

                def cut(i=i, b=b, t=t):
                    src = bank[b][:, :].rearrange("p (k t) -> p k t", k=4)
                    tb[b] = split(src, XH[:, :, i * 128:(i + 1) * 128], XL[:, :, i * 128:(i + 1) * 128], t)
                    tX.append(tb[b])
                late.append(cut)
                if i == 3:
                    t_ws = split(wab[:, :, :], wabh[:, :, :], wabl[:, :, :], t_wab, low_eng="gpsimd")
                if len(late) > 2:
                    late.pop(0)()
                if i == 15:
                    late.pop(0)()
                    late.pop(0)()
                while len(tX) >= 4 * len(tZ) + 4:
                    n = len(tZ)
                    sl = slice(n * 512, n * 512 + 512)
                    tZ.append(P(lambda e, n=n, sl=sl: mm3(e, bank[4 + n][:, :], [
                        (wabh[:, k, :], wabl[:, k, :], XH[:, k, sl], XL[:, k, sl]) for k in range(4)]),
                        t_ws, tX[4 * n:4 * n + 4]))
            S = sb(c, "S", [128, T])
            SG = sb(c, "SG", [128, T])
            Gm = sb(c, "Gm", [128, T])
            TB = sb(c, "TB", [128, T])
            BT = sb(c, "BT", [128, T])
            zero = sb(c, "zero", [128, 128])
            gc16 = sb(c, "gc16", [16, 16])
            t_z = G(lambda e: e.memset(zero[:, :], 0.0))
            t_tb = G(lambda e: e.memset(TB[:, :], 0.0))
            tS = []
            for n in range(4):
                sl = slice(n * 512, n * 512 + 512)
                tS.append(A(lambda e, n=n, sl=sl: e.activation(S[:, sl], bank[4 + n][:, :], ACT.Sigmoid,
                                                               bias=bab[:, 0:1]), tZ[n], t_bab))
            t1 = V(lambda e: e.memset(SG[0:16, :].rearrange("p (c t) -> p c t", t=128)[:, :, 127:128], 1.0))
            tg = []
            for ch in range(16):
                o = ch * 128
                a = V(lambda e, o=o: e.tensor_tensor_scan(Gm[0:16, o:o + 128], S[0:16, o:o + 128], zero[0:16, :],
                                                          1.0, ALU.mult, ALU.add), tS[ch // 4], t_z)
                lo = o - 1 if o else None
                b = V(lambda e, o=o: e.tensor_tensor_scan(SG[0:16, o:o + 127][:, ::-1], S[0:16, o + 1:o + 128][:, ::-1],
                                                          zero[0:16, 0:127], 1.0, ALU.mult, ALU.add), t1)
                tg += [a, b]
            t2 = V(lambda e: e.tensor_scalar(TB[0:16, 1:T], Gm[0:16, 0:T - 1], -1.0, None, ALU.mult), tg, t_tb)
            t2 = V(lambda e: e.memset(TB[0:16, :].rearrange("p (c t) -> p c t", t=128)[:, :, 0:1], -1.0), t2)
            t3 = A(lambda e: e.copy(TB[32:48, :], S[32:48, :]), tS, t_tb)
            t4 = A(lambda e: e.copy(BT[0:16, :], S[32:48, :]), tS)
            t5 = V(lambda e: e.tensor_tensor(TB[64:80, :], BT[0:16, :], SG[0:16, :], ALU.mult), t4, tg, t_tb)
            t6 = V(lambda e: e.tensor_copy(gc16[:, :], Gm[0:16, :].rearrange("p (c t) -> p c t", t=128)[:, :, 127]), tg)
            d1 = Q.dma("sync", "ad", scratch["a"], S[0:16, :], tS)
            d2 = Q.dma("sync", "gd", scratch["g"], Gm[0:16, :], tg)
            d3 = Q.dma("sync", "gcd", scratch["gc"].rearrange("(h c) -> h c", h=16), gc16[:, :], t6)
            t_gc = Q.dma("sync", "gcl", GC[:, :, :].rearrange("p h c -> p (h c)"),
                         scratch["gc"].partition_broadcast(128), d3)
            t_coef = []
            for i in range(16):
                b = i % 4
                t = P(lambda e, i=i, b=b: e.transpose(bank[b][:, 0:128], TB[:, i * 128:(i + 1) * 128], ident),
                      [t2, t3, t5], tb[b], t_cst)
                tb[b] = A(lambda e, i=i, b=b: e.copy(
                    coef[:, i, :, :], bank[b][:, 0:96].rearrange("p (q r) -> p q r", q=3)[:, :, 0:16]), t)
                t_coef.append(tb[b])
            t_scr = [d1, d2]
            done = Q.everything()
        if stages == 0:
            Q.dma("sync", "dbg", out["d0"], XH[:, :, :].bitcast(F32), done)
            Q.dma("sync", "dbg", out["d1"], XL[:, :, :].bitcast(F32), done)
            Q.dma("sync", "dbg", out["d2"], coef[:, :, :, :], done)
            Q.dma("sync", "dbg", out["d3"], GC[:, :, :], done)
        if stages >= 1:
            done = ffn0(nc, Q, sb, io, scratch, bank, split, XH, XL, done)
        if stages >= 2:
            done = attn0(nc, Q, sb, io, scratch, bank, split, XH, XL, coef, GC, cst, eps, done)
        layer.close()
        if stages >= 3:
            lay = ctx.enter_context(ExitStack())
            at = (nc.sbuf_base + 31) // 32 * 32
            YH = sb(lay, "XH1", [128, 4, T], F32R)
            YL = sb(lay, "XL1", [128, 4, T], F32R)
            done = mix0(nc, Q, sb, io, scratch, bank, split, cst, eps, YH, YL, done)
        if stages >= 4:
            ffn1(nc, Q, sb, io, scratch, bank, split, YH, YL, at, cst, out, done)
        Q.op("sync", lambda e: None, Q.everything())
        block = ctx.enter_context(nc.Block())
        Q.emit(block)


def ffn0(nc, Q, sb, io, scratch, bank, split, XH, XL, done):
    V = lambda fn, *a: Q.op("vector", fn, *a)
    A = lambda fn, *a: Q.op("scalar", fn, *a)
    P = lambda fn, *a: Q.op("tensor", fn, *a)
    with ExitStack() as c:
        raw = Ring([sb(c, f"fr{i}", [128, 4, 128]) for i in range(3)])
        wh = Slots([sb(c, f"fwh{i}", [128, 4, 128], F32R) for i in range(6)], done)
        wl = [sb(c, f"fwl{i}", [128, 4, 128], F32R) for i in range(6)]
        HH = sb(c, "HH", [128, 4, T], F32R)
        HL = sb(c, "HL", [128, 4, T], F32R)
        ACC = sb(c, "ACC", [128, 4, T])
        sil = Ring([sb(c, f"sil{i}", [128, 512]) for i in range(2)])
        hd = Ring([sb(c, f"hd{i}", [128, 512]) for i in range(2)])
        sc = sb(c, "fsc", [128, 26])
        t_sc = Q.dma("sync", "fsc", sc[:, :], io["ffn0_s"], done)
        bk = Ring(bank)
        for i in range(8):
            bk.hold(i, done)
        for r in (raw, sil, hd):
            for i in range(len(r.slots)):
                r.hold(i, done)

        def weight(src):
            n, r, f = raw.take()
            t = Q.dma("sync", f"fr{n}", r[:, :, :], src, f)
            m, w, f = wh.take()
            ts = split(r[:, :, :], w[:, :, :], wl[m][:, :, :], t, f, low_eng="gpsimd")
            raw.hold(n, ts)
            return m, w, wl[m], ts

        gw = io["gate_wT"].rearrange("(k p) n -> p k n", p=128)
        uw = io["up_wT"].rearrange("(k p) n -> p k n", p=128)
        dw = io["down_wT"]
        tH = [[done for _ in range(4)] for _ in range(4)]
        tA = {}
        both = lambda it: [weight(w[:, :, it * 128:(it + 1) * 128]) for w in (gw, uw)]
        nxt = both(0)
        for g0, g1 in ((0, 4), (4, 8), (8, 11)):
            hs = {}
            for it in range(g0, g1):
                (ng, wg, wgl, tg), (nu, wu, wul, tu) = nxt
                for n in range(4):
                    if n == 1 and it + 1 < g1:
                        nxt = both(it + 1)
                    if n == 1 and it + 1 == g1:
                        ws = [weight(dw[i * 128:(i + 1) * 128, :].rearrange("p (k n) -> p k n", k=4))
                              for i in range(g0, g1)]
                    sl = slice(n * 512, n * 512 + 512)
                    b1, k1, f1 = bk.take()
                    t1 = P(lambda e, k1=k1, wg=wg, wgl=wgl, sl=sl: mm3(e, k1[:, :], [
                        (wg[:, k, :], wgl[:, k, :], XH[:, k, sl], XL[:, k, sl]) for k in range(4)]), tg, f1)
                    b2, k2, f2 = bk.take()
                    t2 = P(lambda e, k2=k2, wu=wu, wul=wul, sl=sl: mm3(e, k2[:, :], [
                        (wu[:, k, :], wul[:, k, :], XH[:, k, sl], XL[:, k, sl]) for k in range(4)]), tu, f2)
                    m, s, f = sil.take()
                    ts = A(lambda e, s=s, k1=k1, it=it: e.activation(s[:, :], k1[:, :], ACT.Silu,
                                                                     scale=sc[:, it:it + 1]), t1, f, t_sc)
                    bk.hold(b1, ts)
                    m2, h, f = hd.take()
                    th = V(lambda e, h=h, k2=k2, s=s, it=it: e.scalar_tensor_tensor(
                        out=h[:, :], in0=k2[:, :], scalar=sc[:, 11 + it:12 + it], in1=s[:, :],
                        op0=ALU.mult, op1=ALU.mult), t2, ts, f)
                    bk.hold(b2, th)
                    sil.hold(m, th)
                    q = it - g0
                    tt = split(h[:, :], HH[:, q, sl], HL[:, q, sl], th, tH[q][n], low_eng="gpsimd")
                    hd.hold(m2, tt)
                    hs[(q, n)] = tt
                wh.hold(ng, t1)
                wh.hold(nu, t2)
            if g1 < 11:
                nxt = both(g1)
            for n in range(4):
                for o in range(4):
                    sl = slice(n * 512, n * 512 + 512)
                    b, kb, f = bk.take()
                    t = P(lambda e, kb=kb, o=o, sl=sl, ws=ws: mm3(e, kb[:, :], [
                        (w[:, o, :], wlo[:, o, :], HH[:, q, sl], HL[:, q, sl])
                        for q, (_, w, wlo, _) in enumerate(ws)]),
                        [w[3] for w in ws], [hs[(q, n)] for q in range(g1 - g0)], f)
                    if g0 == 0:
                        ta = A(lambda e, kb=kb, o=o, sl=sl: e.copy(ACC[:, o, sl], kb[:, :]), t)
                    else:
                        ta = V(lambda e, kb=kb, o=o, sl=sl: e.tensor_tensor(ACC[:, o, sl], ACC[:, o, sl], kb[:, :],
                                                                            ALU.add), t, tA[(o, n)])
                    tA[(o, n)] = ta
                    bk.hold(b, ta)
                    tH[0][n] = t
                    if g1 == 11:
                        ta = A(lambda e, o=o, sl=sl: e.activation(ACC[:, o, sl], ACC[:, o, sl], ACT.Silu,
                                                                  scale=sc[:, 22 + o:23 + o]), ta)
                        Q.dma("sync", "g0d", scratch["g0"][o * 128:(o + 1) * 128, sl], ACC[:, o, sl], ta)
            for n in range(4):
                for q in range(4):
                    tH[q][n] = tH[0][n]
            for w in ws:
                wh.hold(w[0], t)
        return Q.everything()


def merged(*streams):
    order = []
    for k, x in enumerate(streams):
        x = list(x)
        for i, step in enumerate(x):
            at, step = step if isinstance(step, tuple) else ((i + 0.5) / len(x), step)
            order.append((at, k, i, step))
    order.sort(key=lambda o: o[:3])
    for *_, step in order:
        step()


def attn0(nc, Q, sb, io, scratch, bank, split, XH, XL, coef, GC, cst, eps, done):
    V = lambda fn, *a: Q.op("vector", fn, *a)
    A = lambda fn, *a: Q.op("scalar", fn, *a)
    P = lambda fn, *a: Q.op("tensor", fn, *a)
    G = lambda fn, *a: Q.op("gpsimd", fn, *a)
    KS = 128.0 ** -0.5
    with ExitStack() as c:
        def ring(name, n, shape, dt=F32):
            r = Ring([sb(c, f"{name}{i}", shape, dt) for i in range(n)])
            for i in range(n):
                r.hold(i, done)
            return r

        ident, cmat, jmat = cst[:, 0:128], cst[:, C_CM:C_CM + 128], cst[:, C_J:C_J + 128]
        raw = ring("wr", 2, [128, 4, 128])
        wh = ring("wh", 5, [128, 4, 128], F32R)
        wl = [sb(c, f"wl{i}", [128, 4, 128], F32R) for i in range(5)]
        cw = sb(c, "cw", [128, 16, 3, 5])
        lnw = sb(c, "lnw", [128, 2])
        t_cw = Q.dma("sync", "cw", cw[:, :, :, :], io["cw"], done)
        t_ln = Q.dma("sync", "lnw", lnw[:, :], io["ln"], done)
        t_ln = V(lambda e: e.tensor_scalar(lnw[:, :], lnw[:, :], 0.5, None, ALU.mult), t_ln)
        rawx = ring("rx", 2, [128, 515])
        zt = ring("zt", 2, [128, 512])
        vt = ring("vt", 2, [128, 512])
        tails = sb(c, "tails", [128, 3, 2, 3])
        abc = ring("abc", 2, [128, 512])
        gbc = ring("gbc", 1, [128, 512])
        KQA = sb(c, "KQA", [128, 3, 2, 4, 128])
        KQ = Ring([0, 1])
        QG = ring("QG", 2, [128, 2, 4, 128])
        KD = ring("KD", 2, [128, 2, 4, 128])
        VC = ring("VC", 2, [128, 2, 4, 128])
        XPA = sb(c, "XPA", [128, 3, 8, 128])
        XP = Ring([1, 2])
        for r in (KQ, XP):
            for i in range(2):
                r.hold(i, done)
        q_all, X = KQA[:, 2], XPA[:, 0]

        def pair(ap, step, n=128):
            return bass.AP(tensor=ap.tensor, offset=ap.offset, ap=[list(ap.ap[0]), [step, 2], [1, n]])

        MF = ring("MF", 2, [128, 8, 128])
        D = ring("D", 3, [128, 130])
        XD = sb(c, "XD", [128, 16, 32])
        UN = sb(c, "UN", [128, 1024])
        XM = UN[:, 0:512].rearrange("p (m t) -> p m t", m=16)
        YY = UN[:, 512:1024].rearrange("p (m t) -> p m t", m=16)
        E1 = UN[:, :].rearrange("p (w a s b) -> p w a s b", w=2, a=16, s=2)
        XO = sb(c, "XO", [128, 8, 32])
        A16 = sb(c, "A16", [128, 16, 16])
        T16 = sb(c, "T16", [128, 16, 16])
        PR = sb(c, "PR", [128, 64])
        MN = sb(c, "MN", [128, 2, 16, 32])
        ZS = sb(c, "ZS", [128, 8, 32])
        ZT = sb(c, "ZT", [128, 8, 32])
        NF = sb(c, "NF", [64, 8, 64])
        Z2 = sb(c, "Z2", [128, 8, 64])
        ST = sb(c, "ST", [128, 2, 128])
        R = ring("R", 2, [128, 2, 128])
        WS = ring("WS", 2, [128, 2, 128])
        OS = ring("OS", 1, [128, 2, 4, 128])
        sq = sb(c, "sq", [128, 128])
        ss = sb(c, "ss", [128, 3, 8])
        rs = ring("rstd", 1, [128, 512])
        gg = ring("gg", 2, [128, 512])
        bk = Ring(bank[0:4])
        for i in range(4):
            bk.hold(i, done)
        pbk = Ring([bank[5], bank[6]])
        for i in range(2):
            pbk.hold(i, done)
        fb = {n: [done] for n in (4, 7)}
        t_i = []
        t_i.append(V(lambda e: e.memset(XD[:, :, :], 0.0), done))
        t_i.append(V(lambda e: e.memset(NF[:, :, :], 0.0), done))
        for m in MF.slots:
            t_i.append(V(lambda e, m=m: e.memset(m[:, :, :], 0.0), done))
        for d in D.slots:
            t_i.append(V(lambda e, d=d: e.memset(d[:, 0:1], 0.0), done))

        wsrc = {p: io[p].rearrange("(k p) n -> p k n", p=128) for p in ("Wq", "Wk", "Wv", "Wg")}

        loading = {}

        def load(p, h):
            if h < H:
                n, r, f = raw.take()
                loading[p] = (n, r, Q.dma("sync", f"wr{n}", r[:, :, :], wsrc[p][:, :, h * 128:(h + 1) * 128], f))

        def cut(p, h):
            if h < H:
                n, r, t = loading[p]
                m, w, f = wh.take()
                ts = split(r[:, :, :], w[:, :, :], wl[m][:, :, :], t, f, low_eng="gpsimd")
                raw.hold(n, ts)
                W[p, h % 2] = (m, w, wl[m], ts)

        def project(w, n):
            m, wt, wlo, tw = w
            got = {}
            sl = slice(n * 512, n * 512 + 512)

            def part(k0, k1):
                def go():
                    if k0 == 0:
                        got["b"], got["kb"], got["f"] = pbk.take()
                    kb = got["kb"]
                    got["t"] = P(lambda e: mm3(e, kb[:, :], [
                        (wt[:, k, :], wlo[:, k, :], XH[:, k, sl], XL[:, k, sl]) for k in range(k0, k1)],
                        first=k0 == 0, last=k1 == 4), tw, got["f"])
                return go
            return got, [part(0, 2), part(2, 4)]

        W = {}
        t_tail = {}
        unit = {}
        s_prev = {}
        st = {"S": [done]}

        def begin(u):
            s = unit.setdefault(u, {})
            for name, r in (("kq", KQ), ("qg", QG), ("kd", KD), ("vc", VC), ("xp", XP), ("mf", MF)):
                s[name + "n"], s[name], s[name + "f"] = r.take()
            s["k_slot"], s["p_slot"] = s["kq"], s["xp"]
            s["kq"], s["xp"] = KQA[:, s["kq"]], XPA[:, s["xp"]]
            s["t_kd"], s["t_vc"], s["t_xp"] = {}, {}, {}
            return s

        def conv(u, pi, p, b):
            h, half = divmod(u, 2)
            s = unit.setdefault(u, {})
            n = 2 * b + half
            g = {}
            v4 = lambda ap: ap.rearrange("p (c t) -> p c t", c=4)
            pre, mats = {}, [None, None]

            def first():
                pre["got"], pre["steps"] = project(W[p, h % 2], n)
                pre["steps"][0]()
                if p == "Wq":
                    g["gn"], g["g"], gf = gbc.take()
                    g["tl"] = Q.dma("sync", f"gb{g['gn']}", g["g"][:, :], scratch["g"][h:h + 1, n * 512:n * 512 + 512]
                                    .rearrange("a t -> (a t)").partition_broadcast(128), gf)

            def second():
                pre["steps"][1]()
                got = pre["got"]
                kb, t = got["kb"], got["t"]
                s["t_proj", p, b] = t
                rn, rx, rf = rawx.take()
                zn, z, zf = zt.take()
                tr = A(lambda e: e.copy(rx[:, 3:515], kb[:, :]), t, rf)
                tz = A(lambda e: e.activation(z[:, :], kb[:, :], ACT.Copy, scale=cw[:, h, pi, 3:4]), t, zf, t_cw)
                pbk.hold(got["b"], tr, tz)
                if half == 0:
                    th = G(lambda e: e.memset(rx[:, 0:3], 0.0), rf)
                    tt = G(lambda e: e.tensor_copy(tails[:, pi, b, :], rx[:, 512:515]), tr, t_tail.get((pi, b)))
                    t_tail[pi, b] = tt
                else:
                    th = tt = G(lambda e: e.tensor_copy(rx[:, 0:3], tails[:, pi, b, :]), rf, t_tail[pi, b])
                    t_tail[pi, b] = th
                for j in (2, 1, 0):
                    tz = V(lambda e, j=j: e.scalar_tensor_tensor(out=z[:, :], in0=rx[:, j:j + 512],
                                                                 scalar=cw[:, h, pi, j:j + 1], in1=z[:, :],
                                                                 op0=ALU.mult, op1=ALU.add), tz, tr, th)
                rawx.hold(rn, tz, tt)
                g["z"], g["zn"], g["tz"] = z, zn, tz

            def finish():
                z, zn, tz = g["z"], g["zn"], g["tz"]
                bias = cw[:, h, pi, 4:5]
                if p == "Wk":
                    ta = A(lambda e: e.activation(z[:, :], z[:, :], ACT.Silu, bias=bias), tz)
                    ta = V(lambda e: e.tensor_scalar(s["kq"][:, b, :, :], v4(z[:, :]), KS, None, ALU.mult), ta, s["kqf"])
                    s["t_k", b] = ta
                elif p == "Wq":
                    ta = A(lambda e: e.activation(q_all[:, b, :, :], v4(z[:, :]), ACT.Silu, bias=bias), tz,
                           s_prev.get("q"))
                    s["t_q", b] = ta
                    gg_, gn = g["g"], g["gn"]
                    tg = G(lambda e: e.tensor_tensor(s["qg"][:, b, :, :], q_all[:, b, :, :], v4(gg_[:, :]), ALU.mult),
                           ta, g["tl"], s["qgf"])
                    gbc.hold(gn, tg)
                    s["t_qg", b] = tg
                else:
                    vn, v, vf = vt.take()
                    ta = A(lambda e: e.activation(v[:, :], z[:, :], ACT.Silu, bias=bias), tz, vf)
                    s["v", b], s["t_v", b] = (vn, v), ta
                zt.hold(zn, ta)
            return [first, second], finish

        def decays(u, b):
            def go():
                h, half = divmod(u, 2)
                n = 2 * b + half
                an, a, af = abc.take()
                unit[u]["a", b] = (an, Q.dma("sync", f"ab{an}", a[:, :], scratch["a"][h:h + 1, n * 512:n * 512 + 512]
                                             .rearrange("a t -> (a t)").partition_broadcast(128), af))
            return go

        def turn_kv(u, b, c0):
            def steps():
                h, half = divmod(u, 2)
                s = unit[u]
                kq, kd, vc = s["kq"], s["kd"], s["vc"]
                vn, v = s["v", b]
                bn, kb, f = bk.take()

                def go(e):
                    for x in range(2):
                        e.transpose(kb[:, x * 256:x * 256 + 128], kq[:, b, c0 + x, :], ident)
                        m = e.matmul(kb[:, x * 256 + 128:x * 256 + 256], v[:, (c0 + x) * 128:(c0 + x + 1) * 128],
                                     cmat, start=True, stop=True)
                    return m
                t = P(go, s["t_k", b], s["t_v", b], f)
                for x in range(2):
                    i = b * 8 + half * 4 + c0 + x
                    s["t_kd"][b, c0 + x] = A(lambda e, x=x, i=i: e.activation(
                        kd[:, b, c0 + x, :], kb[:, x * 256:x * 256 + 128], ACT.Copy, scale=coef[:, i, 2, h:h + 1]),
                        t, s["kdf"])
                tv = A(lambda e: e.copy(vc[:, b, c0:c0 + 2, :],
                                        kb[:, :].rearrange("p (x a t) -> p x a t", x=2, a=2)[:, :, 1, :]), t, s["vcf"])
                bk.hold(bn, s["t_kd"][b, c0], s["t_kd"][b, c0 + 1], tv)
                s["t_vc"][b, c0] = s["t_vc"][b, c0 + 1] = tv
                if c0 == 2:
                    vt.hold(vn, t)
            return steps

        def scores(u, b, c0):
            def steps():
                h, half = divmod(u, 2)
                s = unit[u]
                kq = s["kq"]
                an, ta = s["a", b]
                bn, kb, f = bk.take()

                def go(e):
                    for x in range(2):
                        m = e.matmul(kb[:, x * 256:x * 256 + 256], kq[:, b, c0 + x, :],
                                     pair(kq[:, b, c0 + x, :], (2 - s["k_slot"]) * 1024), start=True, stop=True)
                    return m
                t = P(go, s["t_k", b], s["t_q", b], f)
                s_prev["q"] = [t, s["t_qg", 0], s.get(("t_qg", 1))]
                ts = []
                for x in range(2):
                    i = b * 8 + half * 4 + c0 + x
                    dn, d, df = D.take()
                    td = V(lambda e, x=x, d=d: e.tensor_tensor_scan(
                        d[:, 1:129], abc.slots[an][:, (c0 + x) * 128:(c0 + x + 1) * 128], ident, 0.0,
                        ALU.mult, ALU.add), ta, df, t_i)
                    tx = V(lambda e, x=x, d=d, i=i: e.scalar_tensor_tensor(
                        out=pair(X[:, b * 4 + c0 + x, :], s["p_slot"] * 1024),
                        in0=kb[:, x * 256:x * 256 + 256].rearrange("p (a t) -> p a t", a=2),
                        scalar=coef[:, i, 1, h:h + 1], in1=pair(d[:, 0:128], 1), op0=ALU.mult, op1=ALU.mult),
                        t, td, s["xpf"], s_prev.get("inv"))
                    D.hold(dn, tx)
                    s["t_xp"][b, c0 + x] = tx
                    ts.append(tx)
                bk.hold(bn, ts)
                if c0 == 2:
                    abc.hold(an, td)
            return steps

        def head_part(u):
            if u >= 2 * H:
                return []
            h, half = divmod(u, 2)
            (k0, fk), (v0, fv), (q0, fq) = (conv(u, i, p, 0) for i, p in ((1, "Wk"), (2, "Wv"), (0, "Wq")))
            k1, fk1 = conv(u, 1, "Wk", 1)

            def with_(a, b):
                return lambda: (a(), b())
            extra = (lambda: load("Wg", h), lambda: cut("Wg", h)) if half == 0 else (lambda: None, lambda: None)
            steps = [with_(lambda: begin(u), with_(decays(u, 0), k0[0])), k0[1], v0[0], with_(fk, v0[1]), with_(extra[0], q0[0]), with_(fv, with_(extra[1], q0[1])),
                    with_(decays(u, 1), k1[0]), with_(fq, k1[1])]
            return list(zip(AT["head"], steps)), fk1

        def rest_part(u, fk1):
            h, half = divmod(u, 2)
            (v1, fv1), (q1, fq1) = (conv(u, i, p, 1) for i, p in ((2, "Wv"), (0, "Wq")))
            nop = lambda: None
            o = half == 1
            ld = lambda p: (lambda: load(p, h + 1)) if o else nop
            ct = lambda p: (lambda: cut(p, h + 1)) if o else nop

            def seq(*fs):
                def go():
                    for f in fs:
                        f()
                return go

            def free(p):
                return (lambda: wh.hold(W[p, h % 2][0], unit[u]["t_proj", p, 1])) if o else nop
            return list(zip(AT["rest"], [
                seq(ld("Wk"), q1[0]), seq(free("Wk"), fk1, q1[1]), seq(free("Wq"), ld("Wq"), scores(u, 0, 0)), ct("Wk"),
                seq(fq1, scores(u, 0, 2)), scores(u, 1, 0), scores(u, 1, 2),
                seq(ct("Wq"), ld("Wv"), v1[0]), seq(v1[1], free("Wv")), turn_kv(u, 0, 0), seq(fv1, turn_kv(u, 0, 2)),
                ct("Wv"), turn_kv(u, 1, 0), turn_kv(u, 1, 2)]))

        def inverse(u):
            L = {}

            def s0():
                s = unit[u]
                tx = L["tx"] = list(s["t_xp"].values())
                prev = L["prev"] = s_prev.get("inv")
                t = []
                for q in range(4):
                    qs = slice(32 * q, 32 * q + 32)
                    t.append(A(lambda e, qs=qs: e.copy(XD[qs, 0:8, :], X[qs, :, qs]), tx, prev, t_i))
                tm = V(lambda e: e.tensor_tensor(XM, XD[:, :, :], cst[:, C_M16:C_M16 + 32].unsqueeze(1)
                                                 .to_broadcast([128, 16, 32]), ALU.mult), t, prev)
                L["to"] = G(lambda e: e.tensor_tensor(XO[:, :, :], XD[:, 0:8, :], cst[:, C_OFF:C_OFF + 32].unsqueeze(1)
                                                      .to_broadcast([128, 8, 32]), ALU.mult), t, prev)
                t = V(lambda e: e.transpose(YY, XM.rearrange("p m (s t) -> p t s m", s=2)), tm, prev)
                L["ta"] = V(lambda e: e.tensor_tensor(A16[:, :, :], YY[:, :, 0:16], YY[:, :, 16:32], ALU.add), t)
                tt = G(lambda e: e.memset(T16[:, :, :], 0.0), prev)
                L["tt"] = G(lambda e: e.memset(T16[:, :, :].rearrange("p a b -> p (a b)")[:, 0:256:17], 1.0), tt)

            def rows(l0, l1):
                def go():
                    tt = L["tt"]
                    for l in range(l0, l1):
                        n = 15 - l
                        pr = PR[:, 0:n * (l + 1)].rearrange("p (a b) -> p a b", a=n)
                        tp = V(lambda e, l=l, n=n, pr=pr: e.tensor_tensor(
                            pr, A16[:, l + 1:16, l:l + 1].to_broadcast([128, n, l + 1]),
                            T16[:, l:l + 1, 0:l + 1].to_broadcast([128, n, l + 1]), ALU.mult), L["ta"], tt)
                        tt = V(lambda e, l=l, pr=pr: e.tensor_tensor(T16[:, l + 1:16, 0:l + 1],
                                                                     T16[:, l + 1:16, 0:l + 1], pr, ALU.add), tp)
                    L["tt"] = tt
                return go

            def s2():
                te = []
                for f in range(2):
                    fl = cst[:, C_FLAG + f:C_FLAG + f + 1]
                    te.append(A(lambda e, f=f, fl=fl: e.activation(E1[:, 0, :, f, :], T16[:, :, :], ACT.Copy, scale=fl),
                                L["tt"], L["prev"]))
                    te.append(A(lambda e, f=f, fl=fl: e.activation(
                        E1[:, 1, :, f, :], T16[:, :, :].rearrange("p t j -> p j t"), ACT.Copy, scale=fl), L["tt"], L["prev"]))
                L["tn"] = [V(lambda e, w=w: e.transpose(MN[:, w, :, :].rearrange("p m (s t) -> p t s m", s=2),
                                                        E1[:, w, :, :, :].rearrange("p a s b -> p a (s b)")),
                             te, L["prev"]) for w in range(2)]

            def s3():
                zb = [bk.take() for _ in range(4)]
                L["tz"] = []
                for q in range(4):
                    qs = slice(32 * q, 32 * q + 32)
                    bn, kb, f = zb[q]

                    def go(e, qs=qs, kb=kb):
                        for m in range(8):
                            r = e.matmul(kb[qs, m * 32:m * 32 + 32], XO[qs, m, :], MN[qs, 1, m, :], start=True, stop=True)
                        return r
                    t = P(go, L["to"], L["tn"], f)
                    L["tz"].append(A(lambda e, qs=qs, kb=kb: e.copy(
                        ZS[qs, :, :], kb[qs, 0:256].rearrange("p (m t) -> p m t", m=8)), t, L["prev"]))
                    bk.hold(bn, L["tz"][-1])

            def s4():
                s = unit[u]
                mf = s["mf"]
                zb = [bk.take() for _ in range(4)]
                tmn = []
                for q in range(4):
                    qs = slice(32 * q, 32 * q + 32)
                    bn, kb, f = zb[q]

                    def go(e, qs=qs, kb=kb):
                        for m in range(8):
                            e.matmul(kb[qs, m * 32:m * 32 + 32], ZS[qs, m, :], MN[qs, 0, m, :], start=True, stop=True)
                            r = e.matmul(kb[qs, 256 + m * 32:288 + m * 32], MN[qs, 0, m, :], ZS[qs, m, :],
                                         start=True, stop=True)
                        return r
                    t = P(go, L["tz"][q], f)
                    tmn.append(V(lambda e, qs=qs, kb=kb: e.tensor_tensor(
                        MN[qs, :, 0:8, :], MN[qs, :, 0:8, :], kb[qs, :].rearrange("p (a m t) -> p a m t", a=2, m=8),
                        ALU.add), t))
                    bk.hold(bn, tmn[-1])
                L["tmn"] = tmn
                L["tmf"] = []
                for q in range(4):
                    qs = slice(32 * q, 32 * q + 32)
                    L["tmf"].append(A(lambda e, qs=qs: e.copy(mf[qs, :, qs], MN[qs, 0, 0:8, :]), tmn[q], s["mff"], t_i))
                for q in range(2):
                    qs = slice(32 * q, 32 * q + 32)
                    L["tmf"].append(A(lambda e, qs=qs: e.copy(NF[qs, :, qs], MN[qs, 1, 0:8, :]), tmn[q], L["prev"], t_i))

            def s5():
                zb = [bk.take() for _ in range(2)]
                L["tz"] = []
                for p in range(2):
                    ra, rb = slice(64 * p, 64 * p + 32), slice(64 * p + 32, 64 * p + 64)
                    bn, kb, f = zb[p]

                    def go(e, ra=ra, rb=rb, kb=kb):
                        for m in range(8):
                            r = e.matmul(kb[rb, m * 32:m * 32 + 32], X[ra, m, rb], MN[ra, 1, m, :], start=True, stop=True)
                        return r
                    t = P(go, L["tmn"], f, L["tx"])
                    L["tz"].append(A(lambda e, rb=rb, kb=kb: e.activation(
                        ZT[rb, :, :], kb[rb, 0:256].rearrange("p (m t) -> p m t", m=8), ACT.Copy, scale=-1.0), t, L["prev"]))
                    bk.hold(bn, L["tz"][-1])

            def s6():
                s = unit[u]
                mf = s["mf"]
                zb = [bk.take() for _ in range(2)]
                for p in range(2):
                    ra, rb = slice(64 * p, 64 * p + 32), slice(64 * p + 32, 64 * p + 64)
                    bn, kb, f = zb[p]

                    def go(e, ra=ra, rb=rb, kb=kb, p=p):
                        for m in range(8):
                            r = e.matmul(kb[ra, m * 32:m * 32 + 32], ZT[rb, m, :], MN[rb, 0, m, :], start=True, stop=True)
                            if p == 0:
                                r = e.matmul(kb[rb, 256 + m * 32:288 + m * 32], MN[rb, 0, m, :], ZT[rb, m, :],
                                             start=True, stop=True)
                        return r
                    t = P(go, L["tz"][p], f)
                    ts = [V(lambda e, ra=ra, rb=rb, kb=kb: e.tensor_copy(
                        mf[ra, :, rb], kb[ra, 0:256].rearrange("p (m t) -> p m t", m=8)), t, s["mff"])]
                    if p == 0:
                        ts.append(V(lambda e, kb=kb: e.tensor_copy(
                            NF[32:64, :, 0:32], kb[32:64, 256:512].rearrange("p (m t) -> p m t", m=8)), t, L["tmf"]))
                    L["tmf"] += ts
                    bk.hold(bn, ts)

            def s7():
                bn, kb, f = bk.take()

                def go(e, kb=kb):
                    for m in range(8):
                        r = e.matmul(kb[64:128, m * 64:m * 64 + 64], X[0:64, m, 64:128], NF[0:64, m, :],
                                     start=True, stop=True)
                    return r
                t = P(go, L["tmf"], f)
                L["tz"] = A(lambda e, kb=kb: e.activation(
                    Z2[64:128, :, :], kb[64:128, :].rearrange("p (m t) -> p m t", m=8), ACT.Copy, scale=-1.0), t, L["prev"])
                bk.hold(bn, L["tz"])

            def s8():
                s = unit[u]
                mf = s["mf"]
                bn, kb, f = bk.take()

                def go(e, kb=kb):
                    for m in range(8):
                        r = e.matmul(kb[0:64, m * 64:m * 64 + 64], Z2[64:128, m, :], mf[64:128, m, 64:128],
                                     start=True, stop=True)
                    return r
                t = P(go, L["tz"], L["tmf"], f)
                tl = V(lambda e, kb=kb: e.tensor_copy(mf[0:64, :, 64:128],
                                                      kb[0:64, :].rearrange("p (m t) -> p m t", m=8)), t)
                bk.hold(bn, tl)
                s["t_mf"] = [tl, L["tmf"]]
                s_prev["inv"] = [t, tl, L["tmf"], L["tn"], L["tmn"]]
            return list(zip(AT["inv"], [s0] + [rows(l, min(l + 2, 15)) for l in range(0, 15, 2)] + [s2, s3, s4, s5, s6, s7, s8]))

        def chain(u):
            h, half = divmod(u, 2)
            steps = []
            L = {}

            def start():
                osn, L["os"], osf = OS.take()
                L["osn"], L["osf"], L["to"] = osn, osf, []
                unit[u]["os"] = L
            for ch in range(4):
                first = half == 0 and ch == 0

                def p1(ch=ch, first=first):
                    s = unit[u]
                    kq, vc = s["kq"], s["vc"]
                    if ch == 0:
                        start()
                    if first:
                        L["tr"] = [s["t_vc"][0, ch], s["t_vc"][1, ch]]
                        L["rhs"] = lambda b: vc[:, b, 0, :]
                        return

                    def go(e):
                        for b in range(2):
                            r = e.matmul(bank[4][:, b * 128:b * 128 + 128], kq[:, b, ch, :], ST[:, b, :],
                                         start=True, stop=True)
                        return r
                    t = P(go, st["S"], fb[4])
                    L["rn"], r_, rf = R.take()
                    tr = []
                    for b in range(2):
                        i = b * 8 + half * 4 + ch
                        tr.append(V(lambda e, b=b, i=i: e.scalar_tensor_tensor(
                            out=r_[:, b, :], in0=bank[4][:, b * 128:b * 128 + 128], scalar=coef[:, i, 0, h:h + 1],
                            in1=vc[:, b, ch, :], op0=ALU.mult, op1=ALU.add), t, rf, s["t_vc"][b, ch]))
                    fb[4] = tr
                    L["tr"] = tr
                    L["rhs"] = lambda b: r_[:, b, :]

                def p2(ch=ch, first=first):
                    s = unit[u]
                    mf, qg = s["mf"], s["qg"]
                    rhs = L["rhs"]

                    def go(e):
                        for b in range(2):
                            r = e.matmul(bank[4][:, b * 128:b * 128 + 128], mf[:, b * 4 + ch, :], rhs(b), start=True, stop=True)
                        return r
                    tw = P(go, L["tr"], s["t_mf"], fb[4])
                    if not first:
                        R.hold(L["rn"], tw)
                    L["wn"], ws, wf = WS.take()
                    L["ws"] = ws
                    L["tws"] = A(lambda e: e.copy(ws[:, :, :], bank[4][:, 0:256].rearrange("p (b t) -> p b t", b=2)), tw, wf)
                    fb[4] = [L["tws"]]

                def p3(ch=ch, first=first):
                    s = unit[u]
                    kd, xp, qg = s["kd"], s["xp"], s["qg"]
                    ws = L["ws"]

                    def go(e):
                        for b in range(2):
                            r = e.matmul(bank[4][:, b * 128:b * 128 + 128], kd[:, b, ch, :], ws[:, b, :], start=True, stop=True)
                        return r
                    tds = P(go, L["tws"], fb[4])

                    def go(e):
                        for b in range(2):
                            o = bank[7][:, b * 128:b * 128 + 128]
                            if not first:
                                e.matmul(o, qg[:, b, ch, :], ST[:, b, :], start=True, stop=False)
                            r = e.matmul(o, xp[:, b * 4 + ch, :], ws[:, b, :], start=first, stop=True)
                        return r
                    tp = P(go, fb[7], s["t_qg", 0], s["t_qg", 1])
                    WS.hold(L["wn"], tp)
                    ts = []
                    for b in range(2):
                        i = b * 8 + half * 4 + ch
                        if first:
                            ts.append(V(lambda e, b=b: e.tensor_copy(ST[:, b, :], bank[4][:, b * 128:b * 128 + 128]),
                                        tds, st["S"], tp))
                        else:
                            ts.append(V(lambda e, b=b, i=i: e.scalar_tensor_tensor(
                                out=ST[:, b, :], in0=ST[:, b, :], scalar=GC[:, h, i:i + 1],
                                in1=bank[4][:, b * 128:b * 128 + 128], op0=ALU.mult, op1=ALU.add), tds, tp))
                    fb[4] = ts
                    st["S"] = ts + [tp]
                    os_ = L["os"]
                    toc = A(lambda e: e.copy(os_[:, :, ch, :], bank[7][:, 0:256].rearrange("p (b t) -> p b t", b=2)),
                            tp, L["osf"])
                    fb[7] = [toc]
                    L["to"].append(toc)
                    if ch == 3:
                        for r, k in ((KQ, "kqn"), (QG, "qgn"), (KD, "kdn"), (VC, "vcn"), (XP, "xpn"), (MF, "mfn")):
                            r.hold(s[k], tp, ts)
                steps += [p1, p2, p3]
            return list(zip(AT["chain"], steps))

        def tail(u):
            h, half = divmod(u, 2)
            L = {}

            def sums():
                o = unit[u]["os"]
                os_ = o["os"]
                tq = s_prev.get("sq")
                ts = []
                for b in range(2):
                    for ch in range(4):
                        tq = A(lambda e, b=b, ch=ch: e.activation(sq[:, :], os_[:, b, ch, :], ACT.Square,
                                                                  accum_out=ss[:, 0, b * 4 + ch:b * 4 + ch + 1]),
                               o["to"], tq, s_prev.get("ss"))
                        ts.append(tq)
                s_prev["sq"] = tq
                v, y, a = ss[:, 0, :], ss[:, 2, :], ss[:, 1, :]
                t = V(lambda e: e.tensor_scalar(v, v, 1.0 / 128, EPS, ALU.mult, ALU.add), ts)
                t = V(lambda e: e.tensor_scalar(a.bitcast(I32), v.bitcast(I32), 1, None, ALU.logical_shift_right), t)
                t = V(lambda e: e.tensor_scalar(y.bitcast(I32), a.bitcast(I32), -1.0, float(0x5F3759DF), ALU.mult, ALU.add), t)
                for _ in range(4):
                    t = G(lambda e: e.tensor_tensor(a, y, y, ALU.mult), t)
                    t = G(lambda e: e.tensor_tensor(a, a, v, ALU.mult), t)
                    t = G(lambda e: e.tensor_scalar(a, a, -0.5, 1.5, ALU.mult, ALU.add), t)
                    t = G(lambda e: e.tensor_tensor(y, y, a, ALU.mult), t)
                L["tr"] = t

            def gate(b):
                def first():
                    L["got"], L["steps"] = project(W["Wg", h % 2], 2 * b + half)
                    L["steps"][0]()

                def second():
                    L["steps"][1]()
                    kb, t = L["got"]["kb"], L["got"]["t"]
                    gn, g, gf = gg.take()
                    L["g", b] = (gn, g, A(lambda e: e.activation(g[:, :], kb[:, :], ACT.Tanh, scale=0.5), t, gf))
                    pbk.hold(L["got"]["b"], L["g", b][2])
                    if half == 1 and b == 1:
                        wh.hold(W["Wg", h % 2][0], t)
                return [first, second]

            def scaled(b):
                def go_():
                    os_ = unit[u]["os"]["os"]
                    L["ts", b] = [V(lambda e, ch=ch: e.tensor_scalar(os_[:, b, ch, :], os_[:, b, ch, :],
                                                                     ss[:, 2, b * 4 + ch:b * 4 + ch + 1], None, ALU.mult),
                                    L["tr"]) for ch in range(4)]
                return go_

            def turn(b):
                def go_():
                    o = unit[u]["os"]
                    os_ = o["os"]
                    gn, g, tg = L["g", b]
                    bn, kb, f = bk.take()

                    def go(e):
                        for ch in range(4):
                            m = e.transpose(kb[:, ch * 128:ch * 128 + 128], os_[:, b, ch, :], ident)
                        return m
                    t = P(go, L["ts", b], f)
                    rn, r_, rf = rs.take()
                    t2 = A(lambda e: e.activation(r_[:, :], kb[:, :], ACT.Identity, scale=lnw[:, 0:1], bias=lnw[:, 1:2]),
                           t, rf, t_ln)
                    bk.hold(bn, t2)
                    t3 = V(lambda e: e.scalar_tensor_tensor(out=g[:, :], in0=g[:, :], scalar=1.0, in1=r_[:, :],
                                                            op0=ALU.add, op1=ALU.mult), t2, tg)
                    rs.hold(rn, t3)
                    a = b * 1024 + half * 512
                    gg.hold(gn, Q.dma("gpsimd", f"og{gn}", scratch["og"][h * 128:(h + 1) * 128, a:a + 512], g[:, :], t3))
                    if b == 1:
                        OS.hold(o["osn"], t)
                        s_prev["ss"] = L["ts", 1]
                return go_
            return list(zip(AT["tail"], [sums] + gate(0) + gate(1) + [scaled(0), turn(0), scaled(1), turn(1)]))

        NU = 2 * H
        AT = {"chain": (0.01, 2.78, 4.44, 7.1, 10.03, 11.73, 12.97, 18.12, 18.76, 23.77, 29.46, 30.57),
              "rest": (2.09, 2.36, 6.1, 7.63, 8.34, 9.63, 12.38, 14.31, 21.62, 26.63, 26.75, 26.92, 36.69, 66.83),
              "inv": (14.74, 15.34, 19.72, 19.8, 22.1, 24.1, 26.96, 27.85, 28.62, 31.12, 36.04, 37.3, 38.25, 40.76, 45.35, 57.41),
              "tail": (30.87, 21.65, 29.03, 32.75, 32.76, 34.04, 37.78, 42.7, 56.14),
              "head": (30.88, 32.78, 33.41, 35.84, 36.51, 37.42, 39.37, 43.06)}
        for p in ("Wk", "Wq", "Wv"):
            load(p, 0)
            cut(p, 0)
        steps, fk1 = head_part(0)
        merged(steps)
        for u in range(NU):
            rest = rest_part(u, fk1)
            steps = []
            if u + 1 < NU:
                steps, fk1 = head_part(u + 1)
            merged(chain(u - 1) if u else [], rest, inverse(u), tail(u - 1) if u else [], steps)
        merged(chain(NU - 1), tail(NU - 1))
        return Q.everything()



def mix0(nc, Q, sb, io, scratch, bank, split, cst, eps, YH, YL, done):
    V = lambda fn, *a: Q.op("vector", fn, *a)
    A = lambda fn, *a: Q.op("scalar", fn, *a)
    P = lambda fn, *a: Q.op("tensor", fn, *a)
    with ExitStack() as c:
        def ring(name, n, shape, dt=F32):
            r = Ring([sb(c, f"{name}{i}", shape, dt) for i in range(n)])
            for i in range(n):
                r.hold(i, done)
            return r
        WOH = sb(c, "WOH", [128, 16, 512], F32R)
        WOL = sb(c, "WOL", [128, 16, 512], F32R)
        raw = ring("mr", 3, [128, 512])
        og = ring("mo", 4, [128, 512])
        oh = ring("moh", 3, [128, 512], F32R)
        ol = ring("mol", 3, [128, 512], F32R)
        g0 = ring("mg", 2, [128, 4, 512])
        xT = ring("mx", 2, [128, 4, 512])
        xr = ring("mxr", 3, [128, 512])
        xn = ring("mxn", 2, [128, 512])
        nst = sb(c, "nst", [128, 16, 6])
        nmv = sb(c, "nmv", [128, 16, 2])
        nsd = sb(c, "nsd", [128, 16])
        nrs = sb(c, "nrs", [128, 16])
        abk, bk = Ring(bank[0:6]), Ring(bank[6:8])
        for i in range(6):
            abk.hold(i, done)
        for i in range(2):
            bk.hold(i, done)
        tw = []
        pend = []

        ready, normed = [], []

        def prepare(i):
            n, k = divmod(i, 16)
            if n == 0:
                m, r, f = raw.take()
                t = Q.dma("sync", f"mr{m}", r[:, :], io["Wo"][k * 128:(k + 1) * 128, :], f)
                ts = split(r[:, :], WOH[:, k, :], WOL[:, k, :], t, done)
                raw.hold(m, ts)
                tw.append(ts)
            m, o, f = og.take()
            t = Q.dma("sync", f"mo{m}", o[:, :], scratch["og"][k * 128:(k + 1) * 128, n * 512:n * 512 + 512], f)
            mh, h, fh = oh.take()
            ml, l, fl = ol.take()
            ts = split(o[:, :], h[:, :], l[:, :], t, [fh, fl], low_eng="gpsimd")
            og.hold(m, ts)
            ready.append((mh, h, ml, l, ts))

        def rows(q0, n, x1, tx1, nx):
            qs = (q0,)
            for q in qs:
                i = n * 4 + q
                b, kb, f = bk.take()

                def go(e, q=q, kb=kb):
                    for k in range(4):
                        m = e.transpose(kb[:, k * 128:(k + 1) * 128], x1[:, k, q * 128:(q + 1) * 128], cst[:, 0:128])
                    return m
                t = P(go, tx1, f)
                m, r, f = xr.take()
                tl = t
                t2 = A(lambda e, kb=kb, r=r: e.copy(r[:, :], kb[:, :]), t, f)
                bk.hold(b, t2)
                td = Q.dma("scalar", f"mxr{m}", scratch["x1"][i * 128:(i + 1) * 128, :], r[:, :], t2)
                t = V(lambda e, r=r, i=i: e.bn_stats(nst[:, i, :], r[:, :]), t2)
                t = V(lambda e, i=i: e.bn_aggr(nmv[:, i, :], nst[:, i, :]), t)
                t = A(lambda e, i=i: e.activation(nsd[:, i:i + 1], nmv[:, i, 1:2], ACT.Sqrt, bias=eps[:, 0:1]), t)
                t = V(lambda e, i=i: e.reciprocal(nrs[:, i:i + 1], nsd[:, i:i + 1]), t)
                mn, xq, f = xn.take()
                t = V(lambda e, r=r, i=i, xq=xq: e.tensor_scalar(xq[:, :], r[:, :], nmv[:, i, 0:1], nrs[:, i:i + 1],
                                                                 ALU.subtract, ALU.mult), t, f)
                xr.hold(m, td, t)
                normed.append((i, mn, xq, t))
            if qs[-1] == 3:
                xT.hold(nx, tl)
                pend.pop(0)

        def turn():
            if normed:
                i, mn, xq, t = normed.pop(0)
                b, kb, f = bk.take()

                def go(e, kb=kb, xq=xq):
                    for k in range(4):
                        m = e.transpose(kb[:, k * 128:(k + 1) * 128],
                                        xq[:, 256 * (k // 2) + k % 2:256 * (k // 2) + 256:2], cst[:, 0:128])
                    return m
                tp = P(go, t, f)
                xn.hold(mn, tp)
                bk.hold(b, split(kb[:, :].rearrange("p (k t) -> p k t", k=4), YH[:, :, i * 128:(i + 1) * 128],
                                 YL[:, :, i * 128:(i + 1) * 128], tp))

        prepare(0)
        prepare(1)
        for n in range(4):
            sl = slice(n * 512, n * 512 + 512)
            ng, g, f = g0.take()
            tg = Q.dma("scalar", f"mg{ng}", g[:, :, :], scratch["g0"].rearrange("(k p) t -> p k t", p=128)[:, :, sl], f)
            nx, x, f = xT.take()
            tx = Q.dma("scalar", f"mx{nx}", x[:, :, :], io["xT"].rearrange("(k p) t -> p k t", p=128)[:, :, sl], f)
            bks = [abk.take() for _ in range(4)]
            for k in range(16):
                if n * 16 + k < 62:
                    prepare(n * 16 + k + 2)
                mh, h, ml, l, ts = ready.pop(0)
                for j in range(4):
                    tp = P(lambda e, j=j, k=k, h=h, l=l, kb=bks[j][1]: mm3(e, kb[:, :], [
                        (WOH[:, k, j * 128:(j + 1) * 128], WOL[:, k, j * 128:(j + 1) * 128], h[:, :], l[:, :])],
                        first=k == 0, last=k == 15), ts, tw[k], bks[j][2])
                oh.hold(mh, tp)
                ol.hold(ml, tp)
                if k in (3, 6, 9, 12) and pend:
                    rows(k // 3 - 1, *pend[0])
                if k in (5, 8, 11, 14):
                    turn()
            tv = []
            for j in range(4):
                t = V(lambda e, j=j, kb=bks[j][1], g=g: e.tensor_tensor(g[:, j, :], g[:, j, :], kb[:, :], ALU.mult), tp, tg)
                abk.hold(bks[j][0], t)
                tv.append(V(lambda e, j=j, g=g, x=x: e.tensor_tensor(x[:, j, :], x[:, j, :], g[:, j, :], ALU.add), t, tx))
            g0.hold(ng, tv)
            pend.append((n, x, tv, nx))
        for q in range(4):
            rows(q, *pend[0])
            if q:
                turn()
        turn()
        return Q.everything()


def attn1(nc, Q, sb, c, io, scratch, bk, split, XH, XL, done):
    V = lambda fn, *a: Q.op("vector", fn, *a)
    A = lambda fn, *a: Q.op("scalar", fn, *a)
    P = lambda fn, *a: Q.op("tensor", fn, *a)
    G = lambda fn, *a: Q.op("gpsimd", fn, *a)
    v = sb(c, "l1v", [128, 4, 3])
    t_v = Q.dma("sync", "l1v", v[:, :, :], io["l1v"], done)
    sp = sb(c, "sp", [128, 8, 4])
    quarter = sb(c, "quarter", [128, 1])
    t_q = V(lambda e: e.memset(quarter[:, :], 0.25), done)
    row = lambda i: sp[:, i, :]
    p = v[:, :, 2]
    t = A(lambda e: e.activation(row(0), p, ACT.Abs), t_v)
    t = A(lambda e: e.activation(row(1), row(0), ACT.Exp, scale=-1.0), t)
    t = V(lambda e: e.tensor_scalar(row(2), row(1), 2.0, None, ALU.add), t)
    t = V(lambda e: e.reciprocal(row(3), row(2)), t)
    t = V(lambda e: e.tensor_tensor(row(2), row(1), row(3), ALU.mult), t)
    t = V(lambda e: e.tensor_tensor(row(4), row(2), row(2), ALU.mult), t)
    t = V(lambda e: e.tensor_scalar(row(5), row(4), 2.0 / 17, 2.0 / 15, ALU.mult, ALU.add), t)
    for k in (13, 11, 9, 7, 5, 3, 1):
        t = V(lambda e: e.tensor_tensor(row(5), row(5), row(4), ALU.mult), t)
        t = V(lambda e, k=k: e.tensor_scalar(row(5), row(5), 2.0 / k, None, ALU.add), t)
    t = V(lambda e: e.tensor_tensor(row(5), row(5), row(2), ALU.mult), t)
    t = V(lambda e: e.tensor_scalar(row(6), p, 0.0, None, ALU.max), t)
    t = V(lambda e: e.tensor_tensor(row(6), row(6), row(5), ALU.add), t)
    t1 = V(lambda e: e.tensor_scalar(row(5), row(6), -4.0, None, ALU.mult), t)
    t_sp = V(lambda e: e.tensor_scalar(row(7), row(6), -8.0, None, ALU.mult), t1)
    t_h = V(lambda e: e.tensor_scalar(v[:, :, 0:2], v[:, :, 0:2], 0.5, None, ALU.mult), t_v)
    wr = sb(c, "l1wr", [128, 2, 2, 128])
    wh = sb(c, "l1wh", [128, 2, 2, 128], F32R)
    wl = sb(c, "l1wl", [128, 2, 2, 128], F32R)
    X, Y, M = (sb(c, n, [128, 1024]) for n in ("l1x", "l1y", "l1m"))
    S = {"wr": [done], "w": [done], "x": [done], "ym": [done], "out": []}

    def weights(m):
        def go():
            t = [Q.dma("sync", "l1w", wr[:, g, :, :], io[n][m], S["wr"]) for g, n in enumerate(("ig_w", "ag_w"))]
            S["tw"] = split(wr[:, :, :, :], wh[:, :, :, :], wl[:, :, :, :], t, S["w"], low_eng="gpsimd")
            S["wr"] = S["tw"]
        return go

    def gates(m, b, n):
        def go():
            sl = slice(b * 1024 + n * 512, b * 1024 + n * 512 + 512)
            to = slice(n * 512, n * 512 + 512)
            q = m // 2
            if n == 0:
                S["tg"] = []
            for g, D, free in ((0, X, S["x"]), (1, Y, S["ym"])):
                bn, kb, f = bk.take()
                t = P(lambda e, g=g, kb=kb: mm3(e, kb[:, :], [
                    (wh[:, g, r, :], wl[:, g, r, :], XH[:, 2 * q + r, sl], XL[:, 2 * q + r, sl]) for r in range(2)]),
                    S["tw"], f)
                S["tg"].append(A(lambda e, g=g, kb=kb, D=D: e.activation(D[:, to], kb[:, :], ACT.Tanh, scale=0.5,
                                                                         bias=v[:, m, g:g + 1]), t, free, t_h))
                bk.hold(bn, S["tg"][-1])
            S["w"] = t
        return go

    def decays(m, b):
        def go():
            t = A(lambda e: e.activation(M[:, :], Y[:, :], ACT.Exp, scale=sp[:, 7, m:m + 1], bias=sp[:, 7, m:m + 1]),
                  S["tg"], t_sp, S["ym"])
            S["ty"] = A(lambda e: e.activation(Y[:, :], Y[:, :], ACT.Exp, scale=sp[:, 5, m:m + 1], bias=sp[:, 5, m:m + 1]), t)
            t = A(lambda e: e.activation(M[:, :], M[:, :], ACT.Sqrt, bias=quarter[:, 0:1], scale=-0.25), t, t_q)
            S["tm"] = V(lambda e: e.memset(M[:, 0:1], 0.5), t)
        return go

    def enter(m, b):
        def go():
            sl = slice(b * 1024, b * 1024 + 1024)
            t = V(lambda e: e.scalar_tensor_tensor(out=X[:, :], in0=X[:, :], scalar=1.0, in1=M[:, :],
                                                   op0=ALU.add, op1=ALU.mult), S["tg"], S["tm"])
            tm = G(lambda e: e.tensor_tensor(M[:, :], f32(XH[:, m, sl]), f32(XL[:, m, sl]), ALU.add), t)
            S["tx"] = G(lambda e: e.tensor_tensor(X[:, :], X[:, :], M[:, :], ALU.mult), t, tm)
        return go

    def scan(m, b):
        def go():
            sl = slice(b * 1024, b * 1024 + 1024)
            tx = S["tx"]
            t = V(lambda e: e.tensor_tensor_scan(X[:, :], Y[:, :], X[:, :], 0.0, ALU.mult, ALU.add), tx, S["ty"])
            S["ym"] = [t, tx]
            r = 256 * (m // 2) + m % 2
            S["x"] = [Q.dma("sync", "s1", scratch["s1"][r:r + 255:2, sl], X[:, :], t)]
            S["out"] = S["x"]
        return go
    steps = []
    for m in range(4):
        for b in range(2):
            steps.append([gates(m, b, 0), gates(m, b, 1), decays(m, b), weights(m + 1) if b == 1 and m < 3 else None,
                          enter(m, b), None, scan(m, b), None])
    weights(0)()
    return S, steps


def ffn1(nc, Q, sb, io, scratch, bank, split, XH, XL, at, cst, out, done):
    V = lambda fn, *a: Q.op("vector", fn, *a)
    A = lambda fn, *a: Q.op("scalar", fn, *a)
    P = lambda fn, *a: Q.op("tensor", fn, *a)
    G = lambda fn, *a: Q.op("gpsimd", fn, *a)
    with ExitStack() as c:
        def ring(name, n, shape, dt=F32):
            r = Ring([sb(c, f"{name}{i}", shape, dt) for i in range(n)])
            for i in range(n):
                r.hold(i, done)
            return r
        pk = ring("pk", 2, [128, 512], I32)
        sc = ring("sc", 2, [128, 512])
        w1 = ring("w1", 1, [128, 512], I32)
        w2 = ring("w2", 1, [128, 512], I32)
        wf = ring("wf", 1, [128, 2, 512])
        wh = Slots([sb(c, f"qh{i}", [128, 2, 512], F32R) for i in range(4)], done)
        wl = [sb(c, f"ql{i}", [128, 2, 512], F32R) for i in range(4)]
        HH = sb(c, "QHH", [128, 2, T], F32R)
        HL = sb(c, "QHL", [128, 2, T], F32R)
        ACC = sb(c, "QACC", [128, 4, T])
        g2 = ring("g2", 2, [128, 512])
        hd = ring("qhd", 2, [128, 512])
        bk = Ring(bank)
        for i in range(8):
            bk.hold(i, done)

        def fetch(pk_src, sc_src):
            n, r, f = pk.take()
            tp = [Q.dma("sync", f"pk{n}", r[:, a:b], s, f) for a, b, s in pk_src]
            m, s_, f = sc.take()
            ts = [Q.dma("sync", f"sc{m}", s_[p0:p0 + 128, a:b], s, f) for p0, a, b, s in sc_src]
            return n, r, tp, m, s_, ts

        def weight(n, r, tp, m, s_, ts, low_eng="gpsimd"):
            i1, a, f1 = w1.take()
            i2, b, f2 = w2.take()
            t = V(lambda e: e.tensor_scalar(a[:, :], r[:, :], 255, None, ALU.bitwise_and), tp, f1)
            pk.hold(n, t)
            t = V(lambda e: e.tensor_scalar(b[:, :], a[:, :], 12, None, ALU.logical_shift_left), t, f2)
            t = V(lambda e: e.tensor_tensor(a[:, :], a[:, :], b[:, :], ALU.bitwise_or), t)
            t = V(lambda e: e.tensor_scalar(b[:, :], a[:, :], 9, 0x0E000E00, ALU.logical_shift_left, ALU.bitwise_and), t)
            t = V(lambda e: e.tensor_scalar(a[:, :], a[:, :], 12, -0x7FFF8000, ALU.logical_shift_left, ALU.bitwise_and), t)
            t = V(lambda e: e.tensor_tensor(a[:, :], a[:, :], b[:, :], ALU.bitwise_or), t)
            w1.hold(i1, t)
            w2.hold(i2, t)
            i3, w, f3 = wf.take()
            half = a[:, :].bitcast(F16).rearrange("p (n s) -> p n s", s=2)
            tw = [V(lambda e, s2=s2: e.scalar_tensor_tensor(out=w[:, s2, :], in0=half[:, :, s2], scalar=16384.0,
                                                            in1=s_[:, :], op0=ALU.mult, op1=ALU.mult), t, ts, f3)
                  for s2 in range(2)]
            w1.hold(i1, tw)
            sc.hold(m, tw)
            i4, h, f4 = wh.take()
            th = split(w[:, :, :], h[:, :, :], wl[i4][:, :, :], tw, f4, low_eng=low_eng)
            wf.hold(i3, th)
            return i4, h, wl[i4], th

        tH = [[done] for _ in range(4)]
        tA = {}

        def down(j, hs, wd, after=None):
            order = [(o, n) for o in range(4) for n in range(4)] if j < 15 else [(o, n) for n in range(4) for o in range(4)]
            for o, n in order:
                sl = slice(n * 512, n * 512 + 512)
                b, kb, f = bk.take()
                i4, w, wlo, tw = wd
                t = P(lambda e, kb=kb, o=o, sl=sl: mm3(e, kb[:, :], [
                    (w[:, s2, o * 128:(o + 1) * 128], wlo[:, s2, o * 128:(o + 1) * 128], HH[:, s2, sl], HL[:, s2, sl])
                    for s2 in range(2)]), tw, hs[n], f)
                if j == 0:
                    ta = A(lambda e, kb=kb, o=o, sl=sl: e.copy(ACC[:, o, sl], kb[:, :]), t)
                else:
                    ta = V(lambda e, kb=kb, o=o, sl=sl: e.tensor_tensor(ACC[:, o, sl], ACC[:, o, sl], kb[:, :],
                                                                        ALU.add), t, tA[(o, n)])
                tA[(o, n)] = ta
                bk.hold(b, ta)
                tH[n] = [t]
                if after and o == 3:
                    after(n)
            wh.hold(wd[0], t)

        def sources():
            def half(p, j):
                src, scs, cols = io[p + "_pk"], io[p + "_sc"], slice(j * 256, j * 256 + 256)
                return ([(q * 256, q * 256 + 256, src[q * 128:(q + 1) * 128, cols]) for q in range(2)],
                        [(0, q * 256, q * 256 + 256, scs[q * 8:q * 8 + 8, cols].unsqueeze(1).to_broadcast([8, 16, 256]))
                         for q in range(2)])
            for j in range(17):
                if j < 16:
                    yield half("gate", j)
                    yield half("up", j)
                if j:
                    i = j - 1
                    yield ([(0, 512, io["down_pk"][i * 128:(i + 1) * 128, :])],
                           [(0, 0, 512, io["down_scT"][i * 8:i * 8 + 8, :].unsqueeze(1).to_broadcast([8, 16, 512]))])

        source = sources()
        ahead = [fetch(*next(source))]

        def following(low_eng="gpsimd"):
            nxt = next(source, None)
            if nxt:
                ahead.append(fetch(*nxt))
            return weight(*ahead.pop(0), low_eng)

        gu = {0: [following(), following("vector")]}
        for j in range(16):
            wg, wu = gu.pop(j)
            gu[j + 1] = []
            hs = [[] for _ in range(4)]
            late = []
            for s2 in range(2):
                cs = [(q * 256 + s2 * 128, q * 256 + s2 * 128 + 128) for q in range(2)]
                for n in range(4):
                    sl = slice(n * 512, n * 512 + 512)

                    def mats(w):
                        return [(w[1][:, par, cs[q][0]:cs[q][1]], w[2][:, par, cs[q][0]:cs[q][1]],
                                 XH[:, 2 * q + par, sl], XL[:, 2 * q + par, sl]) for q in range(2) for par in range(2)]
                    b1, k1, f1 = bk.take()
                    t1 = P(lambda e, k1=k1, m=mats(wg): mm3(e, k1[:, :], m), wg[3], f1)
                    b2, k2, f2 = bk.take()
                    t2 = P(lambda e, k2=k2, m=mats(wu): mm3(e, k2[:, :], m), wu[3], f2)
                    m, s, f = g2.take()
                    t = A(lambda e, s=s, k1=k1: e.activation(s[:, :], k1[:, :], ACT.Square), t1, f)
                    t = V(lambda e, s=s, k1=k1: e.scalar_tensor_tensor(out=s[:, :], in0=s[:, :], scalar=1.0 / 0.044715,
                                                                       in1=k1[:, :], op0=ALU.add, op1=ALU.mult), t)
                    t = A(lambda e, s=s: e.activation(s[:, :], s[:, :], ACT.Tanh, scale=0.7978845608028654 * 0.044715), t)
                    t = V(lambda e, s=s, k1=k1: e.scalar_tensor_tensor(out=s[:, :], in0=s[:, :], scalar=1.0,
                                                                       in1=k1[:, :], op0=ALU.add, op1=ALU.mult), t)
                    bk.hold(b1, t)
                    m2, h, f = hd.take()
                    th = V(lambda e, h=h, s=s, k2=k2: e.scalar_tensor_tensor(out=h[:, :], in0=s[:, :], scalar=0.5,
                                                                             in1=k2[:, :], op0=ALU.mult, op1=ALU.mult), t, t2, f)
                    bk.hold(b2, th)
                    g2.hold(m, th)

                    def cut(s2=s2, n=n, sl=sl, h=h, m2=m2, th=th):
                        tt = split(h[:, :], HH[:, s2, sl], HL[:, s2, sl], th, tH[n], low_eng="gpsimd")
                        hd.hold(m2, tt)
                        hs[n] += tt
                    late.append(cut)
                    g = s2 * 4 + n
                    if j and g == 1:
                        down(j - 1, *prev)
                    if j == 0 or g:
                        while late:
                            late.pop(0)()
                    if g in (1, 4) and j < 15:
                        gu[j + 1].append(following())
                    if g == 2 and j == 15:
                        wd = following("vector")
                    if j == 0 and g == 3:
                        S1, steps1 = attn1(nc, Q, sb, c, io, scratch, bk, split, XH, XL, done)
                    if 0 < j < 9 and steps1[j - 1][g]:
                        steps1[j - 1][g]()
            wh.hold(wg[0], t1)
            wh.hold(wu[0], t2)
            if j < 15:
                wd = following("vector")
                prev = hs, wd
        x1 = nc.alloc_sbuf_tensor_at("b_x1f", [128, 16, 512], F32, offset=at)
        s1 = nc.alloc_sbuf_tensor_at("b_s1f", [128, 4, T], F32, offset=at + 32768)
        tx, ts1 = [], []
        for n in range(4):
            sl = slice(n * 512, n * 512 + 512)
            ts1.append(Q.dma("sync", f"fs{n}", s1[:, :, sl],
                             scratch["s1"].rearrange("(k p) t -> p k t", p=128)[:, :, sl], t1, t2, S1["out"]))
            tx.append(Q.dma("sync", f"fx{n}", x1[:, n * 4:n * 4 + 4, :],
                            scratch["x1"].rearrange("(i p) d -> p i d", p=128)[:, n * 4:n * 4 + 4, :], t1, t2, done))

        def rows(n):
            sl = slice(n * 512, n * 512 + 512)
            tp = []
            for o in range(4):
                t = A(lambda e, o=o: e.activation(ACC[:, o, sl], ACC[:, o, sl], ACT.Silu), tA[o, n])
                tp.append(Q.op("gpsimd" if o % 2 else "vector", lambda e, o=o: e.tensor_tensor(
                    ACC[:, o, sl], ACC[:, o, sl], s1[:, o, sl], ALU.mult), t, ts1[n]))
            done_rows.append((n, tp))

        def store(n, tp):
            for i in range(n * 4, n * 4 + 4):
                b, kb, f = bk.take()

                def go(e, i=i, kb=kb):
                    for k in range(4):
                        m = e.transpose(kb[:, k * 128:(k + 1) * 128], ACC[:, k, i * 128:(i + 1) * 128], cst[:, 0:128])
                    return m
                t = P(go, tp, f)
                t = V(lambda e, i=i, kb=kb: e.tensor_tensor(x1[:, i, :], kb[:, :], x1[:, i, :], ALU.add), t, tx[n])
                bk.hold(b, t)
                Q.dma("sync" if i % 2 else "scalar", f"y{i % 4}", out["y"][i * 128:(i + 1) * 128, :], x1[:, i, :], t)

        done_rows = []

        def after(n):
            rows(n)
            if n:
                store(*done_rows[n - 1])
        down(15, hs, wd, after)
        store(*done_rows[3])


def laid_out(inputs):
    g = {k: np.ascontiguousarray(np.asarray(v)) for k, v in inputs.items()}
    f = np.float32
    x = g["L0_attn_x"].reshape(T, 512)
    o = {"x": x, "xT": x.T}
    for n in ("Wq", "Wk", "Wv", "Wg", "Wo"):
        o[n] = g["L0_attn_" + n]
    wab = np.zeros((512, 128), f)
    wab[:, 0:16], wab[:, 32:48] = g["L0_attn_Wa"], g["L0_attn_Wb"]
    bab = np.zeros((128, 1), f)
    bab[0:16, 0], bab[32:48, 0] = g["L0_attn_ba"], g["L0_attn_bb"]
    o["Wab"], o["bab"] = wab, bab
    cw = np.zeros((128, 16, 3, 5), f)
    for i, n in enumerate("qkv"):
        cw[:, :, i, 0:4] = g[f"L0_attn_{n}cw"].reshape(16, 128, 4).transpose(1, 0, 2)
        cw[:, :, i, 4] = g[f"L0_attn_{n}cb"].reshape(16, 128).T
    o["cw"] = cw
    o["ln"] = np.stack([g["L0_attn_ln_w"], g["L0_attn_ln_b"]], 1)
    o["gate_wT"], o["up_wT"] = g["L0_ffn_gate_w"].T, g["L0_ffn_up_w"].T
    o["down_wT"] = g["L0_ffn_down_w"].T
    s = np.zeros((128, 26), f)
    s[:, 0:11] = g["L0_ffn_gate_s"].reshape(11, 128).T
    s[:, 11:22] = g["L0_ffn_up_s"].reshape(11, 128).T
    s[:, 22:26] = g["L0_ffn_down_s"].reshape(4, 128).T
    o["ffn0_s"] = s
    order = np.arange(512).reshape(2, 128, 2).transpose(0, 2, 1)
    for n in ("ig", "ag"):
        w = np.zeros((512, 512), f)
        for h in range(16):
            w[32 * h:32 * h + 32, 32 * h:32 * h + 32] = g[f"L1_attn_{n}_w"][h]
        o[n + "_w"] = np.stack([np.stack([w[np.ix_(order[m // 2, r], order[m // 2, m % 2])] for r in range(2)], 1)
                                for m in range(4)])
    v = np.zeros((128, 4, 3), f)
    order = order.reshape(4, 128)
    v[:, :, 0] = g["L1_attn_ig_b"].reshape(512)[order].T
    v[:, :, 1] = g["L1_attn_ag_b"].reshape(512)[order].T
    v[:, :, 2] = g["L1_attn_a_param"].reshape(512)[order].T
    o["l1v"] = v
    n = np.arange(4096).reshape(16, 128, 2).transpose(0, 2, 1).reshape(-1)
    for p in ("gate", "up"):
        o[p + "_pk"] = g[f"L1_ffn_{p}_W_packed"].T[:, n]
        o[p + "_sc"] = g[f"L1_ffn_{p}_scales"].T[:, n]
    o["down_pk"] = g["L1_ffn_down_W_packed"].T
    o["down_scT"] = g["L1_ffn_down_scales"].T
    c = np.zeros((128, C_N), f)
    c[:, 0:128] = np.eye(128)
    c[:, C_CM:C_CM + 128] = np.eye(128) - 1.0 / 128
    c[:, C_J:C_J + 128] = 1.0 / 128
    r = np.arange(128) % 32 // 16
    cc = np.arange(32) // 16
    c[:, C_M16:C_M16 + 32] = -1.0 * (r[:, None] == cc[None, :])
    c[:, C_OFF:C_OFF + 32] = -1.0 * ((r[:, None] == 0) & (cc[None, :] == 1))
    c[:, C_FLAG] = r == 0
    c[:, C_FLAG + 1] = r == 1
    o["consts"] = c
    return {k: np.ascontiguousarray(a) for k, a in o.items()}


SCRATCH = {"a": [16, T], "g": [16, T], "gc": [256], "g0": [512, T], "og": [2048, T], "x1": [T, 512],
           "s1": [512, T]}


def kernel(**inputs):
    import concourse.bacc as _bacc
    from concourse.bass_utils import run_bass_kernel_spmd as _run

    nc = _bacc.Bacc("TRN2", target_bir_lowering=False, num_devices=1)
    arrays, io = {}, {}
    for name, a in laid_out(inputs).items():
        arrays["in_" + name] = a
        io[name] = nc.dram_tensor("in_" + name, a.shape, mybir.dt.from_np(a.dtype), kind="ExternalInput").ap()
    out = {"y": nc.dram_tensor("out_y", [T, 512], F32, kind="ExternalOutput").ap()}
    scratch = {n: nc.dram_tensor("tmp_" + n, s, F32).ap() for n, s in SCRATCH.items()}
    program(nc, io, out, scratch)
    r = _run(nc, [arrays], core_ids=[0])
    return r.results[0]["out_y"].reshape(2, 1024, 512)
```
